# Optimizing a Trainium2 kernel written in Bass

```python
import numpy as np
import jax
import jax.numpy as jnp

def _softmax(x, axis=-1):
    return jax.nn.softmax(x, axis=axis)

def _gelu(x):
    return jax.nn.gelu(x, approximate=True)

def _silu(x):
    return jax.nn.silu(x)

def _sigmoid(x):
    return jax.nn.sigmoid(x)

def _layernorm(x, axis=-1, eps=1e-05):
    m = jnp.mean(x, axis=axis, keepdims=True)
    v = jnp.var(x, axis=axis, keepdims=True)
    return (x - m) / jnp.sqrt(v + eps)

def _scatter_add(tgt, idx, src, axis=0):
    return tgt.at[idx].add(src)

def _segment_sum(src, seg, n):
    return jax.ops.segment_sum(src, seg, n)
kernel_name = 'mk_conv_attn_hybrid_d2_conv_nchw256_r2_85c0ba'

def setup_inputs(seed: int=0):
    np.random.seed(seed)
    _w = jnp.asarray

    def _rec_inputs():
        import jax
        import jax.numpy as jnp
        _gk = jax.random.key(seed)
        x = -0.0002928 + 1 * jax.random.normal(jax.random.fold_in(_gk, 1), (4, 128, 32, 32), jnp.float32)
        return x
    x = _rec_inputs()

    def _L0_conv_setup():
        import jax, jax.numpy as jnp
        import numpy as np
        B, C, CI, H, W = (4, 128, 64, 32, 32)

        def conv1x1(x, w, b):
            return jnp.einsum('bchw,oc->bohw', x, w) + b[None, :, None, None]
        key = jax.random.key(seed)
        ks = jax.random.split(key, 9)
        s = 0.02
        return {'x': jax.random.normal(ks[0], (B, C, H, W), dtype=jnp.float32), 'Wg': jax.random.normal(ks[1], (CI, C), dtype=jnp.float32) * s, 'bg': jnp.zeros((CI,), dtype=jnp.float32), 'Wt': jax.random.normal(ks[2], (CI, C), dtype=jnp.float32) * s, 'bt': jnp.zeros((CI,), dtype=jnp.float32), 'Wp': jax.random.normal(ks[3], (CI, C), dtype=jnp.float32) * s, 'bp': jnp.zeros((CI,), dtype=jnp.float32), 'Wo': jax.random.normal(ks[4], (C, CI), dtype=jnp.float32) * s, 'bo': jnp.zeros((C,), dtype=jnp.float32)}
    _L0_conv_all = _L0_conv_setup()
    _L0_conv_in = {k: v for k, v in _L0_conv_all.items() if k in ('Wg', 'bg', 'Wt', 'bt', 'Wp', 'bp', 'Wo', 'bo')}
    del _L0_conv_all

    def _L1_attn_setup():
        import jax, jax.numpy as jnp
        import numpy as np
        N_HEAD = 16
        NOPE = 32
        ROPE = 32
        VDIM = 32
        HD = NOPE + ROPE
        WINDOW = 64
        KEEP = 256
        EPS = 1e-06

        def _freqs(T, dim=ROPE, theta=10000.0):
            f = 1.0 / theta ** (np.arange(0, dim, 2, dtype=np.float32) / dim)
            ang = np.outer(np.arange(T, dtype=np.float32), f)
            return (jnp.asarray(np.cos(ang)), jnp.asarray(np.sin(ang)))

        def _rms(x, w):
            return x * jax.lax.rsqrt(jnp.mean(x * x, -1, keepdims=True) + EPS) * w

        def _rope(x, cos, sin):
            T = x.shape[-2]
            c = cos[:T][None, None]
            s = sin[:T][None, None]
            xr, xi = jnp.split(x, 2, -1)
            return jnp.concatenate([xr * c - xi * s, xr * s + xi * c], -1)

        def _attn(q, k, v, mask=None):
            s = jnp.einsum('bhqd,bhkd->bhqk', q, k) / np.float32(np.sqrt(HD))
            if mask is not None:
                s = jnp.where(mask, s, jnp.float32(-1000000000.0))
            return jnp.einsum('bhqk,bhkd->bhqd', jax.nn.softmax(s, -1), v)
        key = jax.random.key(seed)
        ks = jax.random.split(key, 16)
        w = lambda k, shape: jax.random.normal(k, shape, jnp.float32) * 0.02
        B, T, C = (2, 1024, 128)
        return {'x': jax.random.normal(ks[0], (B, T, C), jnp.float32), 'Wcq': w(ks[1], (C, 48)), 'q_norm_w': jnp.ones((48,), jnp.float32), 'Wq_nope': w(ks[2], (48, N_HEAD * NOPE)), 'Wq_rope': w(ks[3], (48, N_HEAD * ROPE)), 'Wckv': w(ks[4], (C, 32)), 'kv_norm_w': jnp.ones((32,), jnp.float32), 'Wk_nope': w(ks[5], (32, N_HEAD * NOPE)), 'Wv': w(ks[6], (32, N_HEAD * VDIM)), 'Wk_rope': w(ks[7], (C, ROPE)), 'W_imp': w(ks[8], (C, 1)), 'Wsel_k': w(ks[9], (C, N_HEAD * HD)), 'Wsel_v': w(ks[10], (C, N_HEAD * VDIM)), 'Wwin_k': w(ks[11], (C, N_HEAD * HD)), 'Wwin_v': w(ks[12], (C, N_HEAD * VDIM)), 'Wgate': w(ks[13], (C, 3)), 'Wproj': w(ks[14], (N_HEAD * VDIM, C))}
    _L1_attn_all = _L1_attn_setup()
    _L1_attn_in = {k: v for k, v in _L1_attn_all.items() if k in ('Wcq', 'q_norm_w', 'Wq_nope', 'Wq_rope', 'Wckv', 'kv_norm_w', 'Wk_nope', 'Wv', 'Wk_rope', 'W_imp', 'Wsel_k', 'Wsel_v', 'Wwin_k', 'Wwin_v', 'Wgate', 'Wproj')}
    del _L1_attn_all

    def _L1_ffn_setup():
        import jax, jax.numpy as jnp
        import numpy as np
        N_EXPERTS = 8
        TOP_K = 2
        key = jax.random.key(seed)
        ks = jax.random.split(key, 5)
        B, T, C, E, H = (8, 1024, 128, 8, 341)
        scale = 1.0 / np.sqrt(C)
        return {'x': jax.random.normal(ks[0], (B, T, C), dtype=jnp.float32), 'router_w': jax.random.normal(ks[1], (E, C), dtype=jnp.float32) * scale, 'w1': jax.random.normal(ks[2], (E, H, C), dtype=jnp.float32) * scale, 'w2': jax.random.normal(ks[3], (E, C, H), dtype=jnp.float32) * (1.0 / np.sqrt(H)), 'w3': jax.random.normal(ks[4], (E, H, C), dtype=jnp.float32) * scale}
    _L1_ffn_all = _L1_ffn_setup()
    _L1_ffn_in = {k: v for k, v in _L1_ffn_all.items() if k in ('router_w', 'w1', 'w2', 'w3')}
    del _L1_ffn_all
    return {'x': x, 'L0_conv_Wg': _L0_conv_in['Wg'], 'L0_conv_bg': _L0_conv_in['bg'], 'L0_conv_Wt': _L0_conv_in['Wt'], 'L0_conv_bt': _L0_conv_in['bt'], 'L0_conv_Wp': _L0_conv_in['Wp'], 'L0_conv_bp': _L0_conv_in['bp'], 'L0_conv_Wo': _L0_conv_in['Wo'], 'L0_conv_bo': _L0_conv_in['bo'], 'L1_attn_Wcq': _L1_attn_in['Wcq'], 'L1_attn_q_norm_w': _L1_attn_in['q_norm_w'], 'L1_attn_Wq_nope': _L1_attn_in['Wq_nope'], 'L1_attn_Wq_rope': _L1_attn_in['Wq_rope'], 'L1_attn_Wckv': _L1_attn_in['Wckv'], 'L1_attn_kv_norm_w': _L1_attn_in['kv_norm_w'], 'L1_attn_Wk_nope': _L1_attn_in['Wk_nope'], 'L1_attn_Wv': _L1_attn_in['Wv'], 'L1_attn_Wk_rope': _L1_attn_in['Wk_rope'], 'L1_attn_W_imp': _L1_attn_in['W_imp'], 'L1_attn_Wsel_k': _L1_attn_in['Wsel_k'], 'L1_attn_Wsel_v': _L1_attn_in['Wsel_v'], 'L1_attn_Wwin_k': _L1_attn_in['Wwin_k'], 'L1_attn_Wwin_v': _L1_attn_in['Wwin_v'], 'L1_attn_Wgate': _L1_attn_in['Wgate'], 'L1_attn_Wproj': _L1_attn_in['Wproj'], 'L1_ffn_router_w': _L1_ffn_in['router_w'], 'L1_ffn_w1': _L1_ffn_in['w1'], 'L1_ffn_w2': _L1_ffn_in['w2'], 'L1_ffn_w3': _L1_ffn_in['w3']}

def reference(x, L0_conv_Wg, L0_conv_bg, L0_conv_Wt, L0_conv_bt, L0_conv_Wp, L0_conv_bp, L0_conv_Wo, L0_conv_bo, L1_attn_Wcq, L1_attn_q_norm_w, L1_attn_Wq_nope, L1_attn_Wq_rope, L1_attn_Wckv, L1_attn_kv_norm_w, L1_attn_Wk_nope, L1_attn_Wv, L1_attn_Wk_rope, L1_attn_W_imp, L1_attn_Wsel_k, L1_attn_Wsel_v, L1_attn_Wwin_k, L1_attn_Wwin_v, L1_attn_Wgate, L1_attn_Wproj, L1_ffn_router_w, L1_ffn_w1, L1_ffn_w2, L1_ffn_w3):
    import jax
    import jax.numpy as jnp

    def _L0_conv_ref(x, Wg, bg, Wt, bt, Wp, bp, Wo, bo):
        import jax, jax.numpy as jnp
        import numpy as np
        B, C, CI, H, W = (4, 128, 64, 32, 32)

        def conv1x1(x, w, b):
            return jnp.einsum('bchw,oc->bohw', x, w) + b[None, :, None, None]
        b, c, h, w = x.shape
        n = h * w
        g = conv1x1(x, Wg, bg).reshape(b, -1, n)
        th = conv1x1(x, Wt, bt).reshape(b, -1, n)
        ph = conv1x1(x, Wp, bp).reshape(b, -1, n)
        f = jnp.einsum('bci,bcj->bij', th, ph)
        a = jax.nn.softmax(f, axis=-1)
        y = jnp.einsum('bij,bcj->bci', a, g)
        y = y.reshape(b, -1, h, w)
        return conv1x1(y, Wo, bo) + x

    def _L1_attn_ref(x, Wcq, q_norm_w, Wq_nope, Wq_rope, Wckv, kv_norm_w, Wk_nope, Wv, Wk_rope, W_imp, Wsel_k, Wsel_v, Wwin_k, Wwin_v, Wgate, Wproj):
        import jax, jax.numpy as jnp
        import numpy as np
        N_HEAD = 16
        NOPE = 32
        ROPE = 32
        VDIM = 32
        HD = NOPE + ROPE
        WINDOW = 64
        KEEP = 256
        EPS = 1e-06

        def _freqs(T, dim=ROPE, theta=10000.0):
            f = 1.0 / theta ** (np.arange(0, dim, 2, dtype=np.float32) / dim)
            ang = np.outer(np.arange(T, dtype=np.float32), f)
            return (jnp.asarray(np.cos(ang)), jnp.asarray(np.sin(ang)))

        def _rms(x, w):
            return x * jax.lax.rsqrt(jnp.mean(x * x, -1, keepdims=True) + EPS) * w

        def _rope(x, cos, sin):
            T = x.shape[-2]
            c = cos[:T][None, None]
            s = sin[:T][None, None]
            xr, xi = jnp.split(x, 2, -1)
            return jnp.concatenate([xr * c - xi * s, xr * s + xi * c], -1)

        def _attn(q, k, v, mask=None):
            s = jnp.einsum('bhqd,bhkd->bhqk', q, k) / np.float32(np.sqrt(HD))
            if mask is not None:
                s = jnp.where(mask, s, jnp.float32(-1000000000.0))
            return jnp.einsum('bhqk,bhkd->bhqd', jax.nn.softmax(s, -1), v)
        B, T, C = x.shape
        cos, sin = _freqs(T)
        cq = _rms(x @ Wcq, q_norm_w)
        qn = (cq @ Wq_nope).reshape(B, T, N_HEAD, NOPE).transpose(0, 2, 1, 3)
        qr = _rope((cq @ Wq_rope).reshape(B, T, N_HEAD, ROPE).transpose(0, 2, 1, 3), cos, sin)
        q = jnp.concatenate([qn, qr], -1)
        gate = jax.nn.softmax((x @ Wgate).mean(1), -1)
        ckv = _rms(x @ Wckv, kv_norm_w)
        kn = (ckv @ Wk_nope).reshape(B, T, N_HEAD, NOPE).transpose(0, 2, 1, 3)
        v1 = (ckv @ Wv).reshape(B, T, N_HEAD, VDIM).transpose(0, 2, 1, 3)
        kr = (x @ Wk_rope / N_HEAD).reshape(B, T, 1, ROPE).transpose(0, 2, 1, 3)
        kr = _rope(kr, cos, sin)
        k1 = jnp.concatenate([kn, jnp.broadcast_to(kr, (B, N_HEAD, T, ROPE))], -1)
        ii = jnp.arange(T)
        causal = ii[:, None] >= ii[None, :]
        o1 = _attn(q, k1, v1, causal[None, None])
        scores = (x @ W_imp)[..., 0]
        _, idx = jax.lax.top_k(scores, KEEP)
        idx = jnp.sort(idx, 1)
        sel = jnp.take_along_axis(x, idx[..., None], 1)
        ks = (sel @ Wsel_k).reshape(B, KEEP, N_HEAD, HD).transpose(0, 2, 1, 3)
        vs = (sel @ Wsel_v).reshape(B, KEEP, N_HEAD, VDIM).transpose(0, 2, 1, 3)
        ks = jnp.concatenate([ks[..., :NOPE], _rope(ks[..., NOPE:], cos, sin)], -1)
        o2 = _attn(q, ks, vs)
        kw = (x @ Wwin_k).reshape(B, T, N_HEAD, HD).transpose(0, 2, 1, 3)
        vw = (x @ Wwin_v).reshape(B, T, N_HEAD, VDIM).transpose(0, 2, 1, 3)
        kw = jnp.concatenate([kw[..., :NOPE], _rope(kw[..., NOPE:], cos, sin)], -1)
        winmask = causal & (ii[:, None] - ii[None, :] < WINDOW)
        o3 = _attn(q, kw, vw, winmask[None, None])
        g = gate[:, :, None, None, None]
        o = g[:, 0] * o1 + g[:, 1] * o2 + g[:, 2] * o3
        o = o.transpose(0, 2, 1, 3).reshape(B, T, N_HEAD * VDIM)
        return o @ Wproj

    def _L1_ffn_ref(x, router_w, w1, w2, w3):
        import jax, jax.numpy as jnp
        import numpy as np
        N_EXPERTS = 8
        TOP_K = 2
        B, T, C = x.shape
        flat = x.reshape(-1, C)
        logits = flat @ router_w.T
        probs = jax.nn.softmax(logits, axis=-1)
        topk_probs, topk_idx = jax.lax.top_k(probs, TOP_K)
        topk_probs = topk_probs / (jnp.sum(topk_probs, axis=-1, keepdims=True) + 1e-09)
        onehot = jax.nn.one_hot(topk_idx, N_EXPERTS, dtype=flat.dtype)
        gates = jnp.einsum('nk,nke->ne', topk_probs, onehot)
        h1 = jnp.einsum('nc,ehc->neh', flat, w1)
        h3 = jnp.einsum('nc,ehc->neh', flat, w3)
        h = jax.nn.silu(h1) * h3
        y = jnp.einsum('neh,ech->nec', h, w2)
        out = jnp.einsum('ne,nec->nc', gates, y)
        return out.reshape(B, T, C)

    def _gn(v, G=32, eps=1e-05):
        B_, C_, H_, W_ = v.shape
        g = v.reshape(B_, G, C_ // G, H_, W_)
        m = jnp.mean(g, axis=(2, 3, 4), keepdims=True)
        s = jnp.var(g, axis=(2, 3, 4), keepdims=True)
        return ((g - m) / jnp.sqrt(s + eps)).reshape(v.shape)

    def _ln_c(v, eps=1e-06):
        m = jnp.mean(v, axis=1, keepdims=True)
        s = jnp.var(v, axis=1, keepdims=True)
        return (v - m) / jnp.sqrt(s + eps)

    def _ln_t(v, eps=1e-05):
        m = jnp.mean(v, axis=-1, keepdims=True)
        s = jnp.var(v, axis=-1, keepdims=True)
        return (v - m) / jnp.sqrt(s + eps)

    def _to_tokens(v):
        B_, C_, H_, W_ = v.shape
        return v.reshape(B_, C_, H_ * W_).transpose(0, 2, 1)

    def _from_tokens(t, like):
        B_, C_, H_, W_ = like.shape
        return t.transpose(0, 2, 1).reshape(B_, C_, H_, W_)
    x = _L0_conv_ref(x, L0_conv_Wg, L0_conv_bg, L0_conv_Wt, L0_conv_bt, L0_conv_Wp, L0_conv_bp, L0_conv_Wo, L0_conv_bo)
    t = _to_tokens(x)
    t = t + _L1_attn_ref(_ln_t(t), L1_attn_Wcq, L1_attn_q_norm_w, L1_attn_Wq_nope, L1_attn_Wq_rope, L1_attn_Wckv, L1_attn_kv_norm_w, L1_attn_Wk_nope, L1_attn_Wv, L1_attn_Wk_rope, L1_attn_W_imp, L1_attn_Wsel_k, L1_attn_Wsel_v, L1_attn_Wwin_k, L1_attn_Wwin_v, L1_attn_Wgate, L1_attn_Wproj)
    t = t + _L1_ffn_ref(_ln_t(t), L1_ffn_router_w, L1_ffn_w1, L1_ffn_w2, L1_ffn_w3)
    x = _from_tokens(t, x)
    return x

_drawn_inputs = setup_inputs


def setup_inputs(seed=0):
    import zlib

    import numpy as np

    out = dict(_drawn_inputs(seed))
    spreads = {'L0_conv_bg': (0.0, 0.1),
     'L0_conv_bt': (0.0, 0.8),
     'L0_conv_bp': (0.0, 2.0),
     'L0_conv_bo': (0.0, 0.1),
     'L1_attn_q_norm_w': (1.0, 0.6),
     'L1_attn_kv_norm_w': (1.0, 0.6)}
    factors = {'L0_conv_Wg': 4.852,
     'L0_conv_Wt': 5.65,
     'L0_conv_Wp': 4.957,
     'L1_attn_Wcq': 8.0,
     'L1_attn_Wq_nope': 8.0,
     'L1_attn_Wq_rope': 8.0,
     'L1_attn_Wckv': 3.93,
     'L1_attn_Wk_nope': 8.0,
     'L1_attn_Wv': 3.89,
     'L1_attn_Wk_rope': 39.42,
     'L1_attn_W_imp': 3.489,
     'L1_attn_Wsel_k': 8.0,
     'L1_attn_Wsel_v': 3.002,
     'L1_attn_Wwin_k': 8.0,
     'L1_attn_Wgate': 8.0}
    for name, (base, spread) in spreads.items():
        noise = np.random.default_rng([zlib.crc32(name.encode()), seed]).standard_normal(out[name].shape)
        drawn = base * np.exp(spread * noise) if base else spread * noise
        out[name] = jnp.asarray(drawn.astype(out[name].dtype))
    for name, factor in factors.items():
        out[name] = (out[name] * factor).astype(out[name].dtype)
    return out
```

```python
from contextlib import ExitStack

import numpy as np

import concourse.bass as bass
from concourse import mybir

F32 = mybir.dt.float32
F32R = mybir.dt.float32r
BF16 = mybir.dt.bfloat16
ALU = mybir.AluOpType
ACT = mybir.ActivationFunctionType
AX = mybir.AxisListType.X

P = 128
B, C, T = 4, 128, 1024
NT = T // P
CH = 512
NC = T // CH
CI = 64
QR, KVR = 48, 32
NH, HG = 16, 4
NG = NH // HG
NOPE, HALF = 32, 16
HD = NOPE + 2 * HALF
VD = 32
KEEP, WINDOW = 256, 64
SCALE = 1.0 / 8.0
NE, HID = 8, 341
HT = [(0, 128), (128, 128), (256, 85)]
WN = P + WINDOW
LNE, RMSE = 1e-5, 1e-6
MASKED = -8.0e9
A_CQ, A_KV, A_KR, A_IMP, A_GATE, A_N = 0, 48, 80, 112, 113, 116


def phase_end(nc, sems):
    for s in sems.values():
        nc.sync.sem_clear(s)
    nc.all_engine_barrier()


def open_sems(nc, ctx, names):
    return {n: ctx.enter_context(nc.semaphore(n)) for n in names.split()}


def program(nc, d, out):
    with ExitStack() as top:
        def sb(ctx, name, shape, dt=F32):
            return ctx.enter_context(nc.sbuf_tensor(name, shape, dt))

        ps = top.enter_context(nc.psum_tensor("ps", [P, 8, CH], F32))
        t2_dram = nc.dram_tensor("t2_dram", (B, C, T), F32, kind="Internal").ap()
        ident = sb(top, "ident", [P, P])
        eps = sb(top, "eps", [P, 2])
        with ExitStack() as att_mem:
            attention_part(nc, d, t2_dram, ps, ident, eps, lambda *a: sb(att_mem, *a))
        with ExitStack() as ffn_mem:
            experts_part(nc, d, t2_dram, out, ps, ident, eps, lambda *a: sb(ffn_mem, *a))


class Mem:
    pass


def attention_part(nc, d, t2_dram, ps, ident, eps, sb):
    m = Mem()
    m.ps, m.d, m.ident, m.eps = ps, d, ident, eps
    m.ident_bf = sb("ident_bf", [P, P], BF16)
    m.causal_q = sb("causal_q", [P, P], BF16)
    m.causal_k = sb("causal_k", [P, P], BF16)
    m.window_q0 = sb("window_q0", [P, WN], BF16)
    m.window_q = sb("window_q", [P, WN], BF16)
    m.window_k = sb("window_k", [P, WN], BF16)
    m.cos = sb("cos", [P, NT, HALF])
    m.sin = sb("sin", [P, NT, HALF])
    m.before = sb("before", [P, P])
    m.below = sb("below", [P, P])
    m.ones = sb("ones", [P, P])
    m.iota = sb("iota", [P, KEEP])
    m.wt2 = sb("wt2", [C, 2 * CI])
    m.wp2 = sb("wp2", [C, 2 * CI])
    m.wg = sb("wg", [C, CI])
    m.wo = sb("wo", [CI, C])
    m.bias = sb("bias", [P, 4])
    m.wa = sb("wa", [C, A_N])
    m.qnw = sb("qnw", [P, QR])
    m.kvnw = sb("kvnw", [P, KVR])
    m.wqp = sb("wqp", [QR, NG, P])
    m.wvp = sb("wvp", [P, NG, C])
    m.xnT = sb("xnT", [C, T])
    m.cqT = sb("cqT", [QR, T])
    m.k1a = sb("k1a", [P, T], F32R)
    m.k1b = sb("k1b", [66, T], F32R)
    m.v1 = sb("v1", [P, NT, KVR])
    m.selT = sb("selT", [C, KEEP])
    m.t2 = sb("t2", [C, T])
    m.gates = sb("gates", [P, 3])
    m.small = sb("small", [P, 512])
    m.wq_g = sb("wq_g", [QR, 3 * P])
    m.wk_g = sb("wk_g", [C, 3 * P])
    m.ws_g = sb("ws_g", [C, 3 * P])
    m.wproj_g = sb("wproj_g", [P, C])
    m.wvp_g = sb("wvp_g", [P, C])
    m.rawq = sb("rawq", [P, NT, 3 * P])
    m.vw = sb("vw", [P, NT, P])
    m.vs = sb("vs", [P, 2, P])
    m.tok = sb("tok", [P, NT, HG, 2 * HD])
    m.q1a = sb("q1a", [P, HG, T], F32R)
    m.q1b = sb("q1b", [66, HG, T], F32R)
    m.qa = sb("qa", [P, HG, T], F32R)
    m.qb = sb("qb", [66, HG, T], F32R)
    m.kwa = sb("kwa", [P, HG, T], F32R)
    m.kwb = sb("kwb", [66, HG, T], F32R)
    m.ksa = sb("ksa", [P, HG, KEEP], F32R)
    m.ksb = sb("ksb", [66, HG, KEEP], F32R)
    m.prob = sb("prob", [P, 2, HG, CH])
    m.obuf = sb("obuf", [P, 3072])
    m.probf = m.prob[:].rearrange("p a h n -> p (a h n)")
    m.rawk = m.probf[:, 0:NT * 2 * P].rearrange("p (t n) -> p t n", t=NT)
    m.o1 = m.obuf[:, 0:T]
    m.o2 = m.obuf[:, T:2 * T]
    m.rden = m.obuf[:, 2 * T:2 * T + CH]
    m.mrow = m.obuf[0:HG * NT, 2 * T + CH:2 * T + CH + P]
    m.raws = m.obuf[:, 3 * CH:4 * CH].rearrange("p (t n) -> p t n", t=2)
    m.rope_tmp = [m.obuf[:, k * CH:(k + 1) * CH] for k in range(3)]
    m.rawqf = m.rawq[:].rearrange("p t n -> p (t n)")
    m.tokf = m.tok[:].rearrange("p t h n -> p (t h n)")

    m.ones32 = m.ones[:, 0:VD]
    weights_and_constants(nc, m, d)
    with nc.Fori(0, B) as b:
        nonlocal_block(nc, m, b)
        latents(nc, m)
        selection(nc, m)
        with nc.Fori(0, NG) as g:
            head_group(nc, m, g)
        store_stream(nc, m, t2_dram, b)


def store_stream(nc, m, t2_dram, b):
    with ExitStack() as stack:
        s = open_sems(nc, stack, "stored")
        with nc.Block() as block:
            @block.sync
            def _(sp):
                sp.dma_start(t2_dram[b], m.t2[:]).then_inc(s["stored"], 16)
                sp.wait_ge(s["stored"], 16)
        phase_end(nc, s)


def weights_and_constants(nc, m, d):
    stack = ExitStack()
    s = open_sems(nc, stack, "s_load s_zero s_blk s_mm s_copy s_row s_one")
    sqn = m.tokf[:, 0:NG * QR].rearrange("p (g n) -> p g n", g=NG)
    kblk = m.tokf[:, 512:1024].rearrange("p (g n) -> p g n", g=NG)
    vblk = m.tokf[:, 1024:1536].rearrange("p (g n) -> p g n", g=NG)
    wpr = m.tokf[:, 1536:2048].rearrange("p (g n) -> p g n", g=NG)
    ones_row = m.probf[0:1, 0:HG * T]
    with nc.Block() as block:
        consts = [(m.ident, "ident"), (m.ident_bf, "ident_bf"), (m.causal_q, "causal_q"), (m.causal_k, "causal_k"),
                  (m.window_q0, "window_q0"), (m.window_q, "window_q"), (m.window_k, "window_k"), (m.cos, "cos"),
                  (m.sin, "sin"), (m.before, "before"), (m.below, "below"), (m.iota, "iota"), (m.wt2, "wt2"),
                  (m.wp2, "wp2"), (m.wg, "wg"), (m.wo, "wo"), (m.bias, "bias"), (m.wa, "wa"), (m.qnw, "qnw"),
                  (m.kvnw, "kvnw"), (sqn, "wqn_t"), (wpr, "wproj")]

        @block.sync
        def _(sp):
            for dst, name in consts:
                sp.dma_start(dst[:] if not isinstance(dst, bass.AP) else dst, d[name]).then_inc(s["s_load"], 16)
            sp.wait_ge(s["s_zero"], 1)
            for g in range(NG):
                for h in range(HG):
                    r = slice(32 * h, 32 * h + 32)
                    sp.dma_start(kblk[r, g, r], d["wk_t"][g, h]).then_inc(s["s_blk"], 16)
                    sp.dma_start(vblk[r, g, r], d["wv_t"][g, h]).then_inc(s["s_blk"], 16)
            sp.wait_ge(s["s_one"], 7)
            sp.dma_start(m.k1b[64:65, :].bitcast(F32), ones_row[:, 0:T]).then_inc(s["s_row"], 16)
            sp.dma_start(m.kwb[65:66].rearrange("p h n -> p (h n)").bitcast(F32), ones_row).then_inc(s["s_row"], 16)
            sp.dma_start(m.ksb[64:65].rearrange("p h n -> p (h n)").bitcast(F32),
                         ones_row[:, 0:HG * KEEP]).then_inc(s["s_row"], 16)
            sp.wait_ge(s["s_row"], 48)

        @block.vector
        def _(dve):
            dve.memset(m.tokf[:, 512:1536], 0.0).then_inc(s["s_zero"], 1)
            dve.memset(m.ones[:], 1.0).then_inc(s["s_one"], 1)
            dve.memset(ones_row, 1.0).then_inc(s["s_one"], 1)
            dve.memset(m.eps[:, 0:1], LNE).then_inc(s["s_one"], 1)
            dve.memset(m.eps[:, 1:2], RMSE).then_inc(s["s_one"], 1)
            dve.memset(m.k1b[64:66].bitcast(F32), 0.0).then_inc(s["s_one"], 1)
            dve.memset(m.kwb[64:66].bitcast(F32), 0.0).then_inc(s["s_one"], 1)
            dve.memset(m.ksb[64:66].bitcast(F32), 0.0).then_inc(s["s_one"], 1)
            dve.wait_ge(s["s_mm"], 1)
            dve.tensor_copy(m.wqp[:], m.ps[0:QR, 0, :].rearrange("p (g n) -> p g n", g=NG)).then_inc(s["s_copy"], 1)
            dve.tensor_copy(m.wvp[:], m.ps[:, 1, :].rearrange("p (g n) -> p g n", g=NG)).then_inc(s["s_copy"], 1)

        @block.tensor
        def _(pe):
            pe.wait_ge(s["s_load"], 16 * len(consts))
            pe.wait_ge(s["s_blk"], 16 * 2 * NH)
            for g in range(NG):
                pe.matmul(m.ps[0:QR, 0, g * P:(g + 1) * P], sqn[:, g, :], kblk[:, g, :], start=True, stop=True)
                mm = pe.matmul(m.ps[:, 1, g * P:(g + 1) * P], vblk[:, g, :], wpr[:, g, :], start=True, stop=True)
            mm.then_inc(s["s_mm"], 1)
    phase_end(nc, s)
    stack.close()


def nonlocal_block(nc, m, b):
    ps, d = m.ps, m.d
    x = m.tokf[:, 0:T]
    va = m.tokf[:, T:2 * T].rearrange("p (t n) -> p t n", t=NT)
    y = m.tokf[0:CI, 2 * T:3 * T]
    th_a, ph_a = m.q1a[:, 0, :], m.kwa[:, 0, :]
    th_b, ph_b = m.q1b[0:65, 0, :], m.k1b[0:65, :]
    negm = m.small[:, 0:NT]
    mrow = m.mrow[0:NT, :]
    rden = m.rden
    stack = ExitStack()
    s = open_sems(nc, stack, "n_x n_proj n_hi n_lo n_va n_vac n_app n_max n_mt n_mrow n_mdma n_qb "
                           "n_s n_exp n_pv n_chain n_y n_o n_t2")

    with nc.Block() as block:
        @block.sync
        def _(sp):
            sp.dma_start(x, d["x"][b]).then_inc(s["n_x"], 16)
            sp.wait_ge(s["n_mrow"], 1)
            sp.dma_start(th_b[64:65, :].bitcast(F32), mrow).then_inc(s["n_mdma"], 16)
            sp.wait_ge(s["n_hi"], 4)
            sp.dma_start(th_b[0:64, :].bitcast(F32), th_a[0:64, :].bitcast(F32)).then_inc(s["n_mdma"], 16)

        @block.tensor
        def _(pe):
            pe.wait_ge(s["n_x"], 16)
            for c in range(NC):
                xc = x[:, c * CH:(c + 1) * CH]
                pe.matmul(ps[:, c, :], m.wt2[:], xc, start=True, stop=True).then_inc(s["n_proj"], 1)
                pe.matmul(ps[:, 2 + c, :], m.wp2[:], xc, start=True, stop=True).then_inc(s["n_proj"], 1)
            for t in range(NT):
                mm = pe.matmul(ps[:, 4, t * CI:(t + 1) * CI], x[:, t * P:(t + 1) * P], m.wg[:],
                               start=True, stop=True)
            mm.then_inc(s["n_va"], 1)
            pe.wait_ge(s["n_hi"], 4)
            pe.wait_ge(s["n_lo"], 4)
            pe.wait_ge(s["n_vac"], 1)
            for t in range(NT):
                if t >= 2:
                    pe.wait_ge(s["n_max"], t - 1)
                for c in range(NC):
                    mm = pe.matmul(ps[:, 2 * (t % 2) + c, :], th_a[:, t * P:(t + 1) * P],
                                   ph_a[:, c * CH:(c + 1) * CH], start=True, stop=True)
                mm.then_inc(s["n_app"], 1)
            pe.wait_ge(s["n_max"], NT)
            pe.transpose(ps[0:NT, 4, 0:P], negm, m.ident[:]).then_inc(s["n_mt"], 1)
            pe.wait_ge(s["n_mdma"], 32)

            def scores(u):
                c, j = divmod(u, NT)
                if u >= 4:
                    pe.wait_ge(s["n_exp"], u - 3)
                pe.matmul(ps[:, u % 4, :], ph_a[:, j * P:(j + 1) * P], th_a[:, c * CH:(c + 1) * CH],
                          start=True, stop=False)
                pe.matmul(ps[:, u % 4, :], ph_b[:, j * P:(j + 1) * P], th_b[:, c * CH:(c + 1) * CH],
                          start=False, stop=True).then_inc(s["n_s"], 1)

            def values(u):
                c, j = divmod(u, NT)
                pe.wait_ge(s["n_exp"], u + 1)
                pe.matmul(ps[:, 5 + c, :], va[:, j, :], m.probf[:, (u % 4) * CH:(u % 4 + 1) * CH],
                          start=(j == 0), stop=(j == NT - 1)).then_inc(s["n_pv"], 1)

            scores(0)
            scores(1)
            for u in range(NC * NT):
                if u + 2 < NC * NT:
                    scores(u + 2)
                values(u)
            for c in range(NC):
                pe.wait_ge(s["n_y"], c + 1)
                pe.matmul(ps[:, c, :], m.wo[:], y[:, c * CH:(c + 1) * CH], start=True, stop=True)\
                    .then_inc(s["n_o"], 1)

        @block.scalar
        def _(act):
            for c in range(NC):
                cc = slice(c * CH, (c + 1) * CH)
                act.wait_ge(s["n_proj"], 2 * c + 1)
                act.activation(th_a[:, cc], ps[:, c, :], ACT.Identity, bias=m.bias[:, 0:1]).then_inc(s["n_hi"], 1)
                act.wait_ge(s["n_proj"], 2 * c + 2)
                act.activation(ph_a[:, cc], ps[:, 2 + c, :], ACT.Identity, bias=m.bias[:, 1:2])\
                    .then_inc(s["n_hi"], 1)
            for u in range(NC * NT):
                act.wait_ge(s["n_s"], u + 1)
                if u >= 4:
                    act.wait_ge(s["n_pv"], u - 3)
                act.activation(m.probf[:, (u % 4) * CH:(u % 4 + 1) * CH], ps[:, u % 4, :], ACT.Exp)\
                    .then_inc(s["n_exp"], 1)

        @block.vector
        def _(dve):
            dve.memset(va[:, :, CI:2 * CI], 1.0).then_inc(s["n_vac"], 1)
            for c in range(NC):
                cc = slice(c * CH, (c + 1) * CH)
                dve.wait_ge(s["n_hi"], 2 * c + 1)
                dve.scalar_tensor_tensor(out=th_a[64:128, cc], in0=ps[64:128, c, :], scalar=m.bias[64:128, 0:1],
                                         in1=th_a[64:128, cc].bitcast(F32), op0=ALU.add, op1=ALU.subtract)\
                    .then_inc(s["n_lo"], 1)
                dve.wait_ge(s["n_hi"], 2 * c + 2)
                dve.scalar_tensor_tensor(out=ph_b[0:64, cc], in0=ps[0:64, 2 + c, :], scalar=m.bias[0:64, 1:2],
                                         in1=ph_a[0:64, cc].bitcast(F32), op0=ALU.add, op1=ALU.subtract)\
                    .then_inc(s["n_lo"], 1)
            dve.wait_ge(s["n_va"], 1)
            dve.tensor_copy(va[:, :, 0:CI], ps[:, 4, :].rearrange("p (t n) -> p t n", t=NT)).then_inc(s["n_vac"], 1)
            for t in range(NT):
                dve.wait_ge(s["n_app"], t + 1)
                k = 2 * (t % 2)
                dve.tensor_reduce(negm[:, t:t + 1], ps[:, k:k + 2, :].rearrange("p a n -> p (a n)"), AX, ALU.max,
                                  negate=True).then_inc(s["n_max"], 1)
            dve.wait_ge(s["n_mt"], 1)
            dve.tensor_copy(mrow.bitcast(F32R), ps[0:NT, 4, 0:P]).then_inc(s["n_mrow"], 1)
            for c in range(NC):
                cc = slice(c * CH, (c + 1) * CH)
                dve.wait_ge(s["n_pv"], NT * (c + 1))
                dve.reciprocal(rden[0:CI, :], ps[CI:2 * CI, 5 + c, :]).then_inc(s["n_chain"], 1)
                dve.wait_ge(s["n_chain"], 2 * c + 1)
                dve.tensor_tensor(y[:, cc], ps[0:CI, 5 + c, :], rden[0:CI, :], ALU.mult).then_inc(s["n_chain"], 1)
                dve.wait_ge(s["n_chain"], 2 * c + 2)
                dve.tensor_scalar(y[:, cc], y[:, cc], m.bias[0:CI, 2:3], None, ALU.add).then_inc(s["n_y"], 1)
            for c in range(NC):
                cc = slice(c * CH, (c + 1) * CH)
                dve.wait_ge(s["n_o"], c + 1)
                dve.scalar_tensor_tensor(out=m.t2[:, cc], in0=ps[:, c, :], scalar=m.bias[:, 3:4], in1=x[:, cc],
                                         op0=ALU.add, op1=ALU.add).then_inc(s["n_t2"], 1)
    phase_end(nc, s)
    stack.close()


def in_order(engine, sem):
    done = [0]

    def run(ins):
        done[0] += 1
        ins.then_inc(sem, 1)
        engine.wait_ge(sem, done[0])
    return run


def each_tile(col, n):
    return col.unsqueeze(2).to_broadcast([P, col.shape[1], n])


def each_token(row, n):
    return row.unsqueeze(1).to_broadcast([P, n, row.shape[1]])


def latents(nc, m):
    ps = m.ps
    t_tok = m.rawqf[:, 0:T]
    xn = m.rawqf[:, T:2 * T]
    pa = m.rawqf[:, 2 * T:2 * T + NT * A_N].rearrange("p (t n) -> p t n", t=NT)
    sm = m.small
    mv = sm[:, 16:32].rearrange("p (t n) -> p t n", t=NT)
    std, rstd = sm[:, 32:40], sm[:, 40:48]
    st = sm[:, 48:96].rearrange("p (t n) -> p t n", t=NT)
    ssq, rms, rrms = sm[:, 96:112], sm[:, 112:128], sm[:, 128:144]
    gsum, gexp, gnm, gtot = sm[:, 144:147], sm[:, 148:151], sm[:, 152:153], sm[:, 153:154]
    grec = sm[:, 154:155]
    with ExitStack() as stack:
        s = open_sems(nc, stack, "t2_turned t_copied chain std_done xn_done xn_turned xnT_done pa_done pa_copied")
        with nc.Block() as block:
            @block.tensor
            def _(pe):
                for t in range(NT):
                    mm = pe.transpose(ps[:, t // 4, (t % 4) * P:(t % 4 + 1) * P], m.t2[:, t * P:(t + 1) * P],
                                      m.ident[:])
                    if t % 4 == 3:
                        mm.then_inc(s["t2_turned"], 1)
                for t in range(NT):
                    pe.wait_ge(s["xn_done"], t + 1)
                    mm = pe.transpose(ps[:, 2 + t // 4, (t % 4) * P:(t % 4 + 1) * P], xn[:, t * P:(t + 1) * P],
                                      m.ident[:])
                    if t % 4 == 3:
                        mm.then_inc(s["xn_turned"], 1)
                for t in range(NT):
                    pe.wait_ge(s["xnT_done"], t // 4 + 1)
                    mm = pe.matmul(ps[:, 4 + t // 4, (t % 4) * A_N:(t % 4 + 1) * A_N],
                                   m.xnT[:, t * P:(t + 1) * P], m.wa[:], start=True, stop=True)
                    if t % 4 == 3:
                        mm.then_inc(s["pa_done"], 1)

            @block.scalar
            def _(act):
                for k in range(2):
                    act.wait_ge(s["t2_turned"], k + 1)
                    act.copy(t_tok[:, k * CH:(k + 1) * CH], ps[:, k, :]).then_inc(s["t_copied"], 1)
                act.wait_ge(s["chain"], 1)
                act.activation(std, mv[:, :, 1], ACT.Sqrt, bias=m.eps[:, 0:1]).then_inc(s["std_done"], 1)
                for k in range(2):
                    act.wait_ge(s["xn_turned"], k + 1)
                    act.copy(m.xnT[:, k * CH:(k + 1) * CH], ps[:, 2 + k, :]).then_inc(s["xnT_done"], 1)

            @block.vector
            def _(dve):
                for t in range(NT):
                    dve.wait_ge(s["t_copied"], t // 4 + 1)
                    ins = dve.bn_stats(st[:, t, :], t_tok[:, t * P:(t + 1) * P])
                    ins.then_inc(s["pa_copied"], 1)
                dve.wait_ge(s["pa_copied"], NT)
                for t in range(NT):
                    ins = dve.bn_aggr(mv[:, t, :], st[:, t, :])
                ins.then_inc(s["chain"], 1)
                dve.wait_ge(s["std_done"], 1)
                dve.wait_ge(s["chain"], 1)
                dve.reciprocal(rstd, std).then_inc(s["chain"], 1)
                dve.wait_ge(s["chain"], 2)
                for t in range(NT):
                    dve.tensor_scalar(xn[:, t * P:(t + 1) * P], t_tok[:, t * P:(t + 1) * P], mv[:, t, 0:1],
                                      rstd[:, t:t + 1], ALU.subtract, ALU.mult).then_inc(s["xn_done"], 1)
                for k in range(2):
                    dve.wait_ge(s["pa_done"], k + 1)
                    dve.tensor_copy(pa[:, 4 * k:4 * k + 4, :],
                                    ps[:, 4 + k, 0:4 * A_N].rearrange("p (t n) -> p t n", t=4))
        phase_end(nc, s)

    cq, ckv = pa[:, :, A_CQ:A_KV], pa[:, :, A_KV:A_KR]
    kr = pa[:, :, A_KR:A_IMP]
    k1tok = m.obuf[:, 0:T].rearrange("p (t n) -> p t n", t=NT)
    cqn = m.obuf[:, T:T + NT * QR].rearrange("p (t n) -> p t n", t=NT)
    tmp = m.obuf[:, 2 * T:2 * T + NT * QR].rearrange("p (t n) -> p t n", t=NT)
    ro = m.tokf[:, 0:6 * P].rearrange("p (k t n) -> p k t n", k=6, t=NT)
    with ExitStack() as stack:
        s = open_sems(nc, stack, "gate_sum gate_diff gate_exp ssq_done rms_done chain cqn_done k1_done "
                                 "cq_turned k1_turned copied")
        with nc.Block() as block:
            @block.tensor
            def _(pe):
                for t in range(NT):
                    mm = pe.matmul(ps[:, 6, 0:3], m.ones[:], pa[:, t, A_GATE:A_N], start=(t == 0), stop=(t == NT - 1))
                mm.then_inc(s["gate_sum"], 1)
                pe.wait_ge(s["cqn_done"], 1)
                for t in range(NT):
                    mm = pe.transpose(ps[0:QR, t // 4, (t % 4) * P:(t % 4 + 1) * P], cqn[:, t, :], m.ident[:])
                mm.then_inc(s["cq_turned"], 1)
                pe.wait_ge(s["k1_done"], 1)
                for t in range(NT):
                    mm = pe.transpose(ps[:, 2 + t // 4, (t % 4) * P:(t % 4 + 1) * P], k1tok[:, t, :], m.ident[:])
                mm.then_inc(s["k1_turned"], 1)

            @block.scalar
            def _(act):
                act.wait_ge(s["ssq_done"], 2)
                act.activation(rms[:, 0:NT], ssq[:, 0:NT], ACT.Sqrt, bias=m.eps[:, 1:2], scale=1.0 / QR)\
                    .then_inc(s["rms_done"], 1)
                act.activation(rms[:, NT:2 * NT], ssq[:, NT:2 * NT], ACT.Sqrt, bias=m.eps[:, 1:2],
                               scale=1.0 / KVR).then_inc(s["rms_done"], 1)
                act.wait_ge(s["gate_diff"], 1)
                act.activation(gexp, gsum, ACT.Exp, scale=1.0 / T).then_inc(s["gate_exp"], 1)
                act.wait_ge(s["cq_turned"], 1)
                for k in range(2):
                    act.copy(m.cqT[:, k * CH:(k + 1) * CH], ps[0:QR, k, :])
                act.wait_ge(s["k1_turned"], 1)
                for k in range(2):
                    kk = slice(k * CH, (k + 1) * CH)
                    act.copy(m.k1a[0:HD, kk], ps[0:HD, 2 + k, :])
                    act.copy(m.k1a[HD:P, kk], ps[0:HD, 2 + k, :])
                    act.copy(m.k1b[0:HD, kk], ps[HD:P, 2 + k, :])

            @block.vector
            def _(dve):
                run = in_order(dve, s["chain"])
                run(dve.tensor_tensor(tmp, cq, cq, ALU.mult))
                dve.tensor_reduce(ssq[:, 0:NT], tmp, AX, ALU.add).then_inc(s["ssq_done"], 1)
                dve.wait_ge(s["ssq_done"], 1)
                run(dve.tensor_tensor(tmp[:, :, 0:KVR], ckv, ckv, ALU.mult))
                dve.tensor_reduce(ssq[:, NT:2 * NT], tmp[:, :, 0:KVR], AX, ALU.add).then_inc(s["ssq_done"], 1)
                dve.wait_ge(s["gate_sum"], 1)
                run(dve.tensor_reduce(gnm, ps[:, 6, 0:3], AX, ALU.max, negate=True))
                dve.tensor_scalar(gsum, ps[:, 6, 0:3], gnm, None, ALU.add).then_inc(s["gate_diff"], 1)
                dve.wait_ge(s["rms_done"], 2)
                run(dve.reciprocal(rrms, rms))
                run(dve.tensor_tensor(cqn, cq, each_tile(rrms[:, 0:NT], QR), ALU.mult))
                dve.tensor_tensor(cqn, cqn, each_token(m.qnw[:], NT), ALU.mult).then_inc(s["cqn_done"], 1)
                run(dve.tensor_tensor(m.v1[:], ckv, each_tile(rrms[:, NT:2 * NT], KVR), ALU.mult))
                run(dve.tensor_tensor(m.v1[:], m.v1[:], each_token(m.kvnw[:], NT), ALU.mult))
                run(dve.tensor_scalar(kr, kr, 1.0 / NH, None, ALU.mult))
                xr, xi = kr[:, :, 0:HALF], kr[:, :, HALF:2 * HALF]
                dve.tensor_tensor(ro[:, 0], xr, m.cos[:], ALU.mult)
                dve.tensor_tensor(ro[:, 1], xi, m.sin[:], ALU.mult)
                dve.tensor_tensor(ro[:, 2], xr, m.sin[:], ALU.mult)
                run(dve.tensor_tensor(ro[:, 3], xi, m.cos[:], ALU.mult))
                dve.tensor_tensor(ro[:, 4], ro[:, 0], ro[:, 1], ALU.subtract)
                run(dve.tensor_tensor(ro[:, 5], ro[:, 2], ro[:, 3], ALU.add))
                for at, n, src in ((0, KVR, m.v1[:]), (NOPE, HALF, ro[:, 4]), (NOPE + HALF, HALF, ro[:, 5])):
                    hi = k1tok[:, :, at:at + n]
                    run(dve.tensor_copy(hi.bitcast(F32R), src))
                    run(dve.tensor_tensor(k1tok[:, :, HD + at:HD + at + n].bitcast(F32R), src, hi, ALU.subtract))
                dve.tensor_copy(gtot, gnm).then_inc(s["k1_done"], 1)
                dve.wait_ge(s["gate_exp"], 1)
                dve.wait_ge(s["k1_done"], 1)
                run(dve.tensor_reduce(gtot, gexp, AX, ALU.add))
                run(dve.reciprocal(grec, gtot))
                run(dve.tensor_scalar(m.gates[:], gexp, grec, None, ALU.mult))
        phase_end(nc, s)


def selection(nc, m):
    ps = m.ps
    xn = m.rawqf[:, T:2 * T]
    pa = m.rawqf[:, 2 * T:2 * T + NT * A_N].rearrange("p (t n) -> p t n", t=NT)
    imp = pa[:, :, A_IMP]
    onehot = m.tokf[:, 0:NT * KEEP].rearrange("p (t n) -> p t n", t=NT)
    score = m.tokf[:, 2048:2048 + T]
    spread = m.tokf[:, 3072:3072 + T].rearrange("p (t n) -> p t n", t=NT)
    junk = m.obuf[:, 0:T]
    sm = m.small
    cnt = sm[:, 160:192].rearrange("p (t n) -> p t n", t=NT)
    rank, kept, far, pos = sm[:, 192:200], sm[:, 200:208], sm[:, 208:216], sm[:, 216:224]
    with ExitStack() as stack:
        s = open_sems(nc, stack, "spread_done turned score_done chain kept_done pos_summed onehot_done gathered")
        with nc.Block() as block:
            @block.tensor
            def _(pe):
                pe.wait_ge(s["spread_done"], 1)
                for t in range(NT):
                    mm = pe.transpose(ps[:, t // 4, (t % 4) * P:(t % 4 + 1) * P], spread[:, t, :], m.ident[:])
                mm.then_inc(s["turned"], 1)
                pe.wait_ge(s["kept_done"], 1)
                mm = pe.matmul(ps[:, 2, 0:NT], m.before[:], kept, start=True, stop=True)
                for t in range(NT - 1):
                    mm = pe.matmul(ps[:, 2, t + 1:NT], m.ones[:], kept[:, t:t + 1].to_broadcast([P, NT - 1 - t]),
                                   start=False, stop=True, skip_group_check=True)
                mm.then_inc(s["pos_summed"], 1)
                pe.wait_ge(s["onehot_done"], NT)
                for t in range(NT):
                    mm = pe.matmul(ps[:, 3, 0:KEEP], xn[:, t * P:(t + 1) * P], onehot[:, t, :],
                                   start=(t == 0), stop=(t == NT - 1))
                mm.then_inc(s["gathered"], 1)

            @block.scalar
            def _(act):
                act.wait_ge(s["turned"], 1)
                for k in range(2):
                    act.copy(score[:, k * CH:(k + 1) * CH], ps[:, k, :]).then_inc(s["score_done"], 1)
                act.wait_ge(s["gathered"], 1)
                act.copy(m.selT[:], ps[:, 3, 0:KEEP])

            @block.vector
            def _(dve):
                run = in_order(dve, s["chain"])
                dve.tensor_copy(spread, imp.unsqueeze(2).to_broadcast([P, NT, P])).then_inc(s["spread_done"], 1)
                run(dve.memset(cnt, 0.0))
                dve.wait_ge(s["score_done"], 2)
                for t in range(NT):
                    own = imp[:, t:t + 1]
                    lo, hi = t * P, (t + 1) * P
                    if t > 0:
                        run(dve.tensor_scalar(junk[:, 0:lo], score[:, 0:lo], own, None, ALU.is_ge, ALU.add,
                                              accum_out=cnt[:, t, 0:1]))
                    if t < NT - 1:
                        run(dve.tensor_scalar(junk[:, hi:T], score[:, hi:T], own, None, ALU.is_gt, ALU.add,
                                              accum_out=cnt[:, t, 1:2]))
                    run(dve.tensor_scalar(junk[:, lo:hi], score[:, lo:hi], own, None, ALU.is_gt, ALU.add,
                                          accum_out=cnt[:, t, 2:3]))
                    run(dve.scalar_tensor_tensor(out=junk[:, lo:hi], in0=score[:, lo:hi], scalar=own,
                                                 in1=m.below[:], op0=ALU.is_equal, op1=ALU.mult,
                                                 accum_out=cnt[:, t, 3:4]))
                run(dve.tensor_reduce(rank, cnt, AX, ALU.add))
                dve.tensor_scalar(kept, rank, float(KEEP), None, ALU.is_lt).then_inc(s["kept_done"], 1)
                dve.wait_ge(s["kept_done"], 1)
                run(dve.tensor_scalar(far, kept, -4.0 * T, 4.0 * T, ALU.mult, ALU.add))
                dve.wait_ge(s["pos_summed"], 1)
                run(dve.tensor_tensor(pos, ps[:, 2, 0:NT], far, ALU.add))
                for t in range(NT):
                    dve.tensor_scalar(onehot[:, t, :], m.iota[:], pos[:, t:t + 1], None, ALU.is_equal)\
                        .then_inc(s["onehot_done"], 1)
        phase_end(nc, s)


def units():
    found = []
    for c in range(NC):
        for j in range((c + 1) * CH // P):
            q0 = max(c * CH, j * P)
            found.append((0, c, j, q0, (c + 1) * CH - q0))
    for c in range(NC):
        for j in range(KEEP // P):
            found.append((1, c, j, c * CH, CH))
    for c in range(NC):
        for j in range(NT):
            q0, q1 = max(c * CH, j * P), min((c + 1) * CH, j * P + WN)
            if q0 < q1:
                found.append((2, c, j, q0, q1 - q0))
    return found


UNITS = units()
SUMS = [(br, c) for br in range(3) for c in range(NC)]
LAST = [max(u for u, x in enumerate(UNITS) if x[:2] == k) for k in SUMS]


def steps():
    todo = []
    for t in range(NT):
        todo.append(("q", t))
    todo.append(("rotate", "q"))
    todo.append(("split", "q1"))
    for t in range(NT):
        todo.append(("k", t))
    for t in range(2):
        todo.append(("s", t))
    for h in range(HG):
        todo += [("turn_q1", h, k) for k in range(2)]
    todo.append(("split", "q"))
    first = [("max0", h, i, part) for h in range(HG) for i in range(NT) for part in range(1 + (i >= NT // 2))]
    half = len(first) // 2
    todo += first[:half]
    for h in range(HG):
        todo += [("turn_q", h, k) for k in range(2)]
    todo.append(("rotate", "k"))
    todo.append(("split", "k"))
    todo += first[half:]
    todo.append(("rows", 0))
    for h in range(HG):
        todo += [("turn_k", h, k) for k in range(2)]
    todo.append(("rotate", "s"))
    todo.append(("split", "s"))
    todo += [("turn_s", k) for k in range(2)]
    later = [("max1", h, k) for h in range(HG) for k in range(NT // 2)] + \
            [("max2", h, k) for h in range(HG) for k in range(NT // 2)]
    done = [u for u in range(len(UNITS)) if UNITS[u][0] == 0]
    per = -(-len(later) // (len(done) - 1))

    def unit(u):
        if u < len(UNITS):
            todo.append(("scores", u))
        if u > 0:
            todo.append(("products", u - 1))
            if u - 1 in LAST:
                todo.append(("sum", LAST.index(u - 1)))

    for u in done:
        unit(u)
        todo.extend(later[:per])
        later = later[per:]
    todo += later
    todo += [("rows", 1), ("rows", 2)]
    for u in range(len(done), len(UNITS) + 1):
        unit(u)
    todo += [("proj", c) for c in range(NC)]
    return todo


STEPS = steps()
FILLS = [x for x in STEPS if x[0] not in ("rotate", "split", "scores", "products", "sum")]
BY_ACT = ("q", "k", "s", "turn_q1", "turn_q", "turn_k", "turn_s")
SPARE = 6


def emptied(n, act):
    return sum((x[0] in BY_ACT) == act for x in FILLS[:n])


def up_to(kind):
    return max(n for n, x in enumerate(FILLS) if x[0] == kind) + 1


SPLITS = {x[1]: n + 1 for n, x in enumerate(y for y in STEPS if y[0] == "split")}


def head_group(nc, m, g):
    ps, d = m.ps, m.d
    q_parts = {"q": (m.qa, m.qb), "q1": (m.q1a, m.q1b)}
    raw = {"q": m.rawq[:], "q1": m.rawq[:], "k": m.rawk, "s": m.raws}
    stack = ExitStack()
    s = open_sems(nc, stack, "loaded fill_ready emptied_act emptied_dve rotated hi_done split_done "
                             "q_rows1 q_rows k_twice max_rows scores_ready exp_done products_done "
                             "inverse_done banks_free o_done rotation partial_set max_done")
    neg = m.small
    negs = [neg[:, 256 + k * HG * NT:256 + (k + 1) * HG * NT] for k in range(3)]
    partial = neg[:, 352:352 + HG * NT * 2].rearrange("p (h t a) -> p h t a", h=HG, t=NT)
    mrows = m.mrow

    def spare(n):
        return ps[:, SPARE + n % 2, :]

    with nc.Block() as block:
        @block.sync
        def _(sp):
            sp.dma_start(m.wq_g[:, 0:2 * P], d["wq"][g]).then_inc(s["loaded"], 16)
            sp.dma_start(m.wq_g[:, 2 * P:3 * P], m.wqp[:, g, :]).then_inc(s["loaded"], 16)
            sp.dma_start(m.wk_g[:], d["wk"][g]).then_inc(s["loaded"], 16)
            sp.dma_start(m.ws_g[:], d["ws"][g]).then_inc(s["loaded"], 16)
            sp.dma_start(m.wproj_g[:], d["wproj_g"][g]).then_inc(s["loaded"], 16)
            sp.dma_start(m.wvp_g[:], m.wvp[:, g, :]).then_inc(s["loaded"], 16)
            sp.wait_ge(s["emptied_act"], emptied(up_to("turn_q1"), True))
            sp.dma_start(m.q1b[0:HD].bitcast(F32), m.q1a[0:HD].bitcast(F32)).then_inc(s["q_rows1"], 16)
            sp.wait_ge(s["emptied_act"], emptied(up_to("turn_q"), True))
            sp.dma_start(m.qb[0:HD].bitcast(F32), m.qa[0:HD].bitcast(F32)).then_inc(s["q_rows"], 16)
            sp.wait_ge(s["emptied_dve"], emptied(FILLS.index(("rows", 0)) + 1, False))
            sp.dma_start(m.q1b[64:65].rearrange("p h n -> p (h n)").bitcast(F32), mrows)\
                .then_inc(s["max_rows"], 16)
            sp.wait_ge(s["emptied_act"], emptied(up_to("turn_k"), True))
            sp.dma_start(m.kwa[HD:P].bitcast(F32), m.kwa[0:HD].bitcast(F32)).then_inc(s["k_twice"], 16)
            sp.wait_ge(s["emptied_act"], emptied(up_to("turn_s"), True))
            sp.dma_start(m.ksa[HD:P].bitcast(F32), m.ksa[0:HD].bitcast(F32)).then_inc(s["k_twice"], 16)
            for br in (1, 2):
                sp.wait_ge(s["emptied_dve"], emptied(FILLS.index(("rows", br)) + 1, False))
                sp.dma_start(m.qb[63 + br:64 + br].rearrange("p h n -> p (h n)").bitcast(F32), mrows)\
                    .then_inc(s["max_rows"], 16)

        @block.tensor
        def _(pe):
            waited = set()

            def once(name, count):
                if (name, count) not in waited:
                    waited.add((name, count))
                    pe.wait_ge(s[name], count)

            def turn(n, name, h, k):
                once("split_done", SPLITS[name])
                for i in range(4):
                    mm = pe.transpose(spare(n)[:, i * P:(i + 1) * P], m.tok[:, 4 * k + i, h, :], m.ident[:])
                return mm

            def fill(n, kind, *a):
                if n >= 2:
                    by_act = FILLS[n - 2][0] in BY_ACT
                    pe.wait_ge(s["emptied_act" if by_act else "emptied_dve"], emptied(n - 1, by_act))
                bank = spare(n)
                if kind == "q":
                    once("loaded", 96)
                    mm = pe.matmul(bank[:, 0:3 * P], m.cqT[:, a[0] * P:(a[0] + 1) * P], m.wq_g[:],
                                   start=True, stop=True)
                elif kind == "k":
                    mm = pe.matmul(bank[:, 0:3 * P], m.xnT[:, a[0] * P:(a[0] + 1) * P], m.wk_g[:],
                                   start=True, stop=True)
                elif kind == "s":
                    mm = pe.matmul(bank[:, 0:3 * P], m.selT[:, a[0] * P:(a[0] + 1) * P], m.ws_g[:],
                                   start=True, stop=True)
                elif kind == "turn_q1":
                    mm = turn(n, "q1", *a)
                elif kind == "turn_q":
                    mm = turn(n, "q", *a)
                elif kind == "turn_k":
                    mm = turn(n, "k", *a)
                elif kind == "turn_s":
                    once("split_done", SPLITS["s"])
                    for i in range(4):
                        mm = pe.transpose(bank[:, i * P:(i + 1) * P], m.tok[:, i % 2, 2 * a[0] + i // 2, :],
                                          m.ident[:])
                elif kind == "max0":
                    h, i, part = a
                    once("emptied_act", emptied(up_to("turn_q1"), True))
                    k0, k1 = part * CH, min((part + 1) * CH, (i + 1) * P)
                    own = k1 == (i + 1) * P
                    mm = pe.matmul(bank[:, 0:k1 - k0], m.q1a[:, h, i * P:(i + 1) * P], m.k1a[:, k0:k1],
                                   start=True, stop=True)
                    if own:
                        mm = pe.matmul(bank[:, k1 - k0 - P:k1 - k0], m.ident_bf[:], m.causal_q[:],
                                       start=False, stop=True, skip_group_check=True)
                elif kind == "max1":
                    h, k = a
                    once("k_twice", 32)
                    once("emptied_act", emptied(up_to("turn_q"), True))
                    for i in range(2):
                        t = 2 * k + i
                        mm = pe.matmul(bank[:, i * KEEP:(i + 1) * KEEP], m.qa[:, h, t * P:(t + 1) * P],
                                       m.ksa[:, h, :], start=True, stop=True)
                elif kind == "max2":
                    h, k = a
                    once("k_twice", 32)
                    for i in range(2):
                        t = 2 * k + i
                        k0 = max(0, t * P - WINDOW)
                        pe.matmul(bank[:, i * KEEP:i * KEEP + WN], m.qa[:, h, t * P:(t + 1) * P],
                                  m.kwa[:, h, k0:k0 + WN], start=True, stop=True, skip_group_check=True)
                        mm = pe.matmul(bank[:, i * KEEP:i * KEEP + WN], m.ident_bf[:],
                                       m.window_q0[:] if t == 0 else m.window_q[:], start=False, stop=True,
                                       skip_group_check=True)
                elif kind == "rows":
                    if a[0] == 0:
                        pe.wait_ge(s["max_done"], 1)
                    else:
                        pe.wait_ge(s["emptied_dve"], emptied(up_to(("max1", "max2")[a[0] - 1]), False))
                    mm = pe.transpose(bank[0:HG * NT, 0:P], negs[a[0]], m.ident[:])
                elif kind == "proj":
                    cc = slice(a[0] * CH, (a[0] + 1) * CH)
                    pe.wait_ge(s["o_done"], a[0] + 1)
                    pe.matmul(bank, m.wvp_g[:], m.o1[:, cc], start=True, stop=False)
                    mm = pe.matmul(bank, m.wproj_g[:], m.o2[:, cc], start=False, stop=True)
                mm.then_inc(s["fill_ready"], 1)

            def scores(u):
                br, c, j, q0, w = UNITS[u]
                if br == 0:
                    once("q_rows1", 16)
                    once("max_rows", 16)
                    qx, qy, rows = m.q1a, m.q1b, 65
                else:
                    once("q_rows", 16)
                    once("max_rows", 48)
                    qx, qy, rows = m.qa, m.qb, 66
                for half in range(2):
                    n = 2 * u + half
                    if n >= 2:
                        pe.wait_ge(s["exp_done"], n - 1)
                    for i in range(2):
                        h = 2 * half + i
                        if br == 0:
                            kx, ky = m.k1a[:, j * P:(j + 1) * P], m.k1b[0:rows, j * P:(j + 1) * P]
                        elif br == 1:
                            kx, ky = m.ksa[:, h, j * P:(j + 1) * P], m.ksb[0:rows, h, j * P:(j + 1) * P]
                        else:
                            kx, ky = m.kwa[:, h, j * P:(j + 1) * P], m.kwb[0:rows, h, j * P:(j + 1) * P]
                        bank = ps[:, 2 * half + i, 0:w]
                        pe.matmul(bank, kx, qx[:, h, q0:q0 + w], start=True, stop=False, skip_group_check=True)
                        at = q0 - j * P
                        if br == 0 and at == 0:
                            pe.matmul(bank[:, 0:P], m.ident_bf[:], m.causal_k[:], start=False, stop=False,
                                      skip_group_check=True)
                        if br == 2:
                            pe.matmul(bank, m.ident_bf[:], m.window_k[:, at:at + w], start=False, stop=False,
                                      skip_group_check=True)
                        mm = pe.matmul(bank, ky, qy[0:rows, h, q0:q0 + w], start=False, stop=True,
                                       skip_group_check=True)
                    mm.then_inc(s["scores_ready"], 1)

            def products(u):
                br, c, j, q0, w = UNITS[u]
                pe.wait_ge(s["exp_done"], 2 * u + 2)
                k = SUMS.index((br, c))
                first = u == 0 or u - 1 in LAST
                if first and k > 0:
                    pe.wait_ge(s["banks_free"], k)
                for bank in (4, 5):
                    for h in range(HG):
                        if bank == 5:
                            w_ = m.ones[:, 0:VD]
                        elif br == 0:
                            w_ = m.v1[:, j, :]
                        elif br == 1:
                            w_ = m.vs[:, j, h * VD:(h + 1) * VD]
                        else:
                            w_ = m.vw[:, j, h * VD:(h + 1) * VD]
                        mm = pe.matmul(ps[h * VD:(h + 1) * VD, bank, q0 - c * CH:q0 - c * CH + w], w_,
                                       m.prob[:, u % 2, h, 0:w], start=first, stop=True, skip_group_check=True)
                mm.then_inc(s["products_done"], 1)

            n = 0
            for step in STEPS:
                if step[0] == "scores":
                    scores(step[1])
                elif step[0] == "products":
                    products(step[1])
                elif step in FILLS:
                    fill(n, *step)
                    n += 1

        @block.scalar
        def _(act):
            n = 0
            for step in STEPS:
                kind = step[0]
                if kind == "scores":
                    br, c, j, q0, w = UNITS[step[1]]
                    for half in range(2):
                        act.wait_ge(s["scores_ready"], 2 * step[1] + half + 1)
                        if step[1] >= 2:
                            act.wait_ge(s["products_done"], step[1] - 1)
                        act.activation(m.prob[:, step[1] % 2, 2 * half:2 * half + 2, 0:w],
                                       ps[:, 2 * half:2 * half + 2, 0:w], ACT.Exp, scale=SCALE)\
                            .then_inc(s["exp_done"], 1)
                if step not in FILLS:
                    continue
                n += 1
                if kind not in BY_ACT:
                    continue
                act.wait_ge(s["fill_ready"], n)
                bank = spare(n - 1)
                if kind == "q":
                    ins = act.copy(m.rawq[:, step[1], :], bank[:, 0:3 * P])
                elif kind == "k":
                    act.copy(m.rawk[:, step[1], :], bank[:, 0:2 * P])
                    ins = act.copy(m.vw[:, step[1], :], bank[:, 2 * P:3 * P])
                elif kind == "s":
                    act.copy(m.raws[:, step[1], :], bank[:, 0:2 * P])
                    ins = act.copy(m.vs[:, step[1], :], bank[:, 2 * P:3 * P])
                elif kind in ("turn_q1", "turn_q"):
                    _, h, k = step
                    dst = m.q1a if kind == "turn_q1" else m.qa
                    ins = act.copy(dst[:, h, k * CH:(k + 1) * CH], bank)
                elif kind == "turn_k":
                    _, h, k = step
                    act.copy(m.kwa[0:HD, h, k * CH:(k + 1) * CH], bank[0:HD, :])
                    ins = act.copy(m.kwb[0:HD, h, k * CH:(k + 1) * CH], bank[HD:P, :])
                elif kind == "turn_s":
                    hh = slice(2 * step[1], 2 * step[1] + 2)
                    act.copy(m.ksa[0:HD, hh, :], bank[0:HD, :].rearrange("p (h n) -> p h n", h=2))
                    ins = act.copy(m.ksb[0:HD, hh, :], bank[HD:P, :].rearrange("p (h n) -> p h n", h=2))
                ins.then_inc(s["emptied_act"], 1)

        @block.gpsimd
        def _(pool):
            run = in_order(pool, s["rotation"])
            for step in STEPS:
                if step[0] == "rotate":
                    pool.wait_ge(s["emptied_act"], emptied(up_to(step[1]), True))
                    r = raw[step[1]]
                    nt = r.shape[1]
                    xr, xi = [r[:, :, P + k * HG * HALF:P + (k + 1) * HG * HALF]
                              .rearrange("p t (h n) -> p t h n", h=HG) for k in range(2)]
                    co, si = [x[:, 0:nt, :].unsqueeze(2).to_broadcast([P, nt, HG, HALF]) for x in (m.cos, m.sin)]
                    ta, tb, tc = [x[:, 0:nt * HG * HALF].rearrange("p (t h n) -> p t h n", t=nt, h=HG)
                                  for x in m.rope_tmp]
                    pool.tensor_tensor(ta, xr, co, ALU.mult)
                    pool.tensor_tensor(tb, xi, si, ALU.mult)
                    run(pool.tensor_tensor(tc, xr, si, ALU.mult))
                    run(pool.tensor_tensor(xr, ta, tb, ALU.subtract))
                    run(pool.tensor_tensor(ta, xi, co, ALU.mult))
                    run(pool.tensor_tensor(xi, tc, ta, ALU.add))
                elif step[0] == "split":
                    name = step[1]
                    pool.wait_ge(s["hi_done"], SPLITS[name])
                    for at, src in split_pieces(raw[name], name):
                        nt, w = src.shape[1], src.shape[3]
                        ins = pool.tensor_tensor(m.tok[:, 0:nt, :, HD + at:HD + at + w].bitcast(F32R), src,
                                                 m.tok[:, 0:nt, :, at:at + w], ALU.subtract)
                    ins.then_inc(s["split_done"], 1)

        @block.vector
        def _(dve):
            dve.memset(partial, -3.0e38).then_inc(s["partial_set"], 1)
            dve.wait_ge(s["partial_set"], 1)
            n = 0
            for step in STEPS:
                kind = step[0]
                if kind == "split":
                    name = step[1]
                    before_ = {"q": "turn_q1", "k": "turn_q", "s": "turn_k"}.get(name)
                    if before_:
                        dve.wait_ge(s["fill_ready"], up_to(before_))
                    dve.wait_ge(s["rotation"], 4 * ROTATED[name])
                    for at, src in split_pieces(raw[name], name):
                        nt, w = src.shape[1], src.shape[3]
                        ins = dve.tensor_copy(m.tok[:, 0:nt, :, at:at + w].bitcast(F32R), src)
                    ins.then_inc(s["hi_done"], 1)
                elif kind == "sum":
                    k = step[1]
                    br, c = SUMS[k]
                    cc = slice(c * CH, (c + 1) * CH)
                    dve.wait_ge(s["products_done"], LAST[k] + 1)
                    dve.reciprocal(m.rden, ps[:, 5, :]).then_inc(s["inverse_done"], 1)
                    dve.wait_ge(s["inverse_done"], k + 1)
                    dst = (m.o1[:, cc], m.o2[:, cc], m.rden)[br]
                    dve.scalar_tensor_tensor(out=dst, in0=ps[:, 4, :], scalar=m.gates[:, br:br + 1], in1=m.rden,
                                             op0=ALU.mult, op1=ALU.mult).then_inc(s["banks_free"], 1)
                    dve.wait_ge(s["banks_free"], k + 1)
                    if br == 2:
                        dve.tensor_tensor(m.o2[:, cc], m.o2[:, cc], m.rden, ALU.add).then_inc(s["o_done"], 1)
                        dve.wait_ge(s["o_done"], c + 1)
                if step not in FILLS:
                    continue
                n += 1
                if kind in BY_ACT:
                    continue
                bank = spare(n - 1)
                if step == ("rows", 0):
                    dve.wait_ge(s["emptied_dve"], emptied(up_to("max0"), False))
                    dve.tensor_reduce(negs[0], partial, AX, ALU.max, negate=True).then_inc(s["max_done"], 1)
                dve.wait_ge(s["fill_ready"], n)
                if kind == "max0":
                    _, h, i, part = step
                    w = min((part + 1) * CH, (i + 1) * P) - part * CH
                    ins = dve.tensor_reduce(partial[:, h, i, part:part + 1], bank[:, 0:w], AX, ALU.max)
                elif kind in ("max1", "max2"):
                    _, h, k = step
                    w = KEEP if kind == "max1" else WN
                    at = h * NT + 2 * k
                    ins = dve.tensor_reduce(negs[1 if kind == "max1" else 2][:, at:at + 2],
                                            bank.rearrange("p (i n) -> p i n", i=2)[:, :, 0:w], AX, ALU.max,
                                            negate=True)
                elif kind == "rows":
                    if step[1] > 0:
                        dve.wait_ge(s["max_rows"], 16 * step[1])
                    ins = dve.tensor_copy(mrows.bitcast(F32R), bank[0:HG * NT, 0:P])
                else:
                    cc = slice(step[1] * CH, (step[1] + 1) * CH)
                    ins = dve.tensor_tensor(m.t2[:, cc], m.t2[:, cc], bank, ALU.add)
                ins.then_inc(s["emptied_dve"], 1)
    phase_end(nc, s)
    stack.close()


def experts_part(nc, d, t2_dram, out, ps, ident, eps, sb):
    w1h, w1l, w3h, w3l = [sb(n, [C, NE * HID], F32R) for n in ("w1h", "w1l", "w3h", "w3l")]
    w2 = sb("w2", [P, NE, len(HT), C])
    router = sb("router", [C, NE])
    each = sb("each", [NE, NE, P])
    tie = sb("tie", [P, NE, NE])
    stage = [sb(f"stage{k}", [C, NE * HID]) for k in range(2)]
    t2 = sb("t2b", [C, T])
    t_tok = sb("t_tok", [P, NT, P])
    xn = sb("xn", [P, NT, P])
    xf = sb("xf", [C, T])
    xh = sb("xh", [C, T], F32R)
    xl = sb("xl", [C, T], F32R)
    st = sb("st", [P, NT, 6])
    mv = sb("mv", [P, NT, 2])
    std, rstd, top, tot, inv = [sb(n, [P, NT]) for n in ("std", "rstd", "top", "tot", "inv")]
    pr = sb("pr", [P, NT, NE])
    gt = sb("gt", [P, NT, NE])
    rank = sb("rank", [P, NT, NE])
    more = sb("more", [P, NT, NE * NE])
    same = sb("same", [P, NT, NE * NE])
    gT = sb("gT", [NE, T])
    act_s = sb("act_s", [P, 2, CH])
    mid = sb("mid", [P, 2, CH])
    hid = sb("hid", [P, 2, CH])
    res = sb("res", [C, 2, CH])

    with ExitStack() as stack:
        s = open_sems(nc, stack, "loaded w1_loaded w3_loaded hi_done lo_done")
        with nc.Block() as block:
            @block.sync
            def _(sp):
                sp.dma_start(stage[0][:], d["w1"]).then_inc(s["w1_loaded"], 16)
                sp.dma_start(stage[1][:], d["w3"]).then_inc(s["w3_loaded"], 16)
                sp.dma_start(router[:], d["router"]).then_inc(s["loaded"], 16)
                sp.dma_start(each[:], d["each"]).then_inc(s["loaded"], 16)
                sp.dma_start(tie[:], d["tie"]).then_inc(s["loaded"], 16)
                for k, (at, rows) in enumerate(HT):
                    sp.dma_start(w2[0:rows, :, k, :], d["w2"][:, at:at + rows, :].rearrange("e r c -> r e c"))\
                        .then_inc(s["loaded"], 16)
                sp.wait_ge(s["loaded"], 16 * 6)

            @block.vector
            def _(dve):
                for k, (hi, lo) in enumerate(((w1h, w1l), (w3h, w3l))):
                    dve.wait_ge(s["w1_loaded" if k == 0 else "w3_loaded"], 16)
                    dve.tensor_copy(hi[:], stage[k][:]).then_inc(s["hi_done"], 1)
                    dve.wait_ge(s["hi_done"], k + 1)
                    dve.tensor_tensor(lo[:], stage[k][:], hi[:].bitcast(F32), ALU.subtract).then_inc(s["lo_done"], 1)
        phase_end(nc, s)

    with nc.Fori(0, B) as b:
        with ExitStack() as stack:
            s = open_sems(nc, stack, "t2_loaded t2_turned t_copied stats aggregated std_done rstd_done xn_done "
                                     "xn_turned xf_done xh_done xl_done logits shifted exp_done chain gates_done "
                                     "gates_turned gT_done h1_ready h3_ready g_ready silu_done mid_done hid_done "
                                     "y_ready res_done stored used")
            WORK = [(c, e, k) for c in range(NC) for e in range(NE) for k in range(len(HT))]
            K = len(HT)
            with nc.Block() as block:
                @block.sync
                def _(sp):
                    sp.dma_start(t2[:], t2_dram[b]).then_inc(s["t2_loaded"], 16)
                    for c in range(NC):
                        sp.wait_ge(s["res_done"], c + 1)
                        sp.dma_start(out[b, :, c * CH:(c + 1) * CH], res[:, c, :]).then_inc(s["stored"], 16)
                    sp.wait_ge(s["stored"], 16 * NC)

                @block.tensor
                def _(pe):
                    pe.wait_ge(s["t2_loaded"], 16)
                    for t in range(NT):
                        mm = pe.transpose(ps[:, t // 4, (t % 4) * P:(t % 4 + 1) * P], t2[:, t * P:(t + 1) * P],
                                          ident[:])
                        if t % 4 == 3:
                            mm.then_inc(s["t2_turned"], 1)
                    for t in range(NT):
                        pe.wait_ge(s["xn_done"], t + 1)
                        mm = pe.transpose(ps[:, 2 + t // 4, (t % 4) * P:(t % 4 + 1) * P], xn[:, t, :], ident[:])
                        if t % 4 == 3:
                            mm.then_inc(s["xn_turned"], 1)
                    for t in range(NT):
                        pe.wait_ge(s["xf_done"], t // 4 + 1)
                        mm = pe.matmul(ps[:, 4, t * NE:(t + 1) * NE], xf[:, t * P:(t + 1) * P], router[:],
                                       start=True, stop=True)
                    mm.then_inc(s["logits"], 1)
                    pe.wait_ge(s["xh_done"], 2)
                    pe.wait_ge(s["xl_done"], 2)

                    def hidden(n):
                        c, e, k = WORK[n]
                        at, rows = HT[k]
                        if n >= 2:
                            pe.wait_ge(s["mid_done"], n - 1)
                        ww = slice(e * HID + at, e * HID + at + rows)
                        cc = slice(c * CH, (c + 1) * CH)
                        for bank, wh, wl, name in ((n % 2, w1h, w1l, "h1_ready"), (2 + n % 2, w3h, w3l, "h3_ready")):
                            pe.matmul(ps[0:rows, bank, :], wh[:, ww], xh[:, cc], start=True, stop=False)
                            pe.matmul(ps[0:rows, bank, :], wh[:, ww], xl[:, cc], start=False, stop=False)
                            pe.matmul(ps[0:rows, bank, :], wl[:, ww], xh[:, cc], start=False, stop=True)\
                                .then_inc(s[name], 1)

                    def gate(i):
                        c, e = divmod(i, NE)
                        if i >= 2:
                            pe.wait_ge(s["hid_done"], K * (i - 1))
                        pe.matmul(ps[:, 4 + i % 2, :], each[:, e, :], gT[:, c * CH:(c + 1) * CH],
                                  start=True, stop=True).then_inc(s["g_ready"], 1)

                    def output(n):
                        c, e, k = WORK[n]
                        rows = HT[k][1]
                        pe.wait_ge(s["hid_done"], n + 1)
                        mm = pe.matmul(ps[:, 6 + c, :], w2[0:rows, e, k, :], hid[0:rows, n % 2, :],
                                       start=(e == 0 and k == 0), stop=(e == NE - 1 and k == K - 1))
                        mm.then_inc(s["used"], 1)

                    hidden(0)
                    hidden(1)
                    pe.wait_ge(s["gates_done"], 1)
                    for t in range(NT):
                        mm = pe.transpose(ps[0:NE, 5 + t // 4, (t % 4) * P:(t % 4 + 1) * P], gt[:, t, :], ident[:])
                    mm.then_inc(s["gates_turned"], 1)
                    pe.wait_ge(s["gT_done"], 2)
                    gate(0)
                    for n in range(len(WORK)):
                        if n + 2 < len(WORK):
                            if n % K == 0 and n // K + 1 < NC * NE:
                                gate(n // K + 1)
                            hidden(n + 2)
                        output(n)
                        if n in (len(WORK) // NC - 1, len(WORK) - 1):
                            pass

                @block.scalar
                def _(act):
                    for k in range(2):
                        act.wait_ge(s["t2_turned"], k + 1)
                        act.copy(t_tok[:, 4 * k:4 * k + 4, :], ps[:, k, :].rearrange("p (t n) -> p t n", t=4))\
                            .then_inc(s["t_copied"], 1)
                    act.wait_ge(s["aggregated"], NT)
                    act.activation(std[:], mv[:, :, 1], ACT.Sqrt, bias=eps[:, 0:1]).then_inc(s["std_done"], 1)
                    for k in range(2):
                        act.wait_ge(s["xn_turned"], k + 1)
                        kk = slice(k * CH, (k + 1) * CH)
                        act.copy(xf[:, kk], ps[:, 2 + k, :]).then_inc(s["xf_done"], 1)
                        act.copy(xh[:, kk], ps[:, 2 + k, :]).then_inc(s["xh_done"], 1)
                    act.wait_ge(s["shifted"], 1)
                    act.activation(pr[:], pr[:], ACT.Exp).then_inc(s["exp_done"], 1)
                    act.wait_ge(s["gates_turned"], 1)
                    for k in range(2):
                        act.copy(gT[:, k * CH:(k + 1) * CH], ps[0:NE, 5 + k, :]).then_inc(s["gT_done"], 1)
                    for n, (c, e, k) in enumerate(WORK):
                        rows = HT[k][1]
                        act.wait_ge(s["h1_ready"], n + 1)
                        if n >= 2:
                            act.wait_ge(s["mid_done"], n - 1)
                        act.activation(act_s[0:rows, n % 2, :], ps[0:rows, n % 2, :], ACT.Silu)\
                            .then_inc(s["silu_done"], 1)

                @block.vector
                def _(dve):
                    run = in_order(dve, s["chain"])
                    for t in range(NT):
                        dve.wait_ge(s["t_copied"], t // 4 + 1)
                        dve.bn_stats(st[:, t, :], t_tok[:, t, :]).then_inc(s["stats"], 1)
                    dve.wait_ge(s["stats"], NT)
                    for t in range(NT):
                        dve.bn_aggr(mv[:, t, :], st[:, t, :]).then_inc(s["aggregated"], 1)
                    dve.wait_ge(s["std_done"], 1)
                    run(dve.reciprocal(rstd[:], std[:]))
                    for t in range(NT):
                        dve.tensor_scalar(xn[:, t, :], t_tok[:, t, :], mv[:, t, 0:1], rstd[:, t:t + 1],
                                          ALU.subtract, ALU.mult).then_inc(s["xn_done"], 1)
                    for k in range(2):
                        kk = slice(k * CH, (k + 1) * CH)
                        dve.wait_ge(s["xh_done"], k + 1)
                        dve.tensor_tensor(xl[:, kk], ps[:, 2 + k, :], xh[:, kk].bitcast(F32), ALU.subtract)\
                            .then_inc(s["xl_done"], 1)
                    dve.wait_ge(s["logits"], 1)
                    lg = ps[:, 4, 0:NT * NE].rearrange("p (t e) -> p t e", t=NT)
                    run(dve.tensor_reduce(top[:], lg, AX, ALU.max))
                    dve.tensor_tensor(pr[:], lg, each_tile(top[:], NE), ALU.subtract).then_inc(s["shifted"], 1)
                    dve.wait_ge(s["exp_done"], 1)
                    run(dve.tensor_reduce(tot[:], pr[:], AX, ALU.add))
                    run(dve.reciprocal(inv[:], tot[:]))
                    run(dve.tensor_tensor(pr[:], pr[:], each_tile(inv[:], NE), ALU.mult))
                    other = pr[:].unsqueeze(2).to_broadcast([P, NT, NE, NE])
                    own = pr[:].unsqueeze(3).to_broadcast([P, NT, NE, NE])
                    more4 = more[:].rearrange("p t (a b) -> p t a b", a=NE)
                    same4 = same[:].rearrange("p t (a b) -> p t a b", a=NE)
                    run(dve.tensor_tensor(more4, other, own, ALU.is_gt))
                    run(dve.tensor_tensor(same4, other, own, ALU.is_equal))
                    run(dve.tensor_tensor(same[:], same[:], each_token(tie[:].rearrange("p a b -> p (a b)"), NT),
                                          ALU.mult))
                    run(dve.tensor_tensor(more[:], more[:], same[:], ALU.add))
                    run(dve.tensor_reduce(rank[:], more4, AX, ALU.add))
                    run(dve.tensor_scalar(rank[:], rank[:], 1.5, None, ALU.is_lt))
                    run(dve.tensor_tensor(gt[:], pr[:], rank[:], ALU.mult))
                    run(dve.tensor_reduce(tot[:], gt[:], AX, ALU.add))
                    run(dve.tensor_scalar(tot[:], tot[:], 1e-9, None, ALU.add))
                    run(dve.reciprocal(inv[:], tot[:]))
                    dve.tensor_tensor(gt[:], gt[:], each_tile(inv[:], NE), ALU.mult).then_inc(s["gates_done"], 1)
                    for n, (c, e, k) in enumerate(WORK):
                        rows = HT[k][1]
                        dve.wait_ge(s["h3_ready"], n + 1)
                        dve.wait_ge(s["silu_done"], n + 1)
                        dve.tensor_tensor(mid[0:rows, n % 2, :], ps[0:rows, 2 + n % 2, :], act_s[0:rows, n % 2, :],
                                          ALU.mult).then_inc(s["mid_done"], 1)
                        if k == 0:
                            dve.wait_ge(s["g_ready"], n // K + 1)
                        dve.wait_ge(s["mid_done"], n + 1)
                        if n >= 2:
                            dve.wait_ge(s["used"], n - 1)
                        dve.tensor_tensor(hid[0:rows, n % 2, :], ps[0:rows, 4 + (n // K) % 2, :],
                                          mid[0:rows, n % 2, :], ALU.mult).then_inc(s["hid_done"], 1)
                        if e == NE - 1 and k == K - 1:
                            cc = slice(c * CH, (c + 1) * CH)
                            dve.wait_ge(s["used"], n + 1)
                            dve.tensor_tensor(res[:, c, :], ps[:, 6 + c, :], t2[:, cc], ALU.add)\
                                .then_inc(s["res_done"], 1)
            phase_end(nc, s)


def split_pieces(r, name):
    at = 2 * P if name == "q1" else 0
    heads = "p t (h n) -> p t h n"
    found = [(0, r[:, :, at:at + P].rearrange(heads, h=HG))]
    if name != "q":
        n = HG * HALF
        found += [(NOPE + k * HALF, r[:, :, P + k * n:P + (k + 1) * n].rearrange(heads, h=HG)) for k in range(2)]
    return found


ROTATED = {"q1": 1, "q": 1, "k": 2, "s": 3}


def by_group(w, n):
    w = w.reshape(w.shape[0], NG, HG, -1)
    parts = np.split(w, np.cumsum(n)[:-1], axis=3)
    return [p.reshape(w.shape[0], NG, -1).transpose(1, 0, 2) for p in parts]


def kernel(**inputs):
    import concourse.bacc as bacc
    from concourse.bass_utils import run_bass_kernel_spmd
    from ml_dtypes import bfloat16

    f = {k: np.asarray(x) for k, x in inputs.items()}
    c_, a_, e_ = ({k[len(p):]: x for k, x in f.items() if k.startswith(p)} for p in ("L0_conv_", "L1_attn_", "L1_ffn_"))
    arrays = {"x": f["x"].reshape(B, C, T)}
    a, b = np.arange(P)[:, None], np.arange(P)[None]
    w = np.arange(WN)[None]
    arrays["ident"] = np.eye(P, dtype=np.float32)
    arrays["ident_bf"] = np.eye(P).astype(bfloat16)
    arrays["causal_q"] = np.where(b <= a, 0, MASKED).astype(bfloat16)
    arrays["causal_k"] = np.where(a <= b, 0, MASKED).astype(bfloat16)
    arrays["window_q0"] = np.where((w <= a) & (a - w < WINDOW), 0, MASKED).astype(bfloat16)
    arrays["window_q"] = np.where((w > a) & (w <= a + WINDOW), 0, MASKED).astype(bfloat16)
    arrays["window_k"] = np.where((w >= a) & (w - a < WINDOW), 0, MASKED).astype(bfloat16)
    freq = 1.0 / 10000.0 ** (np.arange(0, 2 * HALF, 2, dtype=np.float32) / (2 * HALF))
    angle = np.outer(np.arange(T, dtype=np.float32), freq)
    for name, fn in (("cos", np.cos), ("sin", np.sin)):
        arrays[name] = fn(angle).astype(np.float32).reshape(NT, P, HALF).transpose(1, 0, 2)
    arrays["before"] = (a < b).astype(np.float32)
    arrays["below"] = (b < a).astype(np.float32)
    arrays["iota"] = np.broadcast_to(np.arange(KEEP, dtype=np.float32), (P, KEEP))
    arrays["each"] = np.broadcast_to(np.eye(NE, dtype=np.float32)[:, :, None], (NE, NE, P))
    arrays["tie"] = np.broadcast_to(np.tril(np.ones((NE, NE), np.float32), -1), (P, NE, NE))
    twice = lambda x: np.concatenate([x, x], axis=-1)
    arrays["wt2"], arrays["wp2"] = twice(c_["Wt"].T), twice(c_["Wp"].T)
    arrays["wg"], arrays["wo"] = c_["Wg"].T, c_["Wo"].T
    arrays["bias"] = np.stack([twice(c_["bt"]), twice(c_["bp"]), twice(c_["bg"]), c_["bo"]], axis=1)
    arrays["wa"] = np.concatenate([a_["Wcq"], a_["Wckv"], a_["Wk_rope"], a_["W_imp"], a_["Wgate"]], axis=1)
    arrays["qnw"] = np.broadcast_to(a_["q_norm_w"], (P, QR))
    arrays["kvnw"] = np.broadcast_to(a_["kv_norm_w"], (P, KVR))
    arrays["wqn_t"] = a_["Wq_nope"].reshape(QR, NG, P).transpose(2, 1, 0)
    arrays["wproj"] = a_["Wproj"].reshape(NG, P, C).transpose(1, 0, 2)
    arrays["wproj_g"] = a_["Wproj"].reshape(NG, P, C)
    for name, x in (("wk_t", a_["Wk_nope"]), ("wv_t", a_["Wv"])):
        arrays[name] = x.reshape(KVR, NG, HG, 32).transpose(1, 2, 3, 0)
    rot = [HALF, HALF]
    arrays["wq"] = np.concatenate(by_group(a_["Wq_nope"], [NOPE]) + by_group(a_["Wq_rope"], rot), axis=2)
    arrays["wk"] = np.concatenate(by_group(a_["Wwin_k"], [NOPE] + rot) + by_group(a_["Wwin_v"], [VD]), axis=2)
    arrays["ws"] = np.concatenate(by_group(a_["Wsel_k"], [NOPE] + rot) + by_group(a_["Wsel_v"], [VD]), axis=2)
    arrays["router"] = e_["router_w"].T
    arrays["w1"] = e_["w1"].reshape(NE * HID, C).T
    arrays["w3"] = e_["w3"].reshape(NE * HID, C).T
    arrays["w2"] = e_["w2"].transpose(0, 2, 1)
    arrays = {k: np.ascontiguousarray(x) for k, x in arrays.items()}

    nc = bacc.Bacc("TRN2", target_bir_lowering=False, num_devices=1)
    d = {k: nc.dram_tensor("in_" + k, x.shape, mybir.dt.from_np(x.dtype), kind="ExternalInput").ap()
         for k, x in arrays.items()}
    out = nc.dram_tensor("out", (B, C, T), F32, kind="ExternalOutput").ap()
    program(nc, d, out)
    r = run_bass_kernel_spmd(nc, [{"in_" + k: x for k, x in arrays.items()}], core_ids=[0])
    return r.results[0]["out"].reshape(B, C, 32, 32)
```

```python
from contextlib import ExitStack

import numpy as np

import concourse.bass as bass
from concourse import mybir

F32 = mybir.dt.float32
F32R = mybir.dt.float32r
BF16 = mybir.dt.bfloat16
ALU = mybir.AluOpType
ACT = mybir.ActivationFunctionType
AX = mybir.AxisListType.X

P = 128
B, C, T = 4, 128, 1024
NT = T // P
CH = 512
NC = T // CH
CI = 64
QR, KVR = 48, 32
NH, HG = 16, 4
NG = NH // HG
HP = HG // 2
NOPE, HALF = 32, 16
HD = NOPE + 2 * HALF
VD = 32
NW, RW = HP * NOPE, HP * HALF
KEEP, WINDOW = 256, 64
SCALE = 1.0 / 8.0
NE, HID = 8, 341
WN = P + WINDOW
LNE, RMSE = 1e-5, 1e-6
MASKED = -8.0e9
A_CQ, A_KV, A_KR, A_IMP, A_GATE, A_N = 0, 48, 80, 112, 113, 116


def phase_end(nc, sems):
    for s in sems.values():
        nc.sync.sem_clear(s)
    nc.all_engine_barrier()


def open_sems(nc, ctx, names):
    return {n: ctx.enter_context(nc.semaphore(n)) for n in names.split()}


def program(nc, d, out):
    with ExitStack() as top:
        def sb(ctx, name, shape, dt=F32):
            return ctx.enter_context(nc.sbuf_tensor(name, shape, dt))

        ps = top.enter_context(nc.psum_tensor("ps", [P, 8, CH], F32))
        t2_dram = nc.dram_tensor("t2_dram", (B, C, T), F32, kind="Internal").ap()
        wqp_dram = nc.dram_tensor("wqp_dram", (NG, QR, 2 * NW), F32, kind="Internal").ap()
        wvp_dram = nc.dram_tensor("wvp_dram", (NG, P, C), F32, kind="Internal").ap()
        d = dict(d, wqp=wqp_dram, wvp=wvp_dram)
        ident = sb(top, "ident", [P, P])
        eps = sb(top, "eps", [P, 2])
        with ExitStack() as att_mem:
            attention_part(nc, d, t2_dram, ps, ident, eps, lambda *a: sb(att_mem, *a))
        with ExitStack() as ffn_mem:
            experts_part(nc, d, t2_dram, out, ps, ident, eps, lambda *a: sb(ffn_mem, *a))


class Mem:
    pass


def attention_part(nc, d, t2_dram, ps, ident, eps, sb):
    m = Mem()
    m.ps, m.d, m.ident, m.eps = ps, d, ident, eps
    m.ident_bf = sb("ident_bf", [P, P], BF16)
    m.causal_q = sb("causal_q", [P, P], BF16)
    m.causal_k = sb("causal_k", [P, P], BF16)
    m.window_q0 = sb("window_q0", [P, WN], BF16)
    m.window_q = sb("window_q", [P, WN], BF16)
    m.window_k = sb("window_k", [P, WN], BF16)
    m.cos = sb("cos", [P, NT, HALF])
    m.sin = sb("sin", [P, NT, HALF])
    m.before = sb("before", [P, P])
    m.below = sb("below", [P, P])
    m.ones = sb("ones", [P, P])
    m.iota = sb("iota", [P, KEEP])
    m.wt2 = sb("wt2", [C, 2 * CI])
    m.wp2 = sb("wp2", [C, 2 * CI])
    m.wg = sb("wg", [C, CI])
    m.wo = sb("wo", [CI, C])
    m.bias = sb("bias", [P, 4])
    m.wa = sb("wa", [C, A_N])
    m.qnw = sb("qnw", [P, QR])
    m.kvnw = sb("kvnw", [P, KVR])
    m.xnT = sb("xnT", [C, T])
    m.cqT = sb("cqT", [P, T])
    m.k1a = sb("k1a", [P, T], F32R)
    m.k1b = sb("k1b", [P, T], F32R)
    m.v1 = sb("v1", [P, NT, KVR])
    m.selT = sb("selT", [C, KEEP])
    m.t2 = sb("t2", [C, T])
    m.gates = sb("gates", [P, 3])
    m.small = sb("small", [P, 512])
    m.wq_g = sb("wq_g", [P, 2, 2 * NW + 2 * RW])
    m.wk_g = sb("wk_g", [C, 2, 2 * NW + 2 * RW])
    m.ws_g = sb("ws_g", [C, 2, 2 * NW + 2 * RW])
    m.wproj_g = sb("wproj_g", [P, C])
    m.wvp_g = sb("wvp_g", [P, C])
    m.vw = sb("vw", [P, 2, NT, NW])
    m.vs = sb("vs", [P, 2, KEEP // P, NW])
    m.q1a = sb("q1a", [P, HG, T], F32R)
    m.q1b = sb("q1b", [P, HG, T], F32R)
    m.qa = sb("qa", [P, HG, T], F32R)
    m.qb = sb("qb", [P, HG, T], F32R)
    m.kwa = sb("kwa", [P, HG, T], F32R)
    m.kwb = sb("kwb", [P, HG, T], F32R)
    m.ksa = sb("ksa", [P, HG, KEEP], F32R)
    m.ksb = sb("ksb", [P, HG, KEEP], F32R)
    raw_n = 2 * NW + 2 * RW
    sizes = dict(products=3 * T, sums=3 * T, prob=PROBS * HP * CH, tok=NT * HP * 2 * HD, rawq=NT * raw_n,
                 rawk=NT * (NW + 2 * RW), raws=KEEP // P * (NW + 2 * RW), rope=3 * NT * RW, mrow=P)
    arena = sb("arena", [P, sum(sizes.values())])
    at, part = 0, {}
    for name, n in sizes.items():
        part[name] = arena[:, at:at + n]
        at += n
    m.products = part["products"].rearrange("p (b n) -> p b n", b=3)
    m.sums = part["sums"].rearrange("p (b n) -> p b n", b=3)
    m.prob = part["prob"].rearrange("p (a h n) -> p a h n", a=PROBS, h=HP)
    m.tok = part["tok"].rearrange("p (t h n) -> p t h n", t=NT, h=HP)
    m.rawq = part["rawq"].rearrange("p (t n) -> p t n", t=NT)
    m.rawk = part["rawk"].rearrange("p (t n) -> p t n", t=NT)
    m.raws = part["raws"].rearrange("p (t n) -> p t n", t=KEEP // P)
    m.rope_tmp = [part["rope"][:, k * NT * RW:(k + 1) * NT * RW] for k in range(3)]
    m.mrow = part["mrow"][0:HP * NT]
    m.tokf = arena[:, 0:4 * T]
    m.rawqf = arena[:, 4 * T:7 * T]
    m.obuf = arena[:, 7 * T:10 * T]
    m.probf = arena[:, 10 * T:14 * T]
    m.rden = m.obuf[:, 2 * T:2 * T + CH]

    weights_and_constants(nc, m, d)
    with nc.Fori(0, B) as b:
        nonlocal_block(nc, m, b)
        latents(nc, m)
        selection(nc, m)
        turns(nc, m, PREPARE, NG - 1)
        with nc.Fori(0, NG - 1) as g:
            turns(nc, m, GROUP, g)
        turns(nc, m, LAST_GROUP, NG - 1)
        store_stream(nc, m, t2_dram, b)


def store_stream(nc, m, t2_dram, b):
    with ExitStack() as stack:
        s = open_sems(nc, stack, "stored")
        with nc.Block() as block:
            @block.sync
            def _(sp):
                sp.dma_start(t2_dram[b], m.t2[:]).then_inc(s["stored"], 16)
                sp.wait_ge(s["stored"], 16)
        phase_end(nc, s)


def weights_and_constants(nc, m, d):
    stack = ExitStack()
    s = open_sems(nc, stack, "s_load s_zero s_blk s_mm s_copy s_row s_one s_kept")
    sqn = m.tokf[:, 0:NG * QR].rearrange("p (g n) -> p g n", g=NG)
    kblk = m.tokf[:, 512:1024].rearrange("p (g n) -> p g n", g=NG)
    vblk = m.tokf[:, 1024:1536].rearrange("p (g n) -> p g n", g=NG)
    wpr = m.tokf[:, 1536:2048].rearrange("p (g n) -> p g n", g=NG)
    ones_row = m.probf[0:1, 0:HG * T]
    wqp = m.rawqf[0:QR, 0:NG * P].rearrange("p (g s n) -> p g s n", g=NG, s=2)
    wvp = m.rawqf[:, NG * P:2 * NG * P].rearrange("p (g n) -> p g n", g=NG)
    with nc.Block() as block:
        consts = [(m.ident, "ident"), (m.ident_bf, "ident_bf"), (m.causal_q, "causal_q"), (m.causal_k, "causal_k"),
                  (m.window_q0, "window_q0"), (m.window_q, "window_q"), (m.window_k, "window_k"), (m.cos, "cos"),
                  (m.sin, "sin"), (m.before, "before"), (m.below, "below"), (m.iota, "iota"), (m.wt2, "wt2"),
                  (m.wp2, "wp2"), (m.wg, "wg"), (m.wo, "wo"), (m.bias, "bias"), (m.wa, "wa"), (m.qnw, "qnw"),
                  (m.kvnw, "kvnw"), (sqn, "wqn_t"), (wpr, "wproj")]

        @block.sync
        def _(sp):
            for dst, name in consts:
                sp.dma_start(dst[:] if not isinstance(dst, bass.AP) else dst, d[name]).then_inc(s["s_load"], 16)
            sp.wait_ge(s["s_zero"], 1)
            for g in range(NG):
                for h in range(HG):
                    r = slice(32 * h, 32 * h + 32)
                    sp.dma_start(kblk[r, g, r], d["wk_t"][g, h]).then_inc(s["s_blk"], 16)
                    sp.dma_start(vblk[r, g, r], d["wv_t"][g, h]).then_inc(s["s_blk"], 16)
            sp.wait_ge(s["s_one"], 9)
            sp.dma_start(m.k1b[64:65, :].bitcast(F32), ones_row[:, 0:T]).then_inc(s["s_row"], 16)
            sp.dma_start(m.kwb[65:66].rearrange("p h n -> p (h n)").bitcast(F32), ones_row).then_inc(s["s_row"], 16)
            sp.dma_start(m.ksb[64:65].rearrange("p h n -> p (h n)").bitcast(F32),
                         ones_row[:, 0:HG * KEEP]).then_inc(s["s_row"], 16)
            sp.wait_ge(s["s_row"], 48)
            sp.wait_ge(s["s_copy"], 2)
            sp.dma_start(d["wvp"].rearrange("g p c -> p g c"), wvp).then_inc(s["s_kept"], 16)
            for turn in range(2 * NG):
                g, side = divmod((turn + 1) % (2 * NG), 2)
                sp.dma_start(d["wqp"][turn // 2][:, (turn % 2) * NW:(turn % 2 + 1) * NW], wqp[:, g, side])\
                    .then_inc(s["s_kept"], 16)
            sp.wait_ge(s["s_kept"], 16 * (1 + 2 * NG))

        @block.vector
        def _(dve):
            dve.memset(m.tokf[:, 512:1536], 0.0).then_inc(s["s_zero"], 1)
            dve.memset(m.ones[:], 1.0).then_inc(s["s_one"], 1)
            dve.memset(ones_row, 1.0).then_inc(s["s_one"], 1)
            dve.memset(m.eps[:, 0:1], LNE).then_inc(s["s_one"], 1)
            dve.memset(m.eps[:, 1:2], RMSE).then_inc(s["s_one"], 1)
            for x in (m.k1b, m.kwb, m.ksb, m.q1b, m.qb):
                dve.memset(x[HD:P].bitcast(F32), 0.0).then_inc(s["s_one"], 1)
            dve.memset(m.small[:], -3.0e38)
            dve.memset(m.cqT[:], 0.0)
            dve.memset(m.wq_g[:], 0.0)
            dve.wait_ge(s["s_mm"], 1)
            dve.tensor_copy(wqp, m.ps[0:QR, 0, :].rearrange("p (g s n) -> p g s n", g=NG, s=2)).then_inc(s["s_copy"], 1)
            dve.tensor_copy(wvp, m.ps[:, 1, :].rearrange("p (g n) -> p g n", g=NG)).then_inc(s["s_copy"], 1)

        @block.tensor
        def _(pe):
            pe.wait_ge(s["s_load"], 16 * len(consts))
            pe.wait_ge(s["s_blk"], 16 * 2 * NH)
            for g in range(NG):
                pe.matmul(m.ps[0:QR, 0, g * P:(g + 1) * P], sqn[:, g, :], kblk[:, g, :], start=True, stop=True)
                mm = pe.matmul(m.ps[:, 1, g * P:(g + 1) * P], vblk[:, g, :], wpr[:, g, :], start=True, stop=True)
            mm.then_inc(s["s_mm"], 1)
    phase_end(nc, s)
    stack.close()


def nonlocal_block(nc, m, b):
    ps, d = m.ps, m.d
    x = m.tokf[:, 0:T]
    va = m.tokf[:, T:2 * T].rearrange("p (t n) -> p t n", t=NT)
    y = m.tokf[0:CI, 2 * T:3 * T]
    th_a, ph_a = m.q1a[:, 0, :], m.kwa[:, 0, :]
    th_b, ph_b = m.q1b[:, 0, :], m.k1b[:]
    negm = m.small[:, 0:NT]
    mrow = m.mrow[0:NT, :]
    rden = m.rden
    stack = ExitStack()
    s = open_sems(nc, stack, "n_x n_proj n_hi n_lo n_va n_vac n_app n_max n_mt n_mrow n_mdma n_qb "
                           "n_s n_exp n_pv n_chain n_y n_o n_t2")

    with nc.Block() as block:
        @block.sync
        def _(sp):
            sp.dma_start(x, d["x"][b]).then_inc(s["n_x"], 16)
            sp.wait_ge(s["n_mrow"], 1)
            sp.dma_start(th_b[64:65, :].bitcast(F32), mrow).then_inc(s["n_mdma"], 16)
            sp.wait_ge(s["n_hi"], 4)
            sp.dma_start(th_b[0:64, :].bitcast(F32), th_a[0:64, :].bitcast(F32)).then_inc(s["n_mdma"], 16)

        @block.tensor
        def _(pe):
            pe.wait_ge(s["n_x"], 16)
            for c in range(NC):
                xc = x[:, c * CH:(c + 1) * CH]
                pe.matmul(ps[:, c, :], m.wt2[:], xc, start=True, stop=True).then_inc(s["n_proj"], 1)
                pe.matmul(ps[:, 2 + c, :], m.wp2[:], xc, start=True, stop=True).then_inc(s["n_proj"], 1)
            for t in range(NT):
                mm = pe.matmul(ps[:, 4, t * CI:(t + 1) * CI], x[:, t * P:(t + 1) * P], m.wg[:],
                               start=True, stop=True)
            mm.then_inc(s["n_va"], 1)
            pe.wait_ge(s["n_hi"], 4)
            pe.wait_ge(s["n_lo"], 4)
            pe.wait_ge(s["n_vac"], 1)
            for t in range(NT):
                if t >= 2:
                    pe.wait_ge(s["n_max"], t - 1)
                for c in range(NC):
                    mm = pe.matmul(ps[:, 2 * (t % 2) + c, :], th_a[:, t * P:(t + 1) * P],
                                   ph_a[:, c * CH:(c + 1) * CH], start=True, stop=True)
                mm.then_inc(s["n_app"], 1)
            pe.wait_ge(s["n_max"], NT)
            pe.transpose(ps[0:NT, 4, 0:P], negm, m.ident[:]).then_inc(s["n_mt"], 1)
            pe.wait_ge(s["n_mdma"], 32)

            def scores(u):
                c, j = divmod(u, NT)
                if u >= 4:
                    pe.wait_ge(s["n_exp"], u - 3)
                pe.matmul(ps[:, u % 4, :], ph_a[:, j * P:(j + 1) * P], th_a[:, c * CH:(c + 1) * CH],
                          start=True, stop=False)
                pe.matmul(ps[:, u % 4, :], ph_b[:, j * P:(j + 1) * P], th_b[:, c * CH:(c + 1) * CH],
                          start=False, stop=True).then_inc(s["n_s"], 1)

            def values(u):
                c, j = divmod(u, NT)
                pe.wait_ge(s["n_exp"], u + 1)
                pe.matmul(ps[:, 5 + c, :], va[:, j, :], m.probf[:, (u % 4) * CH:(u % 4 + 1) * CH],
                          start=(j == 0), stop=(j == NT - 1)).then_inc(s["n_pv"], 1)

            scores(0)
            scores(1)
            for u in range(NC * NT):
                if u + 2 < NC * NT:
                    scores(u + 2)
                values(u)
            for c in range(NC):
                pe.wait_ge(s["n_y"], c + 1)
                pe.matmul(ps[:, c, :], m.wo[:], y[:, c * CH:(c + 1) * CH], start=True, stop=True)\
                    .then_inc(s["n_o"], 1)

        @block.scalar
        def _(act):
            for c in range(NC):
                cc = slice(c * CH, (c + 1) * CH)
                act.wait_ge(s["n_proj"], 2 * c + 1)
                act.activation(th_a[:, cc], ps[:, c, :], ACT.Identity, bias=m.bias[:, 0:1]).then_inc(s["n_hi"], 1)
                act.wait_ge(s["n_proj"], 2 * c + 2)
                act.activation(ph_a[:, cc], ps[:, 2 + c, :], ACT.Identity, bias=m.bias[:, 1:2])\
                    .then_inc(s["n_hi"], 1)
            for u in range(NC * NT):
                act.wait_ge(s["n_s"], u + 1)
                if u >= 4:
                    act.wait_ge(s["n_pv"], u - 3)
                act.activation(m.probf[:, (u % 4) * CH:(u % 4 + 1) * CH], ps[:, u % 4, :], ACT.Exp)\
                    .then_inc(s["n_exp"], 1)

        @block.vector
        def _(dve):
            dve.memset(va[:, :, CI:2 * CI], 1.0).then_inc(s["n_vac"], 1)
            for c in range(NC):
                cc = slice(c * CH, (c + 1) * CH)
                dve.wait_ge(s["n_hi"], 2 * c + 1)
                dve.scalar_tensor_tensor(out=th_a[64:128, cc], in0=ps[64:128, c, :], scalar=m.bias[64:128, 0:1],
                                         in1=th_a[64:128, cc].bitcast(F32), op0=ALU.add, op1=ALU.subtract)\
                    .then_inc(s["n_lo"], 1)
                dve.wait_ge(s["n_hi"], 2 * c + 2)
                dve.scalar_tensor_tensor(out=ph_b[0:64, cc], in0=ps[0:64, 2 + c, :], scalar=m.bias[0:64, 1:2],
                                         in1=ph_a[0:64, cc].bitcast(F32), op0=ALU.add, op1=ALU.subtract)\
                    .then_inc(s["n_lo"], 1)
            dve.wait_ge(s["n_va"], 1)
            dve.tensor_copy(va[:, :, 0:CI], ps[:, 4, :].rearrange("p (t n) -> p t n", t=NT)).then_inc(s["n_vac"], 1)
            for t in range(NT):
                dve.wait_ge(s["n_app"], t + 1)
                k = 2 * (t % 2)
                dve.tensor_reduce(negm[:, t:t + 1], ps[:, k:k + 2, :].rearrange("p a n -> p (a n)"), AX, ALU.max,
                                  negate=True).then_inc(s["n_max"], 1)
            dve.wait_ge(s["n_mt"], 1)
            dve.tensor_copy(mrow.bitcast(F32R), ps[0:NT, 4, 0:P]).then_inc(s["n_mrow"], 1)
            for c in range(NC):
                cc = slice(c * CH, (c + 1) * CH)
                dve.wait_ge(s["n_pv"], NT * (c + 1))
                dve.reciprocal(rden[0:CI, :], ps[CI:2 * CI, 5 + c, :]).then_inc(s["n_chain"], 1)
                dve.wait_ge(s["n_chain"], 2 * c + 1)
                dve.tensor_tensor(y[:, cc], ps[0:CI, 5 + c, :], rden[0:CI, :], ALU.mult).then_inc(s["n_chain"], 1)
                dve.wait_ge(s["n_chain"], 2 * c + 2)
                dve.tensor_scalar(y[:, cc], y[:, cc], m.bias[0:CI, 2:3], None, ALU.add).then_inc(s["n_y"], 1)
            for c in range(NC):
                cc = slice(c * CH, (c + 1) * CH)
                dve.wait_ge(s["n_o"], c + 1)
                dve.scalar_tensor_tensor(out=m.t2[:, cc], in0=ps[:, c, :], scalar=m.bias[:, 3:4], in1=x[:, cc],
                                         op0=ALU.add, op1=ALU.add).then_inc(s["n_t2"], 1)
    phase_end(nc, s)
    stack.close()


def in_order(engine, sem):
    done = [0]

    def run(ins):
        done[0] += 1
        ins.then_inc(sem, 1)
        engine.wait_ge(sem, done[0])
    return run


def each_tile(col, n):
    return col.unsqueeze(2).to_broadcast([P, col.shape[1], n])


def each_token(row, n):
    return row.unsqueeze(1).to_broadcast([P, n, row.shape[1]])


def latents(nc, m):
    ps = m.ps
    t_tok = m.rawqf[:, 0:T]
    xn = m.rawqf[:, T:2 * T]
    pa = m.rawqf[:, 2 * T:2 * T + NT * A_N].rearrange("p (t n) -> p t n", t=NT)
    sm = m.small
    mv = sm[:, 16:32].rearrange("p (t n) -> p t n", t=NT)
    std, rstd = sm[:, 32:40], sm[:, 40:48]
    st = sm[:, 48:96].rearrange("p (t n) -> p t n", t=NT)
    ssq, rms, rrms = sm[:, 96:112], sm[:, 112:128], sm[:, 128:144]
    gsum, gexp, gnm, gtot = sm[:, 144:147], sm[:, 148:151], sm[:, 152:153], sm[:, 153:154]
    grec = sm[:, 154:155]
    with ExitStack() as stack:
        s = open_sems(nc, stack, "t2_turned t_copied chain std_done xn_done xn_turned xnT_done pa_done pa_copied")
        with nc.Block() as block:
            @block.tensor
            def _(pe):
                for t in range(NT):
                    mm = pe.transpose(ps[:, t // 4, (t % 4) * P:(t % 4 + 1) * P], m.t2[:, t * P:(t + 1) * P],
                                      m.ident[:])
                    if t % 4 == 3:
                        mm.then_inc(s["t2_turned"], 1)
                for t in range(NT):
                    pe.wait_ge(s["xn_done"], t + 1)
                    mm = pe.transpose(ps[:, 2 + t // 4, (t % 4) * P:(t % 4 + 1) * P], xn[:, t * P:(t + 1) * P],
                                      m.ident[:])
                    if t % 4 == 3:
                        mm.then_inc(s["xn_turned"], 1)
                for t in range(NT):
                    pe.wait_ge(s["xnT_done"], t // 4 + 1)
                    mm = pe.matmul(ps[:, 4 + t // 4, (t % 4) * A_N:(t % 4 + 1) * A_N],
                                   m.xnT[:, t * P:(t + 1) * P], m.wa[:], start=True, stop=True)
                    if t % 4 == 3:
                        mm.then_inc(s["pa_done"], 1)

            @block.scalar
            def _(act):
                for k in range(2):
                    act.wait_ge(s["t2_turned"], k + 1)
                    act.copy(t_tok[:, k * CH:(k + 1) * CH], ps[:, k, :]).then_inc(s["t_copied"], 1)
                act.wait_ge(s["chain"], 1)
                act.activation(std, mv[:, :, 1], ACT.Sqrt, bias=m.eps[:, 0:1]).then_inc(s["std_done"], 1)
                for k in range(2):
                    act.wait_ge(s["xn_turned"], k + 1)
                    act.copy(m.xnT[:, k * CH:(k + 1) * CH], ps[:, 2 + k, :]).then_inc(s["xnT_done"], 1)

            @block.vector
            def _(dve):
                for t in range(NT):
                    dve.wait_ge(s["t_copied"], t // 4 + 1)
                    ins = dve.bn_stats(st[:, t, :], t_tok[:, t * P:(t + 1) * P])
                    ins.then_inc(s["pa_copied"], 1)
                dve.wait_ge(s["pa_copied"], NT)
                for t in range(NT):
                    ins = dve.bn_aggr(mv[:, t, :], st[:, t, :])
                ins.then_inc(s["chain"], 1)
                dve.wait_ge(s["std_done"], 1)
                dve.wait_ge(s["chain"], 1)
                dve.reciprocal(rstd, std).then_inc(s["chain"], 1)
                dve.wait_ge(s["chain"], 2)
                for t in range(NT):
                    dve.tensor_scalar(xn[:, t * P:(t + 1) * P], t_tok[:, t * P:(t + 1) * P], mv[:, t, 0:1],
                                      rstd[:, t:t + 1], ALU.subtract, ALU.mult).then_inc(s["xn_done"], 1)
                for k in range(2):
                    dve.wait_ge(s["pa_done"], k + 1)
                    dve.tensor_copy(pa[:, 4 * k:4 * k + 4, :],
                                    ps[:, 4 + k, 0:4 * A_N].rearrange("p (t n) -> p t n", t=4))
        phase_end(nc, s)

    cq, ckv = pa[:, :, A_CQ:A_KV], pa[:, :, A_KV:A_KR]
    kr = pa[:, :, A_KR:A_IMP]
    k1tok = m.obuf[:, 0:T].rearrange("p (t n) -> p t n", t=NT)
    cqn = m.obuf[:, T:T + NT * QR].rearrange("p (t n) -> p t n", t=NT)
    tmp = m.obuf[:, 2 * T:2 * T + NT * QR].rearrange("p (t n) -> p t n", t=NT)
    ro = m.tokf[:, 0:6 * P].rearrange("p (k t n) -> p k t n", k=6, t=NT)
    with ExitStack() as stack:
        s = open_sems(nc, stack, "gate_sum gate_diff gate_exp ssq_done rms_done chain cqn_done k1_done "
                                 "cq_turned k1_turned copied")
        with nc.Block() as block:
            @block.tensor
            def _(pe):
                for t in range(NT):
                    mm = pe.matmul(ps[:, 6, 0:3], m.ones[:], pa[:, t, A_GATE:A_N], start=(t == 0), stop=(t == NT - 1))
                mm.then_inc(s["gate_sum"], 1)
                pe.wait_ge(s["cqn_done"], 1)
                for t in range(NT):
                    mm = pe.transpose(ps[0:QR, t // 4, (t % 4) * P:(t % 4 + 1) * P], cqn[:, t, :], m.ident[:])
                mm.then_inc(s["cq_turned"], 1)
                pe.wait_ge(s["k1_done"], 1)
                for t in range(NT):
                    mm = pe.transpose(ps[:, 2 + t // 4, (t % 4) * P:(t % 4 + 1) * P], k1tok[:, t, :], m.ident[:])
                mm.then_inc(s["k1_turned"], 1)

            @block.scalar
            def _(act):
                act.wait_ge(s["ssq_done"], 2)
                act.activation(rms[:, 0:NT], ssq[:, 0:NT], ACT.Sqrt, bias=m.eps[:, 1:2], scale=1.0 / QR)\
                    .then_inc(s["rms_done"], 1)
                act.activation(rms[:, NT:2 * NT], ssq[:, NT:2 * NT], ACT.Sqrt, bias=m.eps[:, 1:2],
                               scale=1.0 / KVR).then_inc(s["rms_done"], 1)
                act.wait_ge(s["gate_diff"], 1)
                act.activation(gexp, gsum, ACT.Exp, scale=1.0 / T).then_inc(s["gate_exp"], 1)
                act.wait_ge(s["cq_turned"], 1)
                for k in range(2):
                    act.copy(m.cqT[0:QR, k * CH:(k + 1) * CH], ps[0:QR, k, :])
                act.wait_ge(s["k1_turned"], 1)
                for k in range(2):
                    kk = slice(k * CH, (k + 1) * CH)
                    act.copy(m.k1a[0:HD, kk], ps[0:HD, 2 + k, :])
                    act.copy(m.k1a[HD:P, kk], ps[0:HD, 2 + k, :])
                    act.copy(m.k1b[0:HD, kk], ps[HD:P, 2 + k, :])

            @block.vector
            def _(dve):
                run = in_order(dve, s["chain"])
                run(dve.tensor_tensor(tmp, cq, cq, ALU.mult))
                dve.tensor_reduce(ssq[:, 0:NT], tmp, AX, ALU.add).then_inc(s["ssq_done"], 1)
                dve.wait_ge(s["ssq_done"], 1)
                run(dve.tensor_tensor(tmp[:, :, 0:KVR], ckv, ckv, ALU.mult))
                dve.tensor_reduce(ssq[:, NT:2 * NT], tmp[:, :, 0:KVR], AX, ALU.add).then_inc(s["ssq_done"], 1)
                dve.wait_ge(s["gate_sum"], 1)
                run(dve.tensor_reduce(gnm, ps[:, 6, 0:3], AX, ALU.max, negate=True))
                dve.tensor_scalar(gsum, ps[:, 6, 0:3], gnm, None, ALU.add).then_inc(s["gate_diff"], 1)
                dve.wait_ge(s["rms_done"], 2)
                run(dve.reciprocal(rrms, rms))
                run(dve.tensor_tensor(cqn, cq, each_tile(rrms[:, 0:NT], QR), ALU.mult))
                dve.tensor_tensor(cqn, cqn, each_token(m.qnw[:], NT), ALU.mult).then_inc(s["cqn_done"], 1)
                run(dve.tensor_tensor(m.v1[:], ckv, each_tile(rrms[:, NT:2 * NT], KVR), ALU.mult))
                run(dve.tensor_tensor(m.v1[:], m.v1[:], each_token(m.kvnw[:], NT), ALU.mult))
                run(dve.tensor_scalar(kr, kr, 1.0 / NH, None, ALU.mult))
                xr, xi = kr[:, :, 0:HALF], kr[:, :, HALF:2 * HALF]
                dve.tensor_tensor(ro[:, 0], xr, m.cos[:], ALU.mult)
                dve.tensor_tensor(ro[:, 1], xi, m.sin[:], ALU.mult)
                dve.tensor_tensor(ro[:, 2], xr, m.sin[:], ALU.mult)
                run(dve.tensor_tensor(ro[:, 3], xi, m.cos[:], ALU.mult))
                dve.tensor_tensor(ro[:, 4], ro[:, 0], ro[:, 1], ALU.subtract)
                run(dve.tensor_tensor(ro[:, 5], ro[:, 2], ro[:, 3], ALU.add))
                for at, n, src in ((0, KVR, m.v1[:]), (NOPE, HALF, ro[:, 4]), (NOPE + HALF, HALF, ro[:, 5])):
                    hi = k1tok[:, :, at:at + n]
                    run(dve.tensor_copy(hi.bitcast(F32R), src))
                    run(dve.tensor_tensor(k1tok[:, :, HD + at:HD + at + n].bitcast(F32R), src, hi, ALU.subtract))
                dve.tensor_copy(gtot, gnm).then_inc(s["k1_done"], 1)
                dve.wait_ge(s["gate_exp"], 1)
                dve.wait_ge(s["k1_done"], 1)
                run(dve.tensor_reduce(gtot, gexp, AX, ALU.add))
                run(dve.reciprocal(grec, gtot))
                run(dve.tensor_scalar(m.gates[:], gexp, grec, None, ALU.mult))
        phase_end(nc, s)


def selection(nc, m):
    ps = m.ps
    xn = m.rawqf[:, T:2 * T]
    pa = m.rawqf[:, 2 * T:2 * T + NT * A_N].rearrange("p (t n) -> p t n", t=NT)
    imp = pa[:, :, A_IMP]
    onehot = m.tokf[:, 0:NT * KEEP].rearrange("p (t n) -> p t n", t=NT)
    score = m.tokf[:, 2048:2048 + T]
    spread = m.tokf[:, 3072:3072 + T].rearrange("p (t n) -> p t n", t=NT)
    junk = m.obuf[:, 0:T]
    sm = m.small
    cnt = sm[:, 160:192].rearrange("p (t n) -> p t n", t=NT)
    rank, kept, far, pos = sm[:, 192:200], sm[:, 200:208], sm[:, 208:216], sm[:, 216:224]
    with ExitStack() as stack:
        s = open_sems(nc, stack, "spread_done turned score_done chain kept_done pos_summed onehot_done gathered")
        with nc.Block() as block:
            @block.tensor
            def _(pe):
                pe.wait_ge(s["spread_done"], 1)
                for t in range(NT):
                    mm = pe.transpose(ps[:, t // 4, (t % 4) * P:(t % 4 + 1) * P], spread[:, t, :], m.ident[:])
                mm.then_inc(s["turned"], 1)
                pe.wait_ge(s["kept_done"], 1)
                mm = pe.matmul(ps[:, 2, 0:NT], m.before[:], kept, start=True, stop=True)
                for t in range(NT - 1):
                    mm = pe.matmul(ps[:, 2, t + 1:NT], m.ones[:], kept[:, t:t + 1].to_broadcast([P, NT - 1 - t]),
                                   start=False, stop=True, skip_group_check=True)
                mm.then_inc(s["pos_summed"], 1)
                pe.wait_ge(s["onehot_done"], NT)
                for t in range(NT):
                    mm = pe.matmul(ps[:, 3, 0:KEEP], xn[:, t * P:(t + 1) * P], onehot[:, t, :],
                                   start=(t == 0), stop=(t == NT - 1))
                mm.then_inc(s["gathered"], 1)

            @block.scalar
            def _(act):
                act.wait_ge(s["turned"], 1)
                for k in range(2):
                    act.copy(score[:, k * CH:(k + 1) * CH], ps[:, k, :]).then_inc(s["score_done"], 1)
                act.wait_ge(s["gathered"], 1)
                act.copy(m.selT[:], ps[:, 3, 0:KEEP])

            @block.vector
            def _(dve):
                run = in_order(dve, s["chain"])
                dve.tensor_copy(spread, imp.unsqueeze(2).to_broadcast([P, NT, P])).then_inc(s["spread_done"], 1)
                run(dve.memset(cnt, 0.0))
                dve.wait_ge(s["score_done"], 2)
                for t in range(NT):
                    own = imp[:, t:t + 1]
                    lo, hi = t * P, (t + 1) * P
                    if t > 0:
                        run(dve.tensor_scalar(junk[:, 0:lo], score[:, 0:lo], own, None, ALU.is_ge, ALU.add,
                                              accum_out=cnt[:, t, 0:1]))
                    if t < NT - 1:
                        run(dve.tensor_scalar(junk[:, hi:T], score[:, hi:T], own, None, ALU.is_gt, ALU.add,
                                              accum_out=cnt[:, t, 1:2]))
                    run(dve.tensor_scalar(junk[:, lo:hi], score[:, lo:hi], own, None, ALU.is_gt, ALU.add,
                                          accum_out=cnt[:, t, 2:3]))
                    run(dve.scalar_tensor_tensor(out=junk[:, lo:hi], in0=score[:, lo:hi], scalar=own,
                                                 in1=m.below[:], op0=ALU.is_equal, op1=ALU.mult,
                                                 accum_out=cnt[:, t, 3:4]))
                run(dve.tensor_reduce(rank, cnt, AX, ALU.add))
                dve.tensor_scalar(kept, rank, float(KEEP), None, ALU.is_lt).then_inc(s["kept_done"], 1)
                dve.wait_ge(s["kept_done"], 1)
                run(dve.tensor_scalar(far, kept, -4.0 * T, 4.0 * T, ALU.mult, ALU.add))
                dve.wait_ge(s["pos_summed"], 1)
                run(dve.tensor_tensor(pos, ps[:, 2, 0:NT], far, ALU.add))
                for t in range(NT):
                    dve.tensor_scalar(onehot[:, t, :], m.iota[:], pos[:, t:t + 1], None, ALU.is_equal)\
                        .then_inc(s["onehot_done"], 1)
        phase_end(nc, s)


def units():
    found = []
    for br, c in SUMS:
        for j in range(KEEP // P if br == 1 else NT):
            q0, q1 = c * CH, (c + 1) * CH
            if br != 1:
                q0 = max(q0, j * P)
            if br == 2:
                q1 = min(q1, j * P + WN)
            if q0 < q1:
                found.append((br, c, j, q0, q1 - q0))
    return found


SUMS = [(0, 0), (1, 0), (2, 0), (1, 1), (2, 1), (0, 1)]
UNITS = units()
LAST = [max(u for u, x in enumerate(UNITS) if x[:2] == k) for k in SUMS]


def interleave(exact, prepare, keep, delay):
    spread = prepare[:len(prepare) - keep]
    total = sum(UNITS[x[2]][4] for x in exact if x[0] in ("scores", "products")
                and x[2] >= delay)
    todo, seen, at = [], 0, 0
    for x in exact:
        todo.append(x)
        if x[0] in ("scores", "products"):
            if x[2] < delay:
                continue
            seen += UNITS[x[2]][4]
            n = len(spread) * seen // total
            todo += spread[at:n]
            at = n
    return todo + spread[at:] + prepare[len(prepare) - keep:]


def preparation(side):
    turn = {name: [("turn_" + name, side, h, k) for h in range(HP) for k in range(2)] for name in ("q1", "q", "k")}
    max0 = [("max0", side, h, i, part) for h in range(HP) for i in range(NT) for part in range(1 + (i >= NT // 2))]
    max1, max2 = [[(kind, side, h, k) for h in range(HP) for k in range(NT // 2)] for kind in ("max1", "max2")]
    todo = [("q", side, t) for t in range(NT)] + [("rotate", side, "q")]
    todo += [("k", side, t) for t in range(NT // 2)] + [("split", side, "q1")]
    todo += [("k", side, t) for t in range(NT // 2, NT)] + [("rotate", side, "k")]
    todo += [("s", side, t) for t in range(KEEP // P)] + [("rotate", side, "s")]
    todo += turn["q1"]
    todo += max0[:2] + [("split", side, "q")] + max0[2:8] + weave(max0[8:12], turn["q"]) + [("split", side, "k")]
    todo += max0[12:17] + weave(max0[17:21], turn["k"]) + [("split", side, "s")] + max0[21:] + [("whole", side, 0)]
    todo += max2[:4] + [("turn_s", side, 0), ("rows", side, 0)] + max2[4:] + max1
    todo += [("rows", side, 1), ("rows", side, 2)]
    return todo


def weave(a, b):
    return [x for pair in zip(a, b) for x in pair]


def exact_pass(side):
    todo, pieces = [], []
    for u in range(len(UNITS) + 1):
        if u < len(UNITS):
            todo.append(("scores", side, u))
        if u > 0:
            todo.append(("products", side, u - 1))
            if u - 1 in LAST:
                k = LAST.index(u - 1)
                todo.append(("sum", side, k))
                if side == 1:
                    pieces += [("divide", side, k, piece) for piece in range(PIECES)]
            todo += pieces[:1]
            pieces = pieces[1:]
    return todo + pieces


SPARE = 6
PIECES = 2
PROBS = 3
BY_ACT = ("q", "k", "s", "turn_q1", "turn_q", "turn_k", "turn_s")
BEFORE = {"q1": "turn_s", "q": "turn_q1", "k": "turn_q", "s": "turn_k"}


class Plan:

    def __init__(self, steps, spares):
        self.steps = steps
        self.spares = spares
        self.fills = self.of(BY_ACT + ("max0", "max1", "max2", "rows", "proj"))

    def of(self, kinds):
        return [x for x in self.steps if x[0] in kinds]

    def has(self, kind, side):
        return any(x[0] == kind and x[1] == side for x in self.steps)

    def emptied(self, n, act):
        return sum((x[0] in BY_ACT) == act for x in self.fills[:n])

    def up_to(self, kind, side):
        return max(n for n, x in enumerate(self.fills) if x[0] == kind and x[1] == side) + 1

    def by_act(self, kind, side):
        return self.emptied(self.up_to(kind, side), True)

    def by_dve(self, kind, side):
        return self.emptied(self.up_to(kind, side), False)

    def count(self, *step):
        return self.of((step[0],)).index(step) + 1


def second_turn():
    return [("proj", 1, c) for c in range(NC)]


PREPARE = Plan(preparation(0), 8)
GROUP = Plan(interleave(exact_pass(0), preparation(1), 0, 2) + interleave(exact_pass(1), preparation(0), 12, 0)
             + second_turn(), 2)
LAST_GROUP = Plan(interleave(exact_pass(0), preparation(1), 0, 2) + exact_pass(1) + second_turn(), 2)


def turns(nc, m, plan, g):
    ps, d = m.ps, m.d
    raw = {"q": m.rawq, "q1": m.rawq, "k": m.rawk, "s": m.raws}
    sides = [x for x in (1, 0) if plan.has("q", x)]
    stack = ExitStack()
    s = open_sems(nc, stack, "q_loaded k_loaded s_loaded proj_loaded fill_ready emptied_act emptied_dve rotation hi_done split_done "
                             "q_rows1 q_rows k_twice s_twice max_rows scores_ready exp_done products_done "
                             "banks_free inverse_done divided o_done max_done")
    neg = m.small
    negs = [neg[:, 256 + k * HP * NT:256 + (k + 1) * HP * NT] for k in range(3)]
    partial = neg[:, 352:352 + HP * NT * 2].rearrange("p (h t a) -> p h t a", h=HP, t=NT)

    def heads(side, h=None):
        return slice(HP * side, HP * side + HP) if h is None else HP * side + h

    def spare(n):
        return ps[:, (SPARE + n % 2) if plan.spares == 2 else n % 8, :]

    def weights(w, side):
        return w[:, 1 - side, :]

    with nc.Block() as block:
        @block.sync
        def _(sp):
            sp.dma_start(m.wq_g[0:QR, :, 0:NW + 2 * RW], d["wq"][g]).then_inc(s["q_loaded"], 16)
            sp.dma_start(m.wq_g[0:QR, :, NW + 2 * RW:], d["wqp"][g].rearrange("q (s n) -> q s n", s=2))\
                .then_inc(s["q_loaded"], 16)
            sp.dma_start(m.wk_g[:], d["wk"][g]).then_inc(s["k_loaded"], 16)
            sp.dma_start(m.ws_g[:], d["ws"][g]).then_inc(s["s_loaded"], 16)
            sp.dma_start(m.wproj_g[:], d["wproj_g"][g]).then_inc(s["proj_loaded"], 16)
            sp.dma_start(m.wvp_g[:], d["wvp"][g]).then_inc(s["proj_loaded"], 16)
            if plan is PREPARE:
                sp.wait_ge(s["proj_loaded"], 32)
            for side in sides:
                hh = heads(side)
                sp.wait_ge(s["emptied_act"], plan.by_act("turn_q1", side))
                sp.dma_start(m.q1b[0:HD, hh].bitcast(F32), m.q1a[0:HD, hh].bitcast(F32)).then_inc(s["q_rows1"], 16)
                sp.wait_ge(s["emptied_act"], plan.by_act("turn_q", side))
                sp.dma_start(m.qb[0:HD, hh].bitcast(F32), m.qa[0:HD, hh].bitcast(F32)).then_inc(s["q_rows"], 16)
                sp.wait_ge(s["emptied_act"], plan.by_act("turn_k", side))
                sp.dma_start(m.kwa[HD:P, hh].bitcast(F32), m.kwa[0:HD, hh].bitcast(F32)).then_inc(s["k_twice"], 16)
                sp.wait_ge(s["emptied_dve"], plan.emptied(plan.fills.index(("rows", side, 0)) + 1, False))
                sp.dma_start(m.q1b[64:65, hh].rearrange("p h n -> p (h n)").bitcast(F32), m.mrow)\
                    .then_inc(s["max_rows"], 16)
                sp.wait_ge(s["emptied_act"], plan.by_act("turn_s", side))
                sp.dma_start(m.ksa[HD:P, hh].bitcast(F32), m.ksa[0:HD, hh].bitcast(F32)).then_inc(s["s_twice"], 16)
                for br in (1, 2):
                    sp.wait_ge(s["emptied_dve"], plan.emptied(plan.fills.index(("rows", side, br)) + 1, False))
                    sp.dma_start(m.qb[63 + br:64 + br, hh].rearrange("p h n -> p (h n)").bitcast(F32), m.mrow)\
                        .then_inc(s["max_rows"], 16)
            if sides:
                sp.wait_ge(s["max_rows"], 48 * len(sides))

        @block.tensor
        def _(pe):
            waited = set()

            def once(name, count):
                if (name, count) not in waited:
                    waited.add((name, count))
                    pe.wait_ge(s[name], count)

            def fill(n, kind, side, *a):
                if n >= plan.spares:
                    old = n - plan.spares
                    by_act = plan.fills[old][0] in BY_ACT
                    pe.wait_ge(s["emptied_act" if by_act else "emptied_dve"], plan.emptied(old + 1, by_act))
                bank = spare(n)
                nth = sides.index(side) + 1 if side in sides else 0
                if kind in ("q", "k", "s"):
                    once(kind + "_loaded", 32 if kind == "q" else 16)
                    x, w = {"q": (m.cqT, m.wq_g), "k": (m.xnT, m.wk_g), "s": (m.selT, m.ws_g)}[kind]
                    mm = pe.matmul(bank[:, 0:2 * NW + 2 * RW], x[:, a[0] * P:(a[0] + 1) * P], weights(w, side),
                                   start=True, stop=True)
                elif kind in ("turn_q1", "turn_q", "turn_k"):
                    h, k = a
                    once("split_done", plan.count("split", side, kind[5:]))
                    for i in range(4):
                        mm = pe.transpose(bank[:, i * P:(i + 1) * P], m.tok[:, 4 * k + i, h, :], m.ident[:])
                elif kind == "turn_s":
                    once("split_done", plan.count("split", side, "s"))
                    for i in range(4):
                        mm = pe.transpose(bank[:, i * P:(i + 1) * P], m.tok[:, i % 2, i // 2, :], m.ident[:])
                elif kind == "max0":
                    h, i, part = a
                    once("emptied_act", plan.by_act("turn_q1", side))
                    k0, k1 = part * CH, min((part + 1) * CH, (i + 1) * P)
                    mm = pe.matmul(bank[:, 0:k1 - k0], m.q1a[:, heads(side, h), i * P:(i + 1) * P],
                                   m.k1a[:, k0:k1], start=True, stop=True)
                    if k1 == (i + 1) * P:
                        mm = pe.matmul(bank[:, k1 - k0 - P:k1 - k0], m.ident_bf[:], m.causal_q[:],
                                       start=False, stop=True, skip_group_check=True)
                elif kind == "max1":
                    h, k = a
                    once("s_twice", 16 * nth)
                    for i in range(2):
                        t = 2 * k + i
                        mm = pe.matmul(bank[:, i * KEEP:(i + 1) * KEEP], m.qa[:, heads(side, h), t * P:(t + 1) * P],
                                       m.ksa[:, heads(side, h), :], start=True, stop=True)
                elif kind == "max2":
                    h, k = a
                    once("k_twice", 16 * nth)
                    once("emptied_act", plan.by_act("turn_q", side))
                    for i in range(2):
                        t = 2 * k + i
                        k0 = max(0, t * P - WINDOW)
                        pe.matmul(bank[:, i * KEEP:i * KEEP + WN], m.qa[:, heads(side, h), t * P:(t + 1) * P],
                                  m.kwa[:, heads(side, h), k0:k0 + WN], start=True, stop=True, skip_group_check=True)
                        mm = pe.matmul(bank[:, i * KEEP:i * KEEP + WN], m.ident_bf[:],
                                       m.window_q0[:] if t == 0 else m.window_q[:], start=False, stop=True,
                                       skip_group_check=True)
                elif kind == "rows":
                    if a[0] == 0:
                        pe.wait_ge(s["max_done"], nth)
                    else:
                        pe.wait_ge(s["emptied_dve"], plan.by_dve(("max1", "max2")[a[0] - 1], side))
                    mm = pe.transpose(bank[0:HP * NT, 0:P], negs[a[0]], m.ident[:])
                elif kind == "proj":
                    cc = slice(a[0] * CH, (a[0] + 1) * CH)
                    pe.wait_ge(s["divided"], SUMS.index((0, a[0])) + 1)
                    pe.wait_ge(s["o_done"], a[0] + 1)
                    once("proj_loaded", 32)
                    pe.matmul(bank, m.wvp_g[:], m.products[:, 0, cc], start=True, stop=False)
                    mm = pe.matmul(bank, m.wproj_g[:], m.products[:, 1, cc], start=False, stop=True)
                mm.then_inc(s["fill_ready"], 1)

            def scores(side, u):
                br, c, j, q0, w = UNITS[u]
                if side == 1:
                    if br == 0:
                        once("q_rows1", 16)
                        once("max_rows", 16)
                    else:
                        once("q_rows", 16)
                        once("max_rows", 48)
                qx, qy = (m.q1a, m.q1b) if br == 0 else (m.qa, m.qb)
                n = side * len(UNITS) + u
                if n >= 2:
                    pe.wait_ge(s["exp_done"], n - 1)
                jj = slice(j * P, (j + 1) * P)
                for h in range(HP):
                    hh = heads(side, h)
                    if br == 0:
                        kx, ky = m.k1a[:, jj], m.k1b[:, jj]
                    elif br == 1:
                        kx, ky = m.ksa[:, hh, jj], m.ksb[:, hh, jj]
                    else:
                        kx, ky = m.kwa[:, hh, jj], m.kwb[:, hh, jj]
                    bank = ps[:, 2 * (n % 2) + h, 0:w]
                    pe.matmul(bank, kx, qx[:, hh, q0:q0 + w], start=True, stop=False, skip_group_check=True)
                    at = q0 - j * P
                    if br == 0 and at == 0:
                        pe.matmul(bank[:, 0:P], m.ident_bf[:], m.causal_k[:], start=False, stop=False,
                                  skip_group_check=True)
                    if br == 2:
                        pe.matmul(bank, m.ident_bf[:], m.window_k[:, at:at + w], start=False, stop=False,
                                  skip_group_check=True)
                    mm = pe.matmul(bank, ky, qy[:, hh, q0:q0 + w], start=False, stop=True, skip_group_check=True)
                mm.then_inc(s["scores_ready"], 1)

            def products(side, u):
                br, c, j, q0, w = UNITS[u]
                n = side * len(UNITS) + u
                k = side * len(SUMS) + SUMS.index((br, c))
                first = u == 0 or u - 1 in LAST
                pe.wait_ge(s["exp_done"], n + 1)
                if first and k >= 2:
                    pe.wait_ge(s["banks_free"], k - 1)
                for plain in range(2):
                    for h in range(HP):
                        vv = slice(h * VD, (h + 1) * VD)
                        w_ = m.ones[:, 0:VD] if plain else m.v1[:, j, :] if br == 0 else \
                            m.vs[:, side, j, vv] if br == 1 else m.vw[:, side, j, vv]
                        at = (plain * HP + h) * VD
                        mm = pe.matmul(ps[at:at + VD, 4 + k % 2, q0 - c * CH:q0 - c * CH + w], w_,
                                       m.prob[:, n % PROBS, h, 0:w], start=first, stop=True, skip_group_check=True)
                mm.then_inc(s["products_done"], 1)

            n = 0
            for step in plan.steps:
                if step[0] == "scores":
                    scores(*step[1:])
                elif step[0] == "products":
                    products(*step[1:])
                elif step in plan.fills:
                    fill(n, *step)
                    n += 1

        @block.scalar
        def _(act):
            n = 0
            for step in plan.steps:
                kind, side = step[:2]
                if kind == "scores":
                    w = UNITS[step[2]][4]
                    u = side * len(UNITS) + step[2]
                    act.wait_ge(s["scores_ready"], u + 1)
                    if u >= PROBS:
                        act.wait_ge(s["products_done"], u - PROBS + 1)
                    act.activation(m.prob[:, u % PROBS, :, 0:w], ps[:, 2 * (u % 2):2 * (u % 2) + 2, 0:w], ACT.Exp,
                                   scale=SCALE).then_inc(s["exp_done"], 1)
                if kind == "sum":
                    br, c = SUMS[step[2]]
                    k = side * len(SUMS) + step[2]
                    cc, rows = slice(c * CH, (c + 1) * CH), slice(NW * side, NW * side + NW)
                    act.wait_ge(s["products_done"], side * len(UNITS) + LAST[step[2]] + 1)
                    act.activation(m.products[rows, br, cc], ps[0:NW, 4 + k % 2, :], ACT.Copy,
                                   scale=m.gates[0:NW, br:br + 1])
                    act.copy(m.sums[rows, br, cc], ps[NW:P, 4 + k % 2, :]).then_inc(s["banks_free"], 1)
                if step not in plan.fills:
                    continue
                n += 1
                if kind not in BY_ACT:
                    continue
                act.wait_ge(s["fill_ready"], n)
                if kind in ("q", "k", "s") and step[2] == 0 and side != sides[0]:
                    act.wait_ge(s["split_done"], plan.count("split", sides[0], kind))
                bank = spare(n - 1)
                if kind == "q":
                    ins = act.copy(m.rawq[:, step[2], :], bank[:, 0:2 * NW + 2 * RW])
                elif kind in ("k", "s"):
                    r, v = (m.rawk, m.vw) if kind == "k" else (m.raws, m.vs)
                    act.copy(r[:, step[2], :], bank[:, 0:NW + 2 * RW])
                    ins = act.copy(v[:, side, step[2], :], bank[:, NW + 2 * RW:2 * NW + 2 * RW])
                elif kind in ("turn_q1", "turn_q"):
                    _, _, h, k = step
                    dst = m.q1a if kind == "turn_q1" else m.qa
                    ins = act.copy(dst[:, heads(side, h), k * CH:(k + 1) * CH], bank)
                elif kind == "turn_k":
                    _, _, h, k = step
                    kk = slice(k * CH, (k + 1) * CH)
                    act.copy(m.kwa[0:HD, heads(side, h), kk], bank[0:HD, :])
                    ins = act.copy(m.kwb[0:HD, heads(side, h), kk], bank[HD:P, :])
                elif kind == "turn_s":
                    act.copy(m.ksa[0:HD, heads(side), :], bank[0:HD, :].rearrange("p (h n) -> p h n", h=HP))
                    ins = act.copy(m.ksb[0:HD, heads(side), :], bank[HD:P, :].rearrange("p (h n) -> p h n", h=HP))
                ins.then_inc(s["emptied_act"], 1)

        @block.gpsimd
        def _(pool):
            run = in_order(pool, s["rotation"])
            for step in plan.steps:
                if step[0] == "rotate":
                    _, side, name = step
                    pool.wait_ge(s["emptied_act"], plan.by_act(name, side))
                    r = raw[name]
                    nt = r.shape[1]
                    xr, xi = [r[:, :, NW + k * RW:NW + (k + 1) * RW].rearrange("p t (h n) -> p t h n", h=HP)
                              for k in range(2)]
                    co, si = [x[:, 0:nt, :].unsqueeze(2).to_broadcast([P, nt, HP, HALF]) for x in (m.cos, m.sin)]
                    ta, tb, tc = [x[:, 0:nt * RW].rearrange("p (t h n) -> p t h n", t=nt, h=HP)
                                  for x in m.rope_tmp]
                    pool.tensor_tensor(ta, xr, co, ALU.mult)
                    pool.tensor_tensor(tb, xi, si, ALU.mult)
                    run(pool.tensor_tensor(tc, xr, si, ALU.mult))
                    run(pool.tensor_tensor(xr, ta, tb, ALU.subtract))
                    run(pool.tensor_tensor(ta, xi, co, ALU.mult))
                    run(pool.tensor_tensor(xi, tc, ta, ALU.add))
                elif step[0] == "divide" and step[3] == PIECES - 1:
                    k = step[2]
                    br, c = SUMS[k]
                    cc = slice(c * CH, (c + 1) * CH)
                    o = m.products[:, br, cc]
                    pool.wait_ge(s["inverse_done"], PIECES * (k + 1))
                    pool.tensor_tensor(o, o, m.sums[:, br, cc], ALU.mult).then_inc(s["divided"], 1)
                    if br == 2:
                        pool.wait_ge(s["divided"], k + 1)
                        pool.tensor_tensor(m.products[:, 1, cc], m.products[:, 1, cc], o, ALU.add)\
                            .then_inc(s["o_done"], 1)
                elif step[0] == "split":
                    _, side, name = step
                    pool.wait_ge(s["hi_done"], plan.count(*step))
                    for at, src in split_pieces(raw[name], name):
                        nt, w = src.shape[1], src.shape[3]
                        ins = pool.tensor_tensor(m.tok[:, 0:nt, :, HD + at:HD + at + w].bitcast(F32R), src,
                                                 m.tok[:, 0:nt, :, at:at + w], ALU.subtract)
                    ins.then_inc(s["split_done"], 1)

        @block.vector
        def _(dve):
            n = 0
            rows = 0
            for step in plan.steps:
                kind, side = step[:2]
                if kind == "split":
                    name = step[2]
                    if name != "q1":
                        dve.wait_ge(s["fill_ready"], plan.up_to(BEFORE[name], side))
                    elif side != sides[0]:
                        dve.wait_ge(s["fill_ready"], plan.up_to(BEFORE[name], sides[0]))
                    dve.wait_ge(s["rotation"], 4 * plan.count("rotate", side, "q" if name == "q1" else name))
                    for at, src in split_pieces(raw[name], name):
                        nt, w = src.shape[1], src.shape[3]
                        ins = dve.tensor_copy(m.tok[:, 0:nt, :, at:at + w].bitcast(F32R), src)
                    ins.then_inc(s["hi_done"], 1)
                elif kind == "whole":
                    dve.wait_ge(s["emptied_dve"], plan.by_dve("max0", side))
                    dve.tensor_reduce(negs[0], partial, AX, ALU.max, negate=True).then_inc(s["max_done"], 1)
                elif kind == "divide":
                    _, _, k, piece = step
                    br, c = SUMS[k]
                    w = CH // PIECES
                    total = m.sums[:, br, c * CH + piece * w:c * CH + (piece + 1) * w]
                    dve.wait_ge(s["banks_free"], len(SUMS) + k + 1)
                    dve.reciprocal(total, total).then_inc(s["inverse_done"], 1)
                if step not in plan.fills:
                    continue
                n += 1
                if kind in BY_ACT:
                    continue
                bank = spare(n - 1)
                dve.wait_ge(s["fill_ready"], n)
                if kind == "max0":
                    _, _, h, i, part = step
                    w = min((part + 1) * CH, (i + 1) * P) - part * CH
                    ins = dve.tensor_reduce(partial[:, h, i, part:part + 1], bank[:, 0:w], AX, ALU.max)
                elif kind in ("max1", "max2"):
                    _, _, h, k = step
                    w = KEEP if kind == "max1" else WN
                    at = h * NT + 2 * k
                    ins = dve.tensor_reduce(negs[1 if kind == "max1" else 2][:, at:at + 2],
                                            bank.rearrange("p (i n) -> p i n", i=2)[:, :, 0:w], AX, ALU.max,
                                            negate=True)
                elif kind == "rows":
                    if rows > 0:
                        dve.wait_ge(s["max_rows"], 16 * rows)
                    rows += 1
                    ins = dve.tensor_copy(m.mrow.bitcast(F32R), bank[0:HP * NT, 0:P])
                else:
                    cc = slice(step[2] * CH, (step[2] + 1) * CH)
                    ins = dve.tensor_tensor(m.t2[:, cc], m.t2[:, cc], bank, ALU.add)
                ins.then_inc(s["emptied_dve"], 1)
    phase_end(nc, s)
    stack.close()


TILES = -(-NE * HID // P)
BEHIND = 3
RING = 4
GATE_LO = 32
STAGES = ("turn 0", "turn 1", "stats", "normed", "turn back 0", "turn back 1", "logits", "shift", "softmax",
          "gates", "turn gates 0", "turn gates 1")


def ffn_steps(tiles, prepare):
    if not tiles:
        return list(STAGES)
    first, apart = 2, 3
    todo = []
    for n in range(NC * TILES):
        todo.append(n)
        k, rest = divmod(n - first, apart)
        if prepare and n >= first and rest == 0 and k < len(STAGES):
            todo.append(STAGES[k])
        if n == TILES + BEHIND - 1:
            todo.append("result")
    return todo


def experts_part(nc, d, t2_dram, out, ps, ident, eps, sb):
    m = Mem()
    m.ps, m.d, m.ident, m.eps = ps, d, ident, eps
    m.w1 = [sb(n, [C, TILES * P], F32R) for n in ("w1h", "w1l")]
    m.w3 = [sb(n, [C, TILES * P], F32R) for n in ("w3h", "w3l")]
    m.w2 = [sb(n, [P, TILES * C], F32R) for n in ("w2h", "w2l")]
    m.owner = sb("owner", [P, TILES * P], F32R)
    m.router = sb("router", [C, NE])
    m.tie = sb("tie", [P, NE, NE])
    m.t2 = sb("t2b", [C, T])
    m.xh = sb("xh", [C, T], F32R)
    m.xl = sb("xl", [C, T], F32R)
    m.g = sb("g", [P, T], F32R)
    m.t2n = sb("t2n", [C, T])
    m.xhn = sb("xhn", [C, T], F32R)
    m.xln = sb("xln", [C, T], F32R)
    m.gn = sb("gn", [P, T], F32R)
    m.t_tok = sb("t_tok", [P, NT, P])
    m.xn = sb("xn", [P, NT, P])
    m.xf = sb("xf", [C, T])
    m.st = sb("st", [P, NT, 6])
    m.mv = sb("mv", [P, NT, 2])
    m.std, m.rstd, m.top, m.tot, m.inv = [sb(n, [P, NT]) for n in ("std", "rstd", "top", "tot", "inv")]
    m.pr, m.gt, m.rank = [sb(n, [P, NT, NE]) for n in ("pr", "gt", "rank")]
    m.more, m.same = [sb(n, [P, NT, NE * NE]) for n in ("more", "same")]
    m.act_s = sb("act_s", [P, 2, CH])
    m.mid = sb("mid", [P, 2, CH])
    m.res = sb("res", [C, 2, CH])
    with ExitStack() as stage_mem:
        stage = [stage_mem.enter_context(nc.sbuf_tensor(f"stage_{n}", [P, TILES * P], F32)) 
                 for n in ("w1", "w3", "w2", "owner")]
        experts_block(nc, m, None, t2_dram[0], stage=stage)
    m.hid = sb("hid", [P, RING, CH])
    m.hh = sb("hh", [P, RING, CH], F32R)
    m.hl = sb("hl", [P, RING, CH], F32R)
    with nc.Fori(0, B - 1) as b:
        experts_block(nc, m, (t2_dram[0:B - 1][b], out[0:B - 1][b]), t2_dram[1:B][b])
    experts_block(nc, m, (t2_dram[B - 1], out[B - 1]), None)


def experts_block(nc, m, batch, following, stage=None):
    ps, d = m.ps, m.d
    steps = ffn_steps(batch is not None, following is not None)
    weights = [m.w1, m.w3, m.w2]
    side = ps[:, 7, :]
    stack = ExitStack()
    s = open_sems(nc, stack, "side_ready side_read stream_loaded small_loaded w_loaded w_hi w_lo g_zeroed "
                             "next_loaded t_copied stats aggregated std_done xn_done xh_done xl_done shifted exp_done "
                             "chain gates_done gh_done gl_done h1_ready h3_ready g_ready silu_done mid_done hid_done "
                             "hi_done lo_done used res_done stored moved")

    def once_read(engine, fills):
        if fills:
            engine.wait_ge(s["side_read"], fills)

    FILLED = ("turn 0", "turn 1", "turn back 0", "turn back 1", "logits", "turn gates 0", "turn gates 1")
    READS = {"turn 0": 1, "turn 1": 1, "turn back 0": 2, "turn back 1": 2, "logits": 1, "turn gates 0": 1,
             "turn gates 1": 1}

    def reads_before(stage_):
        return sum(READS[x] for x in FILLED[:FILLED.index(stage_)])

    def filled(stage_):
        return FILLED.index(stage_) + 1

    with nc.Block() as block:
        @block.sync
        def _(sp):
            if following is not None:
                sp.dma_start(m.t2n[:], following).then_inc(s["next_loaded"], 16)
            if stage:
                for k, name in enumerate(("w1", "w3", "w2", "owner")):
                    sp.dma_start(stage[k][:], d[name]).then_inc(s["w_loaded"], 16)
                    sp.wait_ge(s["w_loaded"], 16 * (k + 1))
                sp.dma_start(m.router[:], d["router"]).then_inc(s["small_loaded"], 16)
                sp.dma_start(m.tie[:], d["tie"]).then_inc(s["small_loaded"], 16)
                sp.wait_ge(s["small_loaded"], 32)
            if batch:
                sp.dma_start(m.t2[:], batch[0]).then_inc(s["stream_loaded"], 16)
                for c in range(NC):
                    sp.wait_ge(s["res_done"], c + 1)
                    sp.dma_start(batch[1][:, c * CH:(c + 1) * CH], m.res[:, c, :]).then_inc(s["stored"], 16)
                sp.wait_ge(s["stored"], 16 * NC)

        @block.tensor
        def _(pe):
            def three(bank, w, x, first=True, last=True):
                pe.matmul(bank, w[0], x[0], start=first, stop=False)
                pe.matmul(bank, w[0], x[1], start=False, stop=False)
                return pe.matmul(bank, w[1], x[0], start=False, stop=last)

            def hidden(n):
                c, k = divmod(n, TILES)
                kk, cc = slice(k * P, (k + 1) * P), slice(c * CH, (c + 1) * CH)
                if n >= 2:
                    pe.wait_ge(s["mid_done"], n - 1)
                x = (m.xh[:, cc], m.xl[:, cc])
                three(ps[:, n % 2, :], [w[:, kk] for w in m.w1], x).then_inc(s["h1_ready"], 1)
                three(ps[:, 2 + n % 2, :], [w[:, kk] for w in m.w3], x).then_inc(s["h3_ready"], 1)
                if n >= 2:
                    pe.wait_ge(s["hid_done"], n - 1)
                pe.matmul(ps[:, 4 + n % 2, :], m.owner[:, kk], m.g[:, cc], start=True, stop=True)\
                    .then_inc(s["g_ready"], 1)

            def output(n):
                c, k = divmod(n, TILES)
                if c > 0 and k == 0:
                    pe.wait_ge(s["res_done"], c)
                pe.wait_ge(s["hi_done"], n + 1)
                pe.wait_ge(s["lo_done"], n + 1)
                kk = slice(k * C, (k + 1) * C)
                three(ps[:, 6, :], [w[:, kk] for w in m.w2], (m.hh[:, n % RING, :], m.hl[:, n % RING, :]),
                      first=k == 0, last=k == TILES - 1).then_inc(s["used"], 1)

            for step in steps:
                if step in FILLED:
                    once_read(pe, reads_before(step))
                    k = int(step[-1]) if step[-1] in "01" else 0
                if step in ("turn 0", "turn 1"):
                    pe.wait_ge(s["next_loaded"], 16)
                    for i in range(4):
                        t = 4 * k + i
                        mm = pe.transpose(side[:, i * P:(i + 1) * P], m.t2n[:, t * P:(t + 1) * P], m.ident[:])
                elif step in ("turn back 0", "turn back 1"):
                    pe.wait_ge(s["xn_done"], 4 * (k + 1))
                    for i in range(4):
                        mm = pe.transpose(side[:, i * P:(i + 1) * P], m.xn[:, 4 * k + i, :], m.ident[:])
                elif step == "logits":
                    if stage:
                        pe.wait_ge(s["small_loaded"], 32)
                    for t in range(NT):
                        mm = pe.matmul(side[:, t * NE:(t + 1) * NE], m.xf[:, t * P:(t + 1) * P], m.router[:],
                                       start=True, stop=True)
                elif step in ("turn gates 0", "turn gates 1"):
                    pe.wait_ge(s["gates_done"], 1)
                    for i in range(4):
                        mm = pe.transpose(side[0:NE, i * P:(i + 1) * P], m.gt[:, 4 * k + i, :], m.ident[:])
                if step in FILLED:
                    mm.then_inc(s["side_ready"], 1)
                if isinstance(step, int):
                    hidden(step)
                    if step >= BEHIND:
                        output(step - BEHIND)
            if batch:
                for n in range(NC * TILES - BEHIND, NC * TILES):
                    output(n)

        @block.scalar
        def _(act):
            def split(n):
                if n >= RING:
                    act.wait_ge(s["used"], n - RING + 1)
                act.wait_ge(s["hid_done"], n + 1)
                act.copy(m.hh[:, n % RING, :], m.hid[:, n % RING, :]).then_inc(s["hi_done"], 1)

            if stage:
                for k, w in enumerate(weights):
                    act.wait_ge(s["w_loaded"], 16 * (k + 1))
                    act.copy(w[0][:], stage[k][:]).then_inc(s["w_hi"], 1)
                act.wait_ge(s["w_loaded"], 16 * 4)
                act.copy(m.owner[:], stage[3][:])
            for step in steps:
                if step in FILLED:
                    k = int(step[-1]) if step[-1] in "01" else 0
                    kk = slice(k * CH, (k + 1) * CH)
                if step in ("turn 0", "turn 1"):
                    act.wait_ge(s["side_ready"], filled(step))
                    act.copy(m.t_tok[:, 4 * k:4 * k + 4, :], side.rearrange("p (t n) -> p t n", t=4))\
                        .then_inc(s["side_read"], 1)
                elif step == "stats":
                    act.wait_ge(s["aggregated"], NT)
                    act.activation(m.std[:], m.mv[:, :, 1], ACT.Sqrt, bias=m.eps[:, 0:1]).then_inc(s["std_done"], 1)
                elif step in ("turn back 0", "turn back 1"):
                    act.wait_ge(s["side_ready"], filled(step))
                    act.copy(m.xf[:, kk], side).then_inc(s["side_read"], 1)
                    act.copy(m.xhn[:, kk], side).then_inc(s["xh_done"], 1)
                elif step == "shift":
                    act.wait_ge(s["shifted"], 1)
                    act.activation(m.pr[:], m.pr[:], ACT.Exp).then_inc(s["exp_done"], 1)
                elif step in ("turn gates 0", "turn gates 1"):
                    act.wait_ge(s["side_ready"], filled(step))
                    if stage:
                        act.wait_ge(s["g_zeroed"], 1)
                    act.copy(m.gn[0:NE, kk], side[0:NE, :]).then_inc(s["gh_done"], 1)
                elif isinstance(step, int):
                    act.wait_ge(s["h1_ready"], step + 1)
                    if step >= 2:
                        act.wait_ge(s["mid_done"], step - 1)
                    act.activation(m.act_s[:, step % 2, :], ps[:, step % 2, :], ACT.Silu).then_inc(s["silu_done"], 1)
                    if step >= 1:
                        split(step - 1)
            if batch:
                split(NC * TILES - 1)
            if following is not None:
                if batch:
                    act.wait_ge(s["used"], NC * TILES)
                act.copy(m.xh[:], m.xhn[:]).then_inc(s["moved"], 1)

        @block.gpsimd
        def _(pool):
            if stage:
                pool.memset(m.gn[:].bitcast(F32), 0.0).then_inc(s["g_zeroed"], 1)
                pool.wait_ge(s["w_hi"], 1)
                pool.tensor_tensor(m.w1[1][:], stage[0][:], m.w1[0][:].bitcast(F32), ALU.subtract)\
                    .then_inc(s["w_lo"], 1)
            if batch:
                for n in range(NC * TILES):
                    if n >= RING:
                        pool.wait_ge(s["used"], n - RING + 1)
                    pool.wait_ge(s["hi_done"], n + 1)
                    pool.tensor_tensor(m.hl[:, n % RING, :], m.hid[:, n % RING, :], m.hh[:, n % RING, :].bitcast(F32),
                                       ALU.subtract).then_inc(s["lo_done"], 1)

        @block.vector
        def _(dve):
            run = in_order(dve, s["chain"])

            def result(c):
                dve.wait_ge(s["used"], TILES * (c + 1))
                dve.wait_ge(s["stream_loaded"], 16)
                dve.tensor_tensor(m.res[:, c, :], ps[:, 6, :], m.t2[:, c * CH:(c + 1) * CH], ALU.add)\
                    .then_inc(s["res_done"], 1)

            for step in steps:
                if step in FILLED:
                    k = int(step[-1]) if step[-1] in "01" else 0
                    kk = slice(k * CH, (k + 1) * CH)
                if step == "stats":
                    dve.wait_ge(s["side_read"], 2)
                    for t in range(NT):
                        dve.bn_stats(m.st[:, t, :], m.t_tok[:, t, :]).then_inc(s["stats"], 1)
                    dve.wait_ge(s["stats"], NT)
                    for t in range(NT):
                        dve.bn_aggr(m.mv[:, t, :], m.st[:, t, :]).then_inc(s["aggregated"], 1)
                elif step == "normed":
                    dve.wait_ge(s["std_done"], 1)
                    run(dve.reciprocal(m.rstd[:], m.std[:]))
                    for t in range(NT):
                        dve.tensor_scalar(m.xn[:, t, :], m.t_tok[:, t, :], m.mv[:, t, 0:1], m.rstd[:, t:t + 1],
                                          ALU.subtract, ALU.mult).then_inc(s["xn_done"], 1)
                elif step in ("turn back 0", "turn back 1"):
                    dve.wait_ge(s["xh_done"], k + 1)
                    dve.tensor_tensor(m.xln[:, kk], side, m.xhn[:, kk].bitcast(F32), ALU.subtract)\
                        .then_inc(s["side_read"], 1)
                elif step == "shift":
                    dve.wait_ge(s["side_ready"], filled("logits"))
                    lg = side[:, 0:NT * NE].rearrange("p (t e) -> p t e", t=NT)
                    run(dve.tensor_reduce(m.top[:], lg, AX, ALU.max))
                    dve.tensor_tensor(m.pr[:], lg, each_tile(m.top[:], NE), ALU.subtract).then_inc(s["shifted"], 1)
                elif step == "softmax":
                    dve.wait_ge(s["exp_done"], 1)
                    run(dve.tensor_reduce(m.tot[:], m.pr[:], AX, ALU.add))
                    run(dve.reciprocal(m.inv[:], m.tot[:]))
                    dve.tensor_tensor(m.pr[:], m.pr[:], each_tile(m.inv[:], NE), ALU.mult).then_inc(s["side_read"], 1)
                    if stage:
                        dve.wait_ge(s["small_loaded"], 32)
                    dve.wait_ge(s["side_read"], reads_before("turn gates 0"))
                    other = m.pr[:].unsqueeze(2).to_broadcast([P, NT, NE, NE])
                    own = m.pr[:].unsqueeze(3).to_broadcast([P, NT, NE, NE])
                    more4 = m.more[:].rearrange("p t (a b) -> p t a b", a=NE)
                    same4 = m.same[:].rearrange("p t (a b) -> p t a b", a=NE)
                    dve.tensor_tensor(more4, other, own, ALU.is_gt)
                    run(dve.tensor_tensor(same4, other, own, ALU.is_equal))
                    run(dve.tensor_tensor(m.same[:], m.same[:], each_token(m.tie[:].rearrange("p a b -> p (a b)"), NT),
                                          ALU.mult))
                elif step == "gates":
                    run(dve.tensor_tensor(m.more[:], m.more[:], m.same[:], ALU.add))
                    run(dve.tensor_reduce(m.rank[:], m.more[:].rearrange("p t (a b) -> p t a b", a=NE), AX, ALU.add))
                    run(dve.tensor_scalar(m.rank[:], m.rank[:], 1.5, None, ALU.is_lt))
                    run(dve.tensor_tensor(m.gt[:], m.pr[:], m.rank[:], ALU.mult))
                    run(dve.tensor_reduce(m.tot[:], m.gt[:], AX, ALU.add))
                    run(dve.tensor_scalar(m.tot[:], m.tot[:], 1e-9, None, ALU.add))
                    run(dve.reciprocal(m.inv[:], m.tot[:]))
                    dve.tensor_tensor(m.gt[:], m.gt[:], each_tile(m.inv[:], NE), ALU.mult).then_inc(s["gates_done"], 1)
                elif step in ("turn gates 0", "turn gates 1"):
                    dve.wait_ge(s["gh_done"], k + 1)
                    dve.tensor_tensor(m.gn[GATE_LO:GATE_LO + NE, kk], side[0:NE, :], m.gn[0:NE, kk].bitcast(F32),
                                      ALU.subtract).then_inc(s["side_read"], 1)
                elif step == "result":
                    result(0)
                elif isinstance(step, int):
                    n = step
                    dve.wait_ge(s["h3_ready"], n + 1)
                    dve.wait_ge(s["silu_done"], n + 1)
                    dve.tensor_tensor(m.mid[:, n % 2, :], ps[:, 2 + n % 2, :], m.act_s[:, n % 2, :], ALU.mult)\
                        .then_inc(s["mid_done"], 1)
                    dve.wait_ge(s["g_ready"], n + 1)
                    dve.wait_ge(s["mid_done"], n + 1)
                    if n >= RING:
                        dve.wait_ge(s["lo_done"], n - RING + 1)
                    dve.tensor_tensor(m.hid[:, n % RING, :], ps[:, 4 + n % 2, :], m.mid[:, n % 2, :], ALU.mult)\
                        .then_inc(s["hid_done"], 1)
            if following is not None:
                if batch:
                    dve.wait_ge(s["used"], NC * TILES)
                if stage:
                    dve.wait_ge(s["g_zeroed"], 1)
                dve.tensor_copy(m.xl[:], m.xln[:].bitcast(F32)).then_inc(s["moved"], 1)
                dve.wait_ge(s["side_read"], reads_before("turn gates 1") + READS["turn gates 1"])
                dve.tensor_copy(m.g[:], m.gn[:].bitcast(F32)).then_inc(s["moved"], 1)
            if batch:
                result(NC - 1)
            if stage:
                for k in (1, 2):
                    dve.wait_ge(s["w_hi"], k + 1)
                    dve.tensor_tensor(weights[k][1][:], stage[k][:], weights[k][0][:].bitcast(F32), ALU.subtract)\
                        .then_inc(s["w_lo"], 1)
    phase_end(nc, s)
    stack.close()


def split_pieces(r, name):
    at = NW + 2 * RW if name == "q1" else 0
    heads = "p t (h n) -> p t h n"
    found = [(0, r[:, :, at:at + NW].rearrange(heads, h=HP))]
    if name != "q":
        found += [(NOPE + k * HALF, r[:, :, NW + k * RW:NW + (k + 1) * RW].rearrange(heads, h=HP)) for k in range(2)]
    return found


def by_turn(w, n):
    w = w.reshape(w.shape[0], NH // HP, HP, -1)
    parts = np.split(w, np.cumsum(n)[:-1], axis=3)
    return [np.roll(p.reshape(w.shape[0], NH // HP, -1), -1, axis=1).reshape(w.shape[0], NG, 2, -1)
            .transpose(1, 0, 2, 3) for p in parts]


def kernel(**inputs):
    import concourse.bacc as bacc
    from concourse.bass_utils import run_bass_kernel_spmd
    from ml_dtypes import bfloat16

    f = {k: np.asarray(x) for k, x in inputs.items()}
    c_, a_, e_ = ({k[len(p):]: x for k, x in f.items() if k.startswith(p)} for p in ("L0_conv_", "L1_attn_", "L1_ffn_"))
    arrays = {"x": f["x"].reshape(B, C, T)}
    a, b = np.arange(P)[:, None], np.arange(P)[None]
    w = np.arange(WN)[None]
    arrays["ident"] = np.eye(P, dtype=np.float32)
    arrays["ident_bf"] = np.eye(P).astype(bfloat16)
    arrays["causal_q"] = np.where(b <= a, 0, MASKED).astype(bfloat16)
    arrays["causal_k"] = np.where(a <= b, 0, MASKED).astype(bfloat16)
    arrays["window_q0"] = np.where((w <= a) & (a - w < WINDOW), 0, MASKED).astype(bfloat16)
    arrays["window_q"] = np.where((w > a) & (w <= a + WINDOW), 0, MASKED).astype(bfloat16)
    arrays["window_k"] = np.where((w >= a) & (w - a < WINDOW), 0, MASKED).astype(bfloat16)
    freq = 1.0 / 10000.0 ** (np.arange(0, 2 * HALF, 2, dtype=np.float32) / (2 * HALF))
    angle = np.outer(np.arange(T, dtype=np.float32), freq)
    for name, fn in (("cos", np.cos), ("sin", np.sin)):
        arrays[name] = fn(angle).astype(np.float32).reshape(NT, P, HALF).transpose(1, 0, 2)
    arrays["before"] = (a < b).astype(np.float32)
    arrays["below"] = (b < a).astype(np.float32)
    arrays["iota"] = np.broadcast_to(np.arange(KEEP, dtype=np.float32), (P, KEEP))
    units_of = np.repeat(np.eye(NE, dtype=np.float32), HID, axis=1)
    arrays["owner"] = np.zeros((P, TILES * P), np.float32)
    for row in (0, GATE_LO):
        arrays["owner"][row:row + NE, :NE * HID] = units_of
    arrays["tie"] = np.broadcast_to(np.tril(np.ones((NE, NE), np.float32), -1), (P, NE, NE))
    twice = lambda x: np.concatenate([x, x], axis=-1)
    arrays["wt2"], arrays["wp2"] = twice(c_["Wt"].T), twice(c_["Wp"].T)
    arrays["wg"], arrays["wo"] = c_["Wg"].T, c_["Wo"].T
    arrays["bias"] = np.stack([twice(c_["bt"]), twice(c_["bp"]), twice(c_["bg"]), c_["bo"]], axis=1)
    arrays["wa"] = np.concatenate([a_["Wcq"], a_["Wckv"], a_["Wk_rope"], a_["W_imp"], a_["Wgate"]], axis=1)
    arrays["qnw"] = np.broadcast_to(a_["q_norm_w"], (P, QR))
    arrays["kvnw"] = np.broadcast_to(a_["kv_norm_w"], (P, KVR))
    arrays["wqn_t"] = a_["Wq_nope"].reshape(QR, NG, P).transpose(2, 1, 0)
    arrays["wproj"] = a_["Wproj"].reshape(NG, P, C).transpose(1, 0, 2)
    arrays["wproj_g"] = a_["Wproj"].reshape(NG, P, C)
    for name, x in (("wk_t", a_["Wk_nope"]), ("wv_t", a_["Wv"])):
        arrays[name] = x.reshape(KVR, NG, HG, 32).transpose(1, 2, 3, 0)
    rot = [HALF, HALF]
    arrays["wq"] = np.concatenate(by_turn(a_["Wq_nope"], [NOPE]) + by_turn(a_["Wq_rope"], rot), axis=3)
    arrays["wk"] = np.concatenate(by_turn(a_["Wwin_k"], [NOPE] + rot) + by_turn(a_["Wwin_v"], [VD]), axis=3)
    arrays["ws"] = np.concatenate(by_turn(a_["Wsel_k"], [NOPE] + rot) + by_turn(a_["Wsel_v"], [VD]), axis=3)
    arrays["router"] = e_["router_w"].T
    full = lambda x: np.concatenate([x, np.zeros((TILES * P - NE * HID, C), x.dtype)])
    arrays["w1"] = full(e_["w1"].reshape(NE * HID, C)).T
    arrays["w3"] = full(e_["w3"].reshape(NE * HID, C)).T
    arrays["w2"] = full(e_["w2"].transpose(0, 2, 1).reshape(NE * HID, C)).reshape(TILES, P, C)\
        .transpose(1, 0, 2).reshape(P, TILES * C)
    arrays = {k: np.ascontiguousarray(x) for k, x in arrays.items()}

    nc = bacc.Bacc("TRN2", target_bir_lowering=False, num_devices=1)
    d = {k: nc.dram_tensor("in_" + k, x.shape, mybir.dt.from_np(x.dtype), kind="ExternalInput").ap()
         for k, x in arrays.items()}
    out = nc.dram_tensor("out", (B, C, T), F32, kind="ExternalOutput").ap()
    program(nc, d, out)
    r = run_bass_kernel_spmd(nc, [{"in_" + k: x for k, x in arrays.items()}], core_ids=[0])
    return r.results[0]["out"].reshape(B, C, 32, 32)
```

```python
from contextlib import ExitStack

import numpy as np

import concourse.bass as bass
from concourse import mybir

F32 = mybir.dt.float32
F32R = mybir.dt.float32r
BF16 = mybir.dt.bfloat16
ALU = mybir.AluOpType
ACT = mybir.ActivationFunctionType
AX = mybir.AxisListType.X

P = 128
B, C, T = 4, 128, 1024
NT = T // P
CH = 512
NC = T // CH
CI = 64
QR, KVR = 48, 32
NH, HG = 16, 4
NG = NH // HG
HP = HG // 2
NOPE, HALF = 32, 16
HD = NOPE + 2 * HALF
VD = 32
NW, RW = HP * NOPE, HP * HALF
KEEP, WINDOW = 256, 64
SCALE = 1.0 / 8.0
NE, HID = 8, 341
WN = P + WINDOW
LNE, RMSE = 1e-5, 1e-6
MASKED = -8.0e9
A_CQ, A_KV, A_KR, A_IMP, A_GATE, A_N = 0, 48, 80, 112, 113, 116


def phase_end(nc, sems):
    engines = (nc.sync, nc.gpsimd, nc.tensor, nc.vector, nc.scalar)
    for k, s in enumerate(sems.values()):
        engines[k % len(engines)].sem_clear(s)
    nc.all_engine_barrier()


def open_sems(nc, ctx, names):
    return {n: ctx.enter_context(nc.semaphore(n)) for n in names.split()}


def program(nc, d, out):
    with ExitStack() as top:
        def sb(ctx, name, shape, dt=F32):
            return ctx.enter_context(nc.sbuf_tensor(name, shape, dt))

        ps = top.enter_context(nc.psum_tensor("ps", [P, 8, CH], F32))
        t2_dram = nc.dram_tensor("t2_dram", (B, C, T), F32, kind="Internal").ap()
        wqp_dram = nc.dram_tensor("wqp_dram", (QR, NG, 2 * NW), F32, kind="Internal").ap()
        wvp_dram = nc.dram_tensor("wvp_dram", (NG, P, C), F32, kind="Internal").ap()
        d = dict(d, wqp=wqp_dram, wvp=wvp_dram)
        ident = sb(top, "ident", [P, P])
        eps = sb(top, "eps", [P, 2])
        with ExitStack() as att_mem:
            attention_part(nc, d, t2_dram, ps, ident, eps, lambda *a: sb(att_mem, *a))
        with ExitStack() as ffn_mem:
            experts_part(nc, d, t2_dram, out, ps, ident, eps, lambda *a: sb(ffn_mem, *a))


class Mem:
    pass


def attention_part(nc, d, t2_dram, ps, ident, eps, sb):
    m = Mem()
    m.ps, m.d, m.ident, m.eps = ps, d, ident, eps
    m.ident_bf = sb("ident_bf", [P, P], BF16)
    m.causal_q = sb("causal_q", [P, P], BF16)
    m.causal_k = sb("causal_k", [P, P], BF16)
    m.window_q0 = sb("window_q0", [P, WN], BF16)
    m.window_q = sb("window_q", [P, WN], BF16)
    m.window_k = sb("window_k", [P, WN], BF16)
    m.cos = sb("cos", [P, NT, HALF])
    m.sin = sb("sin", [P, NT, HALF])
    m.before = sb("before", [P, P])
    m.below = sb("below", [P, P])
    m.ones = sb("ones", [P, P])
    m.iota = sb("iota", [P, KEEP])
    m.earlier = sb("earlier", [P, NT, NT])
    m.wt2 = sb("wt2", [C, 2 * CI])
    m.wp2 = sb("wp2", [C, 2 * CI])
    m.wg = sb("wg", [C, CI])
    m.wo = sb("wo", [CI, C])
    m.bias = sb("bias", [P, 4])
    m.wa = sb("wa", [C, A_N])
    m.qnw = sb("qnw", [P, QR])
    m.kvnw = sb("kvnw", [P, KVR])
    m.xnT = sb("xnT", [C, T])
    m.cqT = sb("cqT", [P, T])
    m.k1a = sb("k1a", [P, T], F32R)
    m.k1b = sb("k1b", [P, T], F32R)
    m.v1 = sb("v1", [P, NT, KVR])
    m.selT = sb("selT", [C, KEEP])
    m.t2 = sb("t2", [C, T])
    m.gates = sb("gates", [P, 3])
    m.small = sb("small", [P, 512])
    m.wq_g = sb("wq_g", [P, 2, 2 * NW + 2 * RW])
    m.wk_g = sb("wk_g", [C, 2, 2 * NW + 2 * RW])
    m.ws_g = sb("ws_g", [C, 2, 2 * NW + 2 * RW])
    m.wproj_g = sb("wproj_g", [P, C])
    m.wvp_g = sb("wvp_g", [P, C])
    m.vw = sb("vw", [P, 2, NT, NW])
    m.vs = sb("vs", [P, 2, KEEP // P, NW])
    m.q1a = sb("q1a", [P, HG, T], F32R)
    m.q1b = sb("q1b", [P, HG, T], F32R)
    m.qa = sb("qa", [P, HG, T], F32R)
    m.qb = sb("qb", [P, HG, T], F32R)
    m.kwa = sb("kwa", [P, HG, T], F32R)
    m.kwb = sb("kwb", [P, HG, T], F32R)
    m.ksa = sb("ksa", [P, HG, KEEP], F32R)
    m.ksb = sb("ksb", [P, HG, KEEP], F32R)
    raw_n = 2 * NW + 2 * RW
    sizes = dict(products=3 * T, sums=3 * T, prob=PROBS * HP * CH, tok=NT * HP * 2 * HD, rawq=NT * raw_n,
                 rawk=NT * (NW + 2 * RW), raws=KEEP // P * (NW + 2 * RW), rope=3 * NT * RW, mrow=2 * P)
    arena = sb("arena", [P, sum(sizes.values())])
    at, part = 0, {}
    for name, n in sizes.items():
        part[name] = arena[:, at:at + n]
        at += n
    m.products = part["products"].rearrange("p (b n) -> p b n", b=3)
    m.sums = part["sums"].rearrange("p (b n) -> p b n", b=3)
    m.prob = part["prob"].rearrange("p (a h n) -> p a h n", a=PROBS, h=HP)
    m.tok = part["tok"].rearrange("p (t h n) -> p t h n", t=NT, h=HP)
    m.rawq = part["rawq"].rearrange("p (t n) -> p t n", t=NT)
    m.rawk = part["rawk"].rearrange("p (t n) -> p t n", t=NT)
    m.raws = part["raws"].rearrange("p (t n) -> p t n", t=KEEP // P)
    m.rope_tmp = [part["rope"][:, k * NT * RW:(k + 1) * NT * RW] for k in range(3)]
    m.mrows = [part["mrow"][0:HP * NT, k * P:(k + 1) * P] for k in range(2)]
    m.x = arena[:, 12 * T:13 * T]
    m.tokf = arena[:, 0:4 * T]
    m.rawqf = arena[:, 4 * T:7 * T]
    m.obuf = arena[:, 7 * T:10 * T]
    m.probf = arena[:, 10 * T:12 * T]
    m.ones_row = arena[0:1, 7 * T:11 * T]
    m.rden = m.obuf[:, 2 * T:2 * T + CH]

    m.early = Early(m)
    weights_and_constants(nc, m, d)
    with nc.Fori(0, B) as b:
        nonlocal_block(nc, m, b)
        normed(nc, m)
        turns(nc, m, PREPARE, NG - 1)
        turns(nc, m, FIRST_GROUP, 0)
        with nc.Fori(1, NG - 1) as g:
            turns(nc, m, GROUP, g)
        turns(nc, m, LAST_GROUP, NG - 1, (t2_dram[b], d["x_next"][b]))


def weights_and_constants(nc, m, d):
    stack = ExitStack()
    s = open_sems(nc, stack, "s_load s_mm s_copy s_row s_one s_kept")
    sqn = m.tokf[:, 0:NG * QR].rearrange("p (g n) -> p g n", g=NG)
    kblk = m.tokf[:, 512:1024].rearrange("p (g n) -> p g n", g=NG)
    vblk = m.tokf[:, 1024:1536].rearrange("p (g n) -> p g n", g=NG)
    wpr = m.tokf[:, 1536:2048].rearrange("p (g n) -> p g n", g=NG)
    ones_row = m.ones_row
    wqp = m.rawqf[0:QR, 0:NG * P]
    wvp = m.rawqf[:, NG * P:2 * NG * P].rearrange("p (g n) -> p g n", g=NG)
    with nc.Block() as block:
        consts = [(m.ident, "ident"), (m.ident_bf, "ident_bf"), (m.causal_q, "causal_q"), (m.causal_k, "causal_k"),
                  (m.window_q0, "window_q0"), (m.window_q, "window_q"), (m.window_k, "window_k"), (m.cos, "cos"),
                  (m.sin, "sin"), (m.before, "before"), (m.below, "below"), (m.iota, "iota"), (m.earlier, "tie"), (m.wt2, "wt2"),
                  (m.wp2, "wp2"), (m.wg, "wg"), (m.wo, "wo"), (m.bias, "bias"), (m.wa, "wa"), (m.qnw, "qnw"),
                  (m.kvnw, "kvnw"), (sqn, "wqn_t"), (wpr, "wproj"), (kblk, "wk_t"), (vblk, "wv_t")]
        x_first = (m.x, d["x_next"][B - 1])

        @block.sync
        def _(sp):
            for dst, name in consts:
                sp.dma_start(dst[:] if not isinstance(dst, bass.AP) else dst, d[name]).then_inc(s["s_load"], 16)
            sp.dma_start(*x_first).then_inc(s["s_row"], 16)
            sp.wait_ge(s["s_one"], 9)
            sp.dma_start(m.k1b[64:65, :].bitcast(F32), ones_row[:, 0:T]).then_inc(s["s_row"], 16)
            sp.dma_start(m.kwb[65:66].rearrange("p h n -> p (h n)").bitcast(F32), ones_row).then_inc(s["s_row"], 16)
            sp.dma_start(m.ksb[64:65].rearrange("p h n -> p (h n)").bitcast(F32),
                         ones_row[:, 0:HG * KEEP]).then_inc(s["s_row"], 16)
            sp.wait_ge(s["s_row"], 64)
            sp.wait_ge(s["s_copy"], 2)
            sp.dma_start(d["wvp"].rearrange("g p c -> p g c"), wvp).then_inc(s["s_kept"], 16)
            by_turn_ = d["wqp"].rearrange("q g n -> q (g n)")
            last = (2 * NG - 1) * NW
            sp.dma_start(by_turn_[:, 0:last], wqp[:, NW:]).then_inc(s["s_kept"], 16)
            sp.dma_start(by_turn_[:, last:], wqp[:, 0:NW]).then_inc(s["s_kept"], 16)
            sp.wait_ge(s["s_kept"], 16 * 3)

        @block.vector
        def _(dve):
            dve.memset(m.ones[:], 1.0).then_inc(s["s_one"], 1)
            dve.memset(ones_row, 1.0).then_inc(s["s_one"], 1)
            dve.memset(m.eps[:, 0:1], LNE).then_inc(s["s_one"], 1)
            dve.memset(m.eps[:, 1:2], RMSE).then_inc(s["s_one"], 1)
            for x in (m.k1b, m.kwb, m.ksb, m.q1b, m.qb):
                dve.memset(x[HD:P].bitcast(F32), 0.0).then_inc(s["s_one"], 1)
            dve.memset(m.small[:], -3.0e38)
            dve.memset(m.cqT[:], 0.0)
            dve.memset(m.wq_g[:], 0.0)
            dve.wait_ge(s["s_mm"], 1)
            dve.tensor_copy(wqp, m.ps[0:QR, 0, :]).then_inc(s["s_copy"], 1)
            dve.tensor_copy(wvp, m.ps[:, 1, :].rearrange("p (g n) -> p g n", g=NG)).then_inc(s["s_copy"], 1)

        @block.tensor
        def _(pe):
            pe.wait_ge(s["s_load"], 16 * len(consts))
            for g in range(NG):
                pe.matmul(m.ps[0:QR, 0, g * P:(g + 1) * P], sqn[:, g, :], kblk[:, g, :], start=True, stop=True)
                mm = pe.matmul(m.ps[:, 1, g * P:(g + 1) * P], vblk[:, g, :], wpr[:, g, :], start=True, stop=True)
            mm.then_inc(s["s_mm"], 1)
    phase_end(nc, s)
    stack.close()


def nonlocal_block(nc, m, b):
    ps, d = m.ps, m.d
    x = m.x
    va = m.tokf[:, T:2 * T].rearrange("p (t n) -> p t n", t=NT)
    y = m.tokf[0:CI, 2 * T:3 * T]
    th_a, ph_a = m.q1a[:, 0, :], m.kwa[:, 0, :]
    th_b, ph_b = m.q1b[:, 0, :], m.k1b[:]
    negm = m.small[:, 0:NT]
    mrows = [x[0:NT // NC, :] for x in m.mrows]
    rden = m.rden
    stack = ExitStack()
    s = open_sems(nc, stack, "n_proj n_hi n_lo n_va n_vac n_app n_max n_mt n_mrow n_mdma n_qb "
                           "n_s n_exp n_pv n_chain n_y n_o")

    with nc.Block() as block:
        @block.sync
        def _(sp):
            sp.wait_ge(s["n_hi"], 4)
            sp.dma_start(th_b[0:64, :].bitcast(F32), th_a[0:64, :].bitcast(F32)).then_inc(s["n_qb"], 16)
            for c in range(NC):
                sp.wait_ge(s["n_mrow"], c + 1)
                if c > 0:
                    sp.wait_ge(s["n_mdma"], 16 * c)
                sp.dma_start(th_b[64:65, c * CH:(c + 1) * CH].bitcast(F32), mrows[c]).then_inc(s["n_mdma"], 16)

        @block.tensor
        def _(pe):
            for c in range(NC):
                xc = x[:, c * CH:(c + 1) * CH]
                pe.matmul(ps[:, c, :], m.wt2[:], xc, start=True, stop=True).then_inc(s["n_proj"], 1)
                pe.matmul(ps[:, 2 + c, :], m.wp2[:], xc, start=True, stop=True).then_inc(s["n_proj"], 1)
            for t in range(NT):
                mm = pe.matmul(ps[:, 4, t * CI:(t + 1) * CI], x[:, t * P:(t + 1) * P], m.wg[:],
                               start=True, stop=True)
            mm.then_inc(s["n_va"], 1)
            def turn_max(c):
                n = NT // NC
                pe.wait_ge(s["n_max"], n * (c + 1))
                pe.wait_ge(s["n_vac"], 2)
                pe.transpose(ps[0:n, 4, c * P:(c + 1) * P], negm[:, n * c:n * (c + 1)], m.ident[:])\
                    .then_inc(s["n_mt"], 1)

            pe.wait_ge(s["n_hi"], 4)
            pe.wait_ge(s["n_lo"], 4)
            pe.wait_ge(s["n_vac"], 1)
            for t in range(NT):
                if t >= 2:
                    pe.wait_ge(s["n_max"], t - 1)
                for c in range(NC):
                    mm = pe.matmul(ps[:, 2 * (t % 2) + c, :], th_a[:, t * P:(t + 1) * P],
                                   ph_a[:, c * CH:(c + 1) * CH], start=True, stop=True)
                mm.then_inc(s["n_app"], 1)
                if t == NT - 3:
                    turn_max(0)
            turn_max(1)
            pe.wait_ge(s["n_qb"], 16)

            def scores(u):
                c, j = divmod(u, NT)
                if j == 0:
                    pe.wait_ge(s["n_mdma"], 16 * (c + 1))
                if u >= 4:
                    pe.wait_ge(s["n_exp"], u - 3)
                pe.matmul(ps[:, u % 4, :], ph_a[:, j * P:(j + 1) * P], th_a[:, c * CH:(c + 1) * CH],
                          start=True, stop=False)
                pe.matmul(ps[:, u % 4, :], ph_b[:, j * P:(j + 1) * P], th_b[:, c * CH:(c + 1) * CH],
                          start=False, stop=True).then_inc(s["n_s"], 1)

            def values(u):
                c, j = divmod(u, NT)
                pe.wait_ge(s["n_exp"], u + 1)
                pe.matmul(ps[:, 5 + c, :], va[:, j, :], m.probf[:, (u % 4) * CH:(u % 4 + 1) * CH],
                          start=(j == 0), stop=(j == NT - 1)).then_inc(s["n_pv"], 1)

            scores(0)
            scores(1)
            for u in range(NC * NT):
                if u + 2 < NC * NT:
                    scores(u + 2)
                values(u)
            for c in range(NC):
                pe.wait_ge(s["n_y"], c + 1)
                pe.matmul(ps[:, c, :], m.wo[:], y[:, c * CH:(c + 1) * CH], start=True, stop=True)\
                    .then_inc(s["n_o"], 1)

        @block.scalar
        def _(act):
            for c in range(NC):
                cc = slice(c * CH, (c + 1) * CH)
                act.wait_ge(s["n_proj"], 2 * c + 1)
                act.activation(th_a[:, cc], ps[:, c, :], ACT.Identity, bias=m.bias[:, 0:1]).then_inc(s["n_hi"], 1)
                act.wait_ge(s["n_proj"], 2 * c + 2)
                act.activation(ph_a[:, cc], ps[:, 2 + c, :], ACT.Identity, bias=m.bias[:, 1:2])\
                    .then_inc(s["n_hi"], 1)
            for u in range(NC * NT):
                act.wait_ge(s["n_s"], u + 1)
                if u >= 4:
                    act.wait_ge(s["n_pv"], u - 3)
                act.activation(m.probf[:, (u % 4) * CH:(u % 4 + 1) * CH], ps[:, u % 4, :], ACT.Exp)\
                    .then_inc(s["n_exp"], 1)

        @block.vector
        def _(dve):
            dve.memset(va[:, :, CI:2 * CI], 1.0).then_inc(s["n_vac"], 1)
            for c in range(NC):
                cc = slice(c * CH, (c + 1) * CH)
                dve.wait_ge(s["n_hi"], 2 * c + 1)
                dve.scalar_tensor_tensor(out=th_a[64:128, cc], in0=ps[64:128, c, :], scalar=m.bias[64:128, 0:1],
                                         in1=th_a[64:128, cc].bitcast(F32), op0=ALU.add, op1=ALU.subtract)\
                    .then_inc(s["n_lo"], 1)
                dve.wait_ge(s["n_hi"], 2 * c + 2)
                dve.scalar_tensor_tensor(out=ph_b[0:64, cc], in0=ps[0:64, 2 + c, :], scalar=m.bias[0:64, 1:2],
                                         in1=ph_a[0:64, cc].bitcast(F32), op0=ALU.add, op1=ALU.subtract)\
                    .then_inc(s["n_lo"], 1)
            dve.wait_ge(s["n_va"], 1)
            dve.tensor_copy(va[:, :, 0:CI], ps[:, 4, :].rearrange("p (t n) -> p t n", t=NT)).then_inc(s["n_vac"], 1)
            for t in range(NT):
                dve.wait_ge(s["n_app"], t + 1)
                k = 2 * (t % 2)
                dve.tensor_reduce(negm[:, t:t + 1], ps[:, k:k + 2, :].rearrange("p a n -> p (a n)"), AX, ALU.max,
                                  negate=True).then_inc(s["n_max"], 1)
                if t in (NT - 2, NT - 1):
                    c = t - (NT - 2)
                    dve.wait_ge(s["n_mt"], c + 1)
                    dve.tensor_copy(mrows[c].bitcast(F32R), ps[0:NT // NC, 4, c * P:(c + 1) * P])\
                        .then_inc(s["n_mrow"], 1)
            for c in range(NC):
                cc = slice(c * CH, (c + 1) * CH)
                dve.wait_ge(s["n_pv"], NT * (c + 1))
                dve.reciprocal(rden[0:CI, :], ps[CI:2 * CI, 5 + c, :]).then_inc(s["n_chain"], 1)
                dve.wait_ge(s["n_chain"], 2 * c + 1)
                dve.tensor_tensor(y[:, cc], ps[0:CI, 5 + c, :], rden[0:CI, :], ALU.mult).then_inc(s["n_chain"], 1)
                dve.wait_ge(s["n_chain"], 2 * c + 2)
                dve.tensor_scalar(y[:, cc], y[:, cc], m.bias[0:CI, 2:3], None, ALU.add).then_inc(s["n_y"], 1)
            for c in range(NC):
                cc = slice(c * CH, (c + 1) * CH)
                dve.wait_ge(s["n_o"], c + 1)
                dve.scalar_tensor_tensor(out=m.t2[:, cc], in0=ps[:, c, :], scalar=m.bias[:, 3:4], in1=x[:, cc],
                                         op0=ALU.add, op1=ALU.add)
    phase_end(nc, s)
    stack.close()


def in_order(engine, sem):
    done = [0]

    def run(ins):
        done[0] += 1
        ins.then_inc(sem, 1)
        engine.wait_ge(sem, done[0])
    return run


def each_tile(col, n):
    return col.unsqueeze(2).to_broadcast([P, col.shape[1], n])


def each_token(row, n):
    return row.unsqueeze(1).to_broadcast([P, n, row.shape[1]])


def normed(nc, m):
    ps = m.ps
    t_tok = m.rawqf[:, 0:T]
    xn = m.rawqf[:, T:2 * T]
    pa = m.rawqf[:, 2 * T:2 * T + NT * A_N].rearrange("p (t n) -> p t n", t=NT)
    sm = m.small
    mv = sm[:, 16:32].rearrange("p (t n) -> p t n", t=NT)
    std, rstd = sm[:, 32:40], sm[:, 40:48]
    st = sm[:, 48:96].rearrange("p (t n) -> p t n", t=NT)
    ssq, rms, rrms = sm[:, 96:112], sm[:, 112:128], sm[:, 128:144]
    gsum, gexp, gnm, gtot = sm[:, 144:147], sm[:, 148:151], sm[:, 152:153], sm[:, 153:154]
    grec = sm[:, 154:155]
    with ExitStack() as stack:
        s = open_sems(nc, stack, "t2_turned t_copied chain std_done xn_done xn_turned xnT_done pa_done pa_copied")
        with nc.Block() as block:
            @block.tensor
            def _(pe):
                for t in range(NT):
                    mm = pe.transpose(ps[:, t // 4, (t % 4) * P:(t % 4 + 1) * P], m.t2[:, t * P:(t + 1) * P],
                                      m.ident[:])
                    if t % 4 == 3:
                        mm.then_inc(s["t2_turned"], 1)
                for t in range(NT):
                    pe.wait_ge(s["xn_done"], t + 1)
                    mm = pe.transpose(ps[:, 2 + t // 4, (t % 4) * P:(t % 4 + 1) * P], xn[:, t * P:(t + 1) * P],
                                      m.ident[:])
                    if t % 4 == 3:
                        mm.then_inc(s["xn_turned"], 1)
                for t in range(NT):
                    pe.wait_ge(s["xnT_done"], t // 4 + 1)
                    mm = pe.matmul(ps[:, 4 + t // 4, (t % 4) * A_N:(t % 4 + 1) * A_N],
                                   m.xnT[:, t * P:(t + 1) * P], m.wa[:], start=True, stop=True)
                    if t % 4 == 3:
                        mm.then_inc(s["pa_done"], 1)

            @block.scalar
            def _(act):
                for k in range(2):
                    act.wait_ge(s["t2_turned"], k + 1)
                    act.copy(t_tok[:, k * CH:(k + 1) * CH], ps[:, k, :]).then_inc(s["t_copied"], 1)
                act.wait_ge(s["chain"], 1)
                act.activation(std, mv[:, :, 1], ACT.Sqrt, bias=m.eps[:, 0:1]).then_inc(s["std_done"], 1)
                for k in range(2):
                    act.wait_ge(s["xn_turned"], k + 1)
                    act.copy(m.xnT[:, k * CH:(k + 1) * CH], ps[:, 2 + k, :]).then_inc(s["xnT_done"], 1)

            @block.vector
            def _(dve):
                for t in range(NT):
                    dve.wait_ge(s["t_copied"], t // 4 + 1)
                    ins = dve.bn_stats(st[:, t, :], t_tok[:, t * P:(t + 1) * P])
                    ins.then_inc(s["pa_copied"], 1)
                dve.wait_ge(s["pa_copied"], NT)
                for t in range(NT):
                    ins = dve.bn_aggr(mv[:, t, :], st[:, t, :])
                ins.then_inc(s["chain"], 1)
                dve.wait_ge(s["std_done"], 1)
                dve.wait_ge(s["chain"], 1)
                dve.reciprocal(rstd, std).then_inc(s["chain"], 1)
                dve.wait_ge(s["chain"], 2)
                for t in range(NT):
                    dve.tensor_scalar(xn[:, t * P:(t + 1) * P], t_tok[:, t * P:(t + 1) * P], mv[:, t, 0:1],
                                      rstd[:, t:t + 1], ALU.subtract, ALU.mult).then_inc(s["xn_done"], 1)
                for k in range(2):
                    dve.wait_ge(s["pa_done"], k + 1)
                    dve.tensor_copy(pa[:, 4 * k:4 * k + 4, :],
                                    ps[:, 4 + k, 0:4 * A_N].rearrange("p (t n) -> p t n", t=4))
        phase_end(nc, s)


class Early:

    def __init__(self, m):
        sm = m.small
        self.xn = m.rawqf[:, T:2 * T]
        pa = m.rawqf[:, 2 * T:2 * T + NT * A_N].rearrange("p (t n) -> p t n", t=NT)
        self.cq, self.ckv, self.kr = pa[:, :, A_CQ:A_KV], pa[:, :, A_KV:A_KR], pa[:, :, A_KR:A_IMP]
        self.imp, self.gate = pa[:, :, A_IMP], pa[:, :, A_GATE:A_N]
        self.ssq, self.rms, self.rrms = sm[:, 96:112], sm[:, 112:128], sm[:, 128:144]
        self.gsum, self.gexp, self.gnm, self.gtot = sm[:, 144:147], sm[:, 148:151], sm[:, 152:153], sm[:, 153:154]
        self.grec = sm[:, 154:155]
        self.cnt = sm[:, 160:192].rearrange("p (t n) -> p t n", t=NT)
        self.earlier = m.obuf[:, T:T + NT * NT].rearrange("p (a b) -> p a b", a=NT)
        self.xh, self.xl = m.qa[:, HP, :], m.qa[:, HP + 1, :]
        self.onehot = m.q1a[:, HP:HG, :].rearrange("p h (t n) -> p (h t) n", n=KEEP)
        self.rank, self.kept, self.far, self.pos = sm[:, 192:200], sm[:, 200:208], sm[:, 208:216], sm[:, 216:224]
        self.k1tok = m.obuf[:, 0:T].rearrange("p (t n) -> p t n", t=NT)
        self.cqn = m.obuf[:, T:T + NT * QR].rearrange("p (t n) -> p t n", t=NT)
        self.tmp = m.obuf[:, 2 * T:2 * T + NT * QR].rearrange("p (t n) -> p t n", t=NT)
        self.ro = m.tokf[:, 0:6 * P].rearrange("p (k t n) -> p k t n", k=6, t=NT)
        self.junk = [m.tokf[:, k * T:(k + 1) * T] for k in range(2)]
        self.score = m.tokf[:, 2 * T:3 * T]
        self.spread = m.tokf[:, 3 * T:4 * T].rearrange("p (t n) -> p t n", t=NT)


EARLY_SEMS = ("gate_sum gate_diff gate_exp ssq_done rms_done chain cqn_done k1_done cq_turned k1_turned cq_copied "
              "k1_copied xn_hi xn_lo spread_done turned score_done kept_done pos_summed onehot_done gathered selT_done ")


def early_tensor(pe, m, s, name):
    e, ps = m.early, m.ps
    if name == "squares":
        for t in range(NT):
            mm = pe.matmul(ps[:, 0, 0:3], m.ones[:], e.gate[:, t], start=(t == 0), stop=(t == NT - 1))
        mm.then_inc(s["gate_sum"], 1)
    elif name == "latents":
        pe.wait_ge(s["cqn_done"], 1)
        pe.wait_ge(s["gate_diff"], 1)
        for t in range(NT):
            mm = pe.transpose(ps[0:QR, t // 4, (t % 4) * P:(t % 4 + 1) * P], e.cqn[:, t, :], m.ident[:])
        mm.then_inc(s["cq_turned"], 1)
    elif name == "key":
        pe.wait_ge(s["k1_done"], 1)
        pe.wait_ge(s["score_done"], 2)
        for t in range(NT):
            mm = pe.transpose(ps[:, 2 + t // 4, (t % 4) * P:(t % 4 + 1) * P], e.k1tok[:, t, :], m.ident[:])
        mm.then_inc(s["k1_turned"], 1)
    elif name == "spread":
        pe.wait_ge(s["spread_done"], 1)
        for t in range(NT):
            mm = pe.transpose(ps[:, 2 + t // 4, (t % 4) * P:(t % 4 + 1) * P], e.spread[:, t, :], m.ident[:])
        mm.then_inc(s["turned"], 1)
    elif name == "place":
        pe.wait_ge(s["kept_done"], 1)
        pe.wait_ge(s["k1_copied"], 2)
        pe.matmul(ps[:, 2, 0:NT], m.before[:], e.kept, start=True, stop=True)
        pe.matmul(ps[:, 2, NT:2 * NT], m.ones[:], e.kept, start=True, stop=True).then_inc(s["pos_summed"], 1)
    elif name == "gather":
        pe.wait_ge(s["onehot_done"], NT)
        pe.wait_ge(s["xn_lo"], 1)
        for t in range(NT):
            for k, x in enumerate((e.xh, e.xl)):
                mm = pe.matmul(ps[:, 3, 0:KEEP], x[:, t * P:(t + 1) * P],
                               e.onehot[:, t, :], start=(t == 0 and k == 0),
                               stop=(t == NT - 1 and k == 1))
        mm.then_inc(s["gathered"], 1)


def early_scalar(act, m, s, name):
    e, ps = m.early, m.ps
    if name == "squares":
        act.wait_ge(s["ssq_done"], 2)
        act.activation(e.rms[:, 0:NT], e.ssq[:, 0:NT], ACT.Sqrt, bias=m.eps[:, 1:2], scale=1.0 / QR)\
            .then_inc(s["rms_done"], 1)
        act.activation(e.rms[:, NT:2 * NT], e.ssq[:, NT:2 * NT], ACT.Sqrt, bias=m.eps[:, 1:2], scale=1.0 / KVR)\
            .then_inc(s["rms_done"], 1)
        act.wait_ge(s["gate_diff"], 1)
        act.activation(e.gexp, e.gsum, ACT.Exp, scale=1.0 / T).then_inc(s["gate_exp"], 1)
    elif name == "latents":
        act.wait_ge(s["cq_turned"], 1)
        for k in range(2):
            act.copy(m.cqT[0:QR, k * CH:(k + 1) * CH], ps[0:QR, k, :]).then_inc(s["cq_copied"], 1)
    elif name == "key":
        act.wait_ge(s["k1_turned"], 1)
        for k in range(2):
            kk = slice(k * CH, (k + 1) * CH)
            act.copy(m.k1a[0:HD, kk], ps[0:HD, 2 + k, :])
            act.copy(m.k1a[HD:P, kk], ps[0:HD, 2 + k, :])
            act.copy(m.k1b[0:HD, kk], ps[HD:P, 2 + k, :]).then_inc(s["k1_copied"], 1)
    elif name == "spread":
        act.copy(e.xh, e.xn).then_inc(s["xn_hi"], 1)
        act.wait_ge(s["turned"], 1)
        for k in range(2):
            act.copy(e.score[:, k * CH:(k + 1) * CH], ps[:, 2 + k, :]).then_inc(s["score_done"], 1)
    elif name == "gather":
        act.wait_ge(s["gathered"], 1)
        act.copy(m.selT[:], ps[:, 3, 0:KEEP]).then_inc(s["selT_done"], 1)


def early_vector(dve, m, s, run, name, t):
    e, ps = m.early, m.ps
    if name == "squares":
        run(dve.tensor_tensor(e.tmp, e.cq, e.cq, ALU.mult))
        dve.tensor_reduce(e.ssq[:, 0:NT], e.tmp, AX, ALU.add).then_inc(s["ssq_done"], 1)
        dve.wait_ge(s["ssq_done"], 1)
        run(dve.tensor_tensor(e.tmp[:, :, 0:KVR], e.ckv, e.ckv, ALU.mult))
        dve.tensor_reduce(e.ssq[:, NT:2 * NT], e.tmp[:, :, 0:KVR], AX, ALU.add).then_inc(s["ssq_done"], 1)
        dve.tensor_copy(e.spread, e.imp.unsqueeze(2).to_broadcast([P, NT, P])).then_inc(s["spread_done"], 1)
        dve.wait_ge(s["gate_sum"], 1)
        run(dve.tensor_reduce(e.gnm, ps[:, 0, 0:3], AX, ALU.max, negate=True))
        dve.tensor_scalar(e.gsum, ps[:, 0, 0:3], e.gnm, None, ALU.add).then_inc(s["gate_diff"], 1)
    elif name == "latents":
        dve.wait_ge(s["rms_done"], 2)
        run(dve.reciprocal(e.rrms, e.rms))
        run(dve.tensor_tensor(e.cqn, e.cq, each_tile(e.rrms[:, 0:NT], QR), ALU.mult))
        dve.tensor_tensor(e.cqn, e.cqn, each_token(m.qnw[:], NT), ALU.mult).then_inc(s["cqn_done"], 1)
    elif name == "key":
        run(dve.tensor_tensor(m.v1[:], e.ckv, each_tile(e.rrms[:, NT:2 * NT], KVR), ALU.mult))
        dve.tensor_tensor(m.v1[:], m.v1[:], each_token(m.kvnw[:], NT), ALU.mult)
        run(dve.tensor_scalar(e.kr, e.kr, 1.0 / NH, None, ALU.mult))
        ro = e.ro
        xr, xi = e.kr[:, :, 0:HALF], e.kr[:, :, HALF:2 * HALF]
        dve.tensor_tensor(ro[:, 0], xr, m.cos[:], ALU.mult)
        dve.tensor_tensor(ro[:, 1], xi, m.sin[:], ALU.mult)
        dve.tensor_tensor(ro[:, 2], xr, m.sin[:], ALU.mult)
        run(dve.tensor_tensor(ro[:, 3], xi, m.cos[:], ALU.mult))
        dve.tensor_tensor(ro[:, 4], ro[:, 0], ro[:, 1], ALU.subtract)
        run(dve.tensor_tensor(ro[:, 5], ro[:, 2], ro[:, 3], ALU.add))
        pieces = ((0, KVR, m.v1[:]), (NOPE, HALF, ro[:, 4]), (NOPE + HALF, HALF, ro[:, 5]))
        for at, n, src in pieces:
            ins = dve.tensor_copy(e.k1tok[:, :, at:at + n].bitcast(F32R), src)
        run(ins)
        for at, n, src in pieces:
            ins = dve.tensor_tensor(e.k1tok[:, :, HD + at:HD + at + n].bitcast(F32R), src, e.k1tok[:, :, at:at + n],
                                    ALU.subtract)
        ins.then_inc(s["k1_done"], 1)
        dve.wait_ge(s["gate_exp"], 1)
        run(dve.tensor_reduce(e.gtot, e.gexp, AX, ALU.add))
        run(dve.reciprocal(e.grec, e.gtot))
        run(dve.tensor_scalar(m.gates[:], e.gexp, e.grec, None, ALU.mult))
        run(dve.memset(e.cnt, 0.0))
    elif name == "count":
        if t == 0:
            dve.wait_ge(s["score_done"], 2)
            dve.wait_ge(s["k1_done"], 1)
        own, junk = e.imp[:, t:t + 1], e.junk[t % 2]
        lo, hi = t * P, (t + 1) * P
        if t > 0:
            dve.tensor_scalar(junk[:, 0:lo], e.score[:, 0:lo], own, None, ALU.is_ge, ALU.add,
                              accum_out=e.cnt[:, t, 0:1])
        if t < NT - 1:
            dve.tensor_scalar(junk[:, hi:T], e.score[:, hi:T], own, None, ALU.is_gt, ALU.add,
                              accum_out=e.cnt[:, t, 1:2])
        dve.scalar_tensor_tensor(out=e.spread[:, t, :], in0=e.score[:, lo:hi], scalar=own, in1=m.below[:],
                                 op0=ALU.is_equal, op1=ALU.mult, accum_out=e.cnt[:, t, 3:4])
        run(dve.tensor_scalar(junk[:, lo:hi], e.score[:, lo:hi], own, None, ALU.is_gt, ALU.add,
                              accum_out=e.cnt[:, t, 2:3]))
    elif name == "place":
        run(dve.tensor_reduce(e.rank, e.cnt, AX, ALU.add))
        dve.tensor_scalar(e.kept, e.rank, float(KEEP), None, ALU.is_lt).then_inc(s["kept_done"], 1)
        dve.wait_ge(s["kept_done"], 1)
        run(dve.tensor_scalar(e.far, e.kept, -4.0 * T, 4.0 * T, ALU.mult, ALU.add))
    elif name == "gather":
        dve.wait_ge(s["pos_summed"], 1)
        totals = ps[:, 2, NT:2 * NT].unsqueeze(1).to_broadcast([P, NT, NT])
        run(dve.tensor_tensor(e.earlier, totals, m.earlier[:], ALU.mult))
        run(dve.tensor_reduce(e.pos, e.earlier, AX, ALU.add))
        run(dve.tensor_tensor(e.pos, e.pos, e.far, ALU.add))
        run(dve.tensor_tensor(e.pos, ps[:, 2, 0:NT], e.pos, ALU.add))
        for t in range(NT):
            dve.tensor_scalar(e.onehot[:, t, :], m.iota[:], e.pos[:, t:t + 1], None, ALU.is_equal)\
                .then_inc(s["onehot_done"], 1)


def first_preparation():
    own = [x for x in preparation(0) if x[0] not in ("s",) and x[2] != "s" and x[0] != "turn_s"]
    early = lambda name, t=0: ("early", 0, name, t)
    todo = [early("squares"), early("spread")] + [x for x in own if x[0] == "k"]
    todo += [early("latents")] + [x for x in own if x[0] == "q"] + [("rotate", 0, "q"), early("key")]
    counts = [early("count", t) for t in range(NT)]
    todo += counts[:4] + [("split", 0, "q1"), ("rotate", 0, "k")] + counts[4:6]
    rest = [x for x in own if x[0] not in ("k", "q", "rotate") and x != ("split", 0, "q1")]
    at_rows = rest.index(("rows", 0, 0))
    first, max1, max2 = rest[:at_rows], [x for x in rest if x[0] == "max1"], [x for x in rest if x[0] == "max2"]
    turned = max(k for k, x in enumerate(first) if x[0] == "turn_k")
    for k, x in enumerate(first):
        todo.append(x)
        if k in (6, 9):
            todo.append(counts[k // 3 + 4])
        if k == 12:
            todo.append(early("place"))
        if k == turned:
            todo.append(early("gather"))
    todo += [("s", 0, t) for t in range(KEEP // P)] + [("rotate", 0, "s"), ("rows", 0, 0)]
    todo += max2[:2] + [("split", 0, "s")] + max2[2:5] + [("turn_s", 0, 0)] + max2[5:]
    return todo + max1[:3] + [("rows", 0, 2)] + max1[3:] + [("rows", 0, 1)]


def units():
    found = []
    for br, c in SUMS:
        for j in range(KEEP // P if br == 1 else NT):
            q0, q1 = c * CH, (c + 1) * CH
            if br != 1:
                q0 = max(q0, j * P)
            if br == 2:
                q1 = min(q1, j * P + WN)
            if q0 < q1:
                found.append((br, c, j, q0, q1 - q0))
    return found


SUMS = [(0, 0), (1, 0), (2, 0), (1, 1), (2, 1), (0, 1)]
UNITS = units()
LAST = [max(u for u, x in enumerate(UNITS) if x[:2] == k) for k in SUMS]


def interleave(exact, prepare, keep, delay):
    spread, kept = prepare[:len(prepare) - keep], prepare[len(prepare) - keep:]
    ends = max(k for k, x in enumerate(exact) if x[0] == "sum") + 1
    units_of = [x for x in exact if x[0] in ("scores", "products") and x[2] >= delay]
    total = sum(UNITS[x[2]][4] for x in units_of)
    todo, seen, at = [], 0, 0
    for x in exact[:ends]:
        todo.append(x)
        if x in units_of:
            seen += UNITS[x[2]][4]
            n = len(spread) * seen // total
            todo += spread[at:n]
            at = n
    todo += spread[at:]
    for k, x in enumerate(exact[ends:]):
        todo += kept[2 * k:2 * k + 2] + [x]
    return todo + kept[2 * len(exact[ends:]):]


def preparation(side):
    turn = {name: [("turn_" + name, side, h, k) for h in range(HP) for k in range(2)] for name in ("q1", "q", "k")}
    max0 = [("max0", side, h, i, part) for h in range(HP) for i in range(NT) for part in range(1 + (i >= NT // 2))]
    max1, max2 = [[(kind, side, h, k) for h in range(HP) for k in range(NT // 2)] for kind in ("max1", "max2")]
    todo = [("q", side, t) for t in range(NT)] + [("rotate", side, "q")]
    todo += [("k", side, t) for t in range(NT // 2)] + [("split", side, "q1")]
    todo += [("k", side, t) for t in range(NT // 2, NT)] + [("rotate", side, "k")]
    todo += [("s", side, t) for t in range(KEEP // P)] + [("rotate", side, "s")]
    todo += turn["q1"]
    todo += max0[:2] + [("split", side, "q")] + max0[2:6] + weave(max0[6:10], turn["q"]) + [("split", side, "k")]
    todo += max0[10:15] + weave(max0[15:19], turn["k"]) + [("split", side, "s")] + max0[19:] + [("whole", side, 0)]
    todo += max2[:2] + [("turn_s", side, 0), ("rows", side, 0)] + max2[2:]
    todo += max1[:3] + [("rows", side, 2)] + max1[3:] + [("rows", side, 1)]
    return todo


def weave(a, b):
    return [x for pair in zip(a, b) for x in pair]


def exact_pass(side):
    todo, pieces = [], []
    for u in range(len(UNITS) + 1):
        if u < len(UNITS):
            todo.append(("scores", side, u))
        if u > 0:
            todo.append(("products", side, u - 1))
            if u - 1 in LAST:
                k = LAST.index(u - 1)
                todo.append(("sum", side, k))
                if side == 1:
                    pieces += [("divide", side, k, piece) for piece in range(PIECES)]
                    if k == len(SUMS) - 1:
                        todo.append(("proj", side, 0))
            todo += pieces[:1]
            pieces = pieces[1:]
    return todo + pieces


SCORES = 3
PIECES = 2
PROBS = 3
BY_ACT = ("q", "k", "s", "turn_q1", "turn_q", "turn_k", "turn_s")
BEFORE = {"q1": "turn_s", "q": "turn_q1", "k": "turn_q", "s": "turn_k"}


class Plan:

    def __init__(self, steps, spares):
        self.steps = steps
        self.spares = spares
        self.fills = self.of(BY_ACT + ("max0", "max1", "max2", "rows", "proj"))

    def of(self, kinds):
        return [x for x in self.steps if x[0] in kinds]

    def has(self, kind, side):
        return any(x[0] == kind and x[1] == side for x in self.steps)

    def emptied(self, n, act):
        return sum((x[0] in BY_ACT) == act for x in self.fills[:n])

    def up_to(self, kind, side):
        return max(n for n, x in enumerate(self.fills) if x[0] == kind and x[1] == side) + 1

    def by_act(self, kind, side):
        return self.emptied(self.up_to(kind, side), True)

    def by_dve(self, kind, side):
        return self.emptied(self.up_to(kind, side), False)

    def count(self, *step):
        return self.of((step[0],)).index(step) + 1


KEPT = 1
PREPARE = Plan(first_preparation(), 4)


def left_over(exact):
    todo = [("divide", 2, len(SUMS) - 1, piece) for piece in range(PIECES)] + [("proj", 2, 1)]
    found = []
    for x in exact:
        found.append(x)
        if x[0] == "products" and todo:
            found.append(todo.pop(0))
    return found


FIRST, SECOND = exact_pass(0), exact_pass(1)
CUT = [x for x in SECOND if x[:3] != ("divide", 1, len(SUMS) - 1)]
FIRST_GROUP = Plan(interleave(FIRST, preparation(1), 0, 1) + interleave(CUT, preparation(0), KEPT, 0), 3)
GROUP = Plan(interleave(left_over(FIRST), preparation(1), 0, 1) + interleave(CUT, preparation(0), KEPT, 0), 3)
LAST_GROUP = Plan(interleave(left_over(FIRST), preparation(1), 0, 1) + SECOND + [("proj", 1, 1)], 3)


def turns(nc, m, plan, g, ends=None):
    ps, d = m.ps, m.d
    raw = {"q": m.rawq, "q1": m.rawq, "k": m.rawk, "s": m.raws}
    sides = [x for x in (1, 0) if plan.has("q", x)]
    stack = ExitStack()
    s = open_sems(nc, stack, "x_loaded stored q_loaded k_loaded s_loaded proj_loaded fill_ready emptied_act emptied_dve rotation hi_done split_done "
                             "q_rows1 q_rows k_twice s_twice max_rows scores_ready exp_done products_done "
                             "banks_free inverse_done divided o_done max_done " + (EARLY_SEMS if plan is PREPARE else ""))
    neg = m.small
    negs = [neg[:, 256 + k * HP * NT:256 + (k + 1) * HP * NT] for k in range(3)]
    partial = neg[:, 352:352 + HP * NT * 2].rearrange("p (h t a) -> p h t a", h=HP, t=NT)

    def heads(side, h=None):
        return slice(HP * side, HP * side + HP) if h is None else HP * side + h

    def spare(n):
        return ps[:, 8 - plan.spares + n % plan.spares, :]

    def weights(w, side):
        return w[:, 1 - side, :]

    with nc.Block() as block:
        @block.sync
        def _(sp):
            sp.dma_start(m.wq_g[0:QR, :, 0:NW + 2 * RW], d["wq"][g]).then_inc(s["q_loaded"], 16)
            sp.dma_start(m.wq_g[0:QR, :, NW + 2 * RW:], d["wqp"][:, g].rearrange("q (s n) -> q s n", s=2))\
                .then_inc(s["q_loaded"], 16)
            sp.dma_start(m.wk_g[:], d["wk"][g]).then_inc(s["k_loaded"], 16)
            sp.dma_start(m.ws_g[:], d["ws"][g]).then_inc(s["s_loaded"], 16)
            if plan.has("proj", 2):
                sp.wait_ge(s["fill_ready"], plan.up_to("proj", 2))
            sp.dma_start(m.wproj_g[:], d["wproj_g"][g]).then_inc(s["proj_loaded"], 16)
            sp.dma_start(m.wvp_g[:], d["wvp"][g]).then_inc(s["proj_loaded"], 16)
            if plan is PREPARE:
                sp.wait_ge(s["proj_loaded"], 32)
            for nth, side in enumerate(sides):
                hh = heads(side)
                sp.wait_ge(s["emptied_act"], plan.by_act("turn_q1", side))
                sp.dma_start(m.q1b[0:HD, hh].bitcast(F32), m.q1a[0:HD, hh].bitcast(F32)).then_inc(s["q_rows1"], 16)
                sp.wait_ge(s["emptied_act"], plan.by_act("turn_q", side))
                sp.dma_start(m.qb[0:HD, hh].bitcast(F32), m.qa[0:HD, hh].bitcast(F32)).then_inc(s["q_rows"], 16)
                sp.wait_ge(s["emptied_act"], plan.by_act("turn_k", side))
                sp.dma_start(m.kwa[HD:P, hh].bitcast(F32), m.kwa[0:HD, hh].bitcast(F32)).then_inc(s["k_twice"], 16)
                sp.wait_ge(s["emptied_dve"], plan.emptied(plan.fills.index(("rows", side, 0)) + 1, False))
                if nth > 0:
                    sp.wait_ge(s["max_rows"], 48 * nth)
                sp.dma_start(m.q1b[64:65, hh].rearrange("p h n -> p (h n)").bitcast(F32), m.mrows[3 * nth % 2])\
                    .then_inc(s["max_rows"], 16)
                sp.wait_ge(s["emptied_act"], plan.by_act("turn_s", side))
                sp.dma_start(m.ksa[HD:P, hh].bitcast(F32), m.ksa[0:HD, hh].bitcast(F32)).then_inc(s["s_twice"], 16)
                for br in (2, 1):
                    sp.wait_ge(s["emptied_dve"], plan.emptied(plan.fills.index(("rows", side, br)) + 1, False))
                    sp.wait_ge(s["max_rows"], 16 * (3 * nth + 3 - br))
                    sp.dma_start(m.qb[63 + br:64 + br, hh].rearrange("p h n -> p (h n)").bitcast(F32), m.mrows[(3 * nth + 3 - br) % 2])\
                        .then_inc(s["max_rows"], 16)
            sp.wait_ge(s["max_rows"], 48 * len(sides))
            if ends:
                sp.wait_ge(s["split_done"], len(plan.of(("split",))))
                sp.dma_start(m.x, ends[1]).then_inc(s["x_loaded"], 16)
                for c in range(NC):
                    done = plan.emptied(plan.fills.index(("proj", 1, c)) + 1, False)
                    cc = slice(c * CH, (c + 1) * CH)
                    sp.wait_ge(s["emptied_dve"], done)
                    sp.dma_start(ends[0][:, cc], m.t2[:, cc]).then_inc(s["stored"], 16)
                sp.wait_ge(s["x_loaded"], 16)
                sp.wait_ge(s["stored"], 16 * NC)

        @block.tensor
        def _(pe):
            waited = set()

            def once(name, count):
                if (name, count) not in waited:
                    waited.add((name, count))
                    pe.wait_ge(s[name], count)

            def fill(n, kind, side, *a):
                if n >= plan.spares:
                    old = n - plan.spares
                    by_act = plan.fills[old][0] in BY_ACT
                    pe.wait_ge(s["emptied_act" if by_act else "emptied_dve"], plan.emptied(old + 1, by_act))
                bank = spare(n)
                nth = sides.index(side) + 1 if side in sides else 0
                if plan is PREPARE:
                    if kind == "q":
                        once("cq_copied", 2)
                    elif kind == "s":
                        once("selT_done", 1)
                    elif kind == "max0":
                        once("k1_copied", 2)
                if kind in ("q", "k", "s"):
                    once(kind + "_loaded", 32 if kind == "q" else 16)
                    x, w = {"q": (m.cqT, m.wq_g), "k": (m.xnT, m.wk_g), "s": (m.selT, m.ws_g)}[kind]
                    mm = pe.matmul(bank[:, 0:2 * NW + 2 * RW], x[:, a[0] * P:(a[0] + 1) * P], weights(w, side),
                                   start=True, stop=True)
                elif kind in ("turn_q1", "turn_q", "turn_k"):
                    h, k = a
                    once("split_done", plan.count("split", side, kind[5:]))
                    for i in range(4):
                        mm = pe.transpose(bank[:, i * P:(i + 1) * P], m.tok[:, 4 * k + i, h, :], m.ident[:])
                elif kind == "turn_s":
                    once("split_done", plan.count("split", side, "s"))
                    for i in range(4):
                        mm = pe.transpose(bank[:, i * P:(i + 1) * P], m.tok[:, i % 2, i // 2, :], m.ident[:])
                elif kind == "max0":
                    h, i, part = a
                    once("emptied_act", plan.by_act("turn_q1", side))
                    k0, k1 = part * CH, min((part + 1) * CH, (i + 1) * P)
                    mm = pe.matmul(bank[:, 0:k1 - k0], m.q1a[:, heads(side, h), i * P:(i + 1) * P],
                                   m.k1a[:, k0:k1], start=True, stop=True)
                    if k1 == (i + 1) * P:
                        mm = pe.matmul(bank[:, k1 - k0 - P:k1 - k0], m.ident_bf[:], m.causal_q[:],
                                       start=False, stop=True, skip_group_check=True)
                elif kind == "max1":
                    h, k = a
                    once("s_twice", 16 * nth)
                    for i in range(2):
                        t = 2 * k + i
                        mm = pe.matmul(bank[:, i * KEEP:(i + 1) * KEEP], m.qa[:, heads(side, h), t * P:(t + 1) * P],
                                       m.ksa[:, heads(side, h), :], start=True, stop=True)
                elif kind == "max2":
                    h, k = a
                    once("k_twice", 16 * nth)
                    once("emptied_act", plan.by_act("turn_q", side))
                    for i in range(2):
                        t = 2 * k + i
                        k0 = max(0, t * P - WINDOW)
                        pe.matmul(bank[:, i * KEEP:i * KEEP + WN], m.qa[:, heads(side, h), t * P:(t + 1) * P],
                                  m.kwa[:, heads(side, h), k0:k0 + WN], start=True, stop=True, skip_group_check=True)
                        mm = pe.matmul(bank[:, i * KEEP:i * KEEP + WN], m.ident_bf[:],
                                       m.window_q0[:] if t == 0 else m.window_q[:], start=False, stop=True,
                                       skip_group_check=True)
                elif kind == "rows":
                    if a[0] == 0:
                        pe.wait_ge(s["max_done"], nth)
                    else:
                        pe.wait_ge(s["emptied_dve"], plan.by_dve(("max1", "max2")[a[0] - 1], side))
                    mm = pe.transpose(bank[0:HP * NT, 0:P], negs[a[0]], m.ident[:])
                elif kind == "proj":
                    cc = slice(a[0] * CH, (a[0] + 1) * CH)
                    pe.wait_ge(s["divided"], plan.count("divide", side, SUMS.index((0, a[0])), PIECES - 1))
                    if side == 1:
                        pe.wait_ge(s["o_done"], PIECES * (a[0] + 1))
                        once("proj_loaded", 32)
                    pe.matmul(bank, m.wvp_g[:], m.products[:, 0, cc], start=True, stop=False)
                    mm = pe.matmul(bank, m.wproj_g[:], m.products[:, 1, cc], start=False, stop=True)
                mm.then_inc(s["fill_ready"], 1)

            def scores(side, u):
                br, c, j, q0, w = UNITS[u]
                if side == 1:
                    if br == 0:
                        once("q_rows1", 16)
                        once("max_rows", 16)
                    else:
                        once("q_rows", 16)
                        once("max_rows", 48)
                qx, qy = (m.q1a, m.q1b) if br == 0 else (m.qa, m.qb)
                n = side * len(UNITS) + u
                jj = slice(j * P, (j + 1) * P)
                for h in range(HP):
                    hh = heads(side, h)
                    if br == 0:
                        kx, ky = m.k1a[:, jj], m.k1b[:, jj]
                    elif br == 1:
                        kx, ky = m.ksa[:, hh, jj], m.ksb[:, hh, jj]
                    else:
                        kx, ky = m.kwa[:, hh, jj], m.kwb[:, hh, jj]
                    turn = HP * n + h
                    if turn >= SCORES:
                        pe.wait_ge(s["exp_done"], turn - SCORES + 1)
                    bank = ps[:, turn % SCORES, 0:w]
                    pe.matmul(bank, kx, qx[:, hh, q0:q0 + w], start=True, stop=False, skip_group_check=True)
                    at = q0 - j * P
                    if br == 0 and at == 0:
                        pe.matmul(bank[:, 0:P], m.ident_bf[:], m.causal_k[:], start=False, stop=False,
                                  skip_group_check=True)
                    if br == 2:
                        pe.matmul(bank, m.ident_bf[:], m.window_k[:, at:at + w], start=False, stop=False,
                                  skip_group_check=True)
                    pe.matmul(bank, ky, qy[:, hh, q0:q0 + w], start=False, stop=True, skip_group_check=True)\
                        .then_inc(s["scores_ready"], 1)

            def products(side, u):
                br, c, j, q0, w = UNITS[u]
                n = side * len(UNITS) + u
                k = side * len(SUMS) + SUMS.index((br, c))
                first = u == 0 or u - 1 in LAST
                pe.wait_ge(s["exp_done"], HP * (n + 1))
                if first and k >= 2:
                    pe.wait_ge(s["banks_free"], k - 1)
                for plain in range(2):
                    for h in range(HP):
                        vv = slice(h * VD, (h + 1) * VD)
                        w_ = m.ones[:, 0:VD] if plain else m.v1[:, j, :] if br == 0 else \
                            m.vs[:, side, j, vv] if br == 1 else m.vw[:, side, j, vv]
                        at = (plain * HP + h) * VD
                        mm = pe.matmul(ps[at:at + VD, SCORES + k % 2, q0 - c * CH:q0 - c * CH + w], w_,
                                       m.prob[:, n % PROBS, h, 0:w], start=first, stop=True, skip_group_check=True)
                mm.then_inc(s["products_done"], 1)

            n = 0
            for step in plan.steps:
                if step[0] == "early":
                    early_tensor(pe, m, s, step[2])
                if step[0] == "scores":
                    scores(*step[1:])
                elif step[0] == "products":
                    products(*step[1:])
                elif step in plan.fills:
                    fill(n, *step)
                    n += 1

        @block.scalar
        def _(act):
            n = 0
            for step in plan.steps:
                kind, side = step[:2]
                if kind == "early":
                    early_scalar(act, m, s, step[2])
                if kind == "scores":
                    w = UNITS[step[2]][4]
                    u = side * len(UNITS) + step[2]
                    if u >= PROBS:
                        act.wait_ge(s["products_done"], u - PROBS + 1)
                    for h in range(HP):
                        turn = HP * u + h
                        act.wait_ge(s["scores_ready"], turn + 1)
                        act.activation(m.prob[:, u % PROBS, h, 0:w], ps[:, turn % SCORES, 0:w], ACT.Exp,
                                       scale=SCALE).then_inc(s["exp_done"], 1)
                if kind == "sum":
                    br, c = SUMS[step[2]]
                    k = side * len(SUMS) + step[2]
                    cc, rows = slice(c * CH, (c + 1) * CH), slice(NW * side, NW * side + NW)
                    act.wait_ge(s["products_done"], side * len(UNITS) + LAST[step[2]] + 1)
                    act.activation(m.products[rows, br, cc], ps[0:NW, SCORES + k % 2, :], ACT.Copy,
                                   scale=m.gates[0:NW, br:br + 1])
                    act.copy(m.sums[rows, br, cc], ps[NW:P, SCORES + k % 2, :]).then_inc(s["banks_free"], 1)
                if step not in plan.fills:
                    continue
                n += 1
                if kind not in BY_ACT:
                    continue
                act.wait_ge(s["fill_ready"], n)
                if kind in ("q", "k", "s") and step[2] == 0 and side != sides[0]:
                    act.wait_ge(s["split_done"], plan.count("split", sides[0], kind))
                bank = spare(n - 1)
                if kind == "q":
                    ins = act.copy(m.rawq[:, step[2], :], bank[:, 0:2 * NW + 2 * RW])
                elif kind in ("k", "s"):
                    r, v = (m.rawk, m.vw) if kind == "k" else (m.raws, m.vs)
                    act.copy(r[:, step[2], :], bank[:, 0:NW + 2 * RW])
                    ins = act.copy(v[:, side, step[2], :], bank[:, NW + 2 * RW:2 * NW + 2 * RW])
                elif kind in ("turn_q1", "turn_q"):
                    _, _, h, k = step
                    dst = m.q1a if kind == "turn_q1" else m.qa
                    ins = act.copy(dst[:, heads(side, h), k * CH:(k + 1) * CH], bank)
                elif kind == "turn_k":
                    _, _, h, k = step
                    kk = slice(k * CH, (k + 1) * CH)
                    act.copy(m.kwa[0:HD, heads(side, h), kk], bank[0:HD, :])
                    ins = act.copy(m.kwb[0:HD, heads(side, h), kk], bank[HD:P, :])
                elif kind == "turn_s":
                    act.copy(m.ksa[0:HD, heads(side), :], bank[0:HD, :].rearrange("p (h n) -> p h n", h=HP))
                    ins = act.copy(m.ksb[0:HD, heads(side), :], bank[HD:P, :].rearrange("p (h n) -> p h n", h=HP))
                ins.then_inc(s["emptied_act"], 1)

        @block.gpsimd
        def _(pool):
            run = in_order(pool, s["rotation"])
            for step in plan.steps:
                if step == ("early", 0, "place", 0):
                    pool.wait_ge(s["xn_hi"], 1)
                    pool.tensor_tensor(m.early.xl, m.early.xn, m.early.xh.bitcast(F32), ALU.subtract)\
                        .then_inc(s["xn_lo"], 1)
                if step[0] == "rotate":
                    _, side, name = step
                    pool.wait_ge(s["emptied_act"], plan.by_act(name, side))
                    r = raw[name]
                    nt = r.shape[1]
                    xr, xi = [r[:, :, NW + k * RW:NW + (k + 1) * RW].rearrange("p t (h n) -> p t h n", h=HP)
                              for k in range(2)]
                    co, si = [x[:, 0:nt, :].unsqueeze(2).to_broadcast([P, nt, HP, HALF]) for x in (m.cos, m.sin)]
                    ta, tb, tc = [x[:, 0:nt * RW].rearrange("p (t h n) -> p t h n", t=nt, h=HP)
                                  for x in m.rope_tmp]
                    pool.tensor_tensor(ta, xr, co, ALU.mult)
                    pool.tensor_tensor(tb, xi, si, ALU.mult)
                    run(pool.tensor_tensor(tc, xr, si, ALU.mult))
                    run(pool.tensor_tensor(xr, ta, tb, ALU.subtract))
                    run(pool.tensor_tensor(ta, xi, co, ALU.mult))
                    run(pool.tensor_tensor(xi, tc, ta, ALU.add))
                elif step[0] == "divide":
                    _, _, k, piece = step
                    br, c = SUMS[k]
                    w = CH // PIECES
                    cc = slice(c * CH + piece * w, c * CH + (piece + 1) * w)
                    nth = plan.count(*step)
                    o = m.products[:, br, cc]
                    pool.wait_ge(s["inverse_done"], nth)
                    pool.tensor_tensor(o, o, m.sums[:, br, cc], ALU.mult).then_inc(s["divided"], 1)
                    if br == 2:
                        pool.wait_ge(s["divided"], nth)
                        pool.tensor_tensor(m.products[:, 1, cc], m.products[:, 1, cc], o, ALU.add)\
                            .then_inc(s["o_done"], 1)
                elif step[0] == "split":
                    _, side, name = step
                    pool.wait_ge(s["hi_done"], plan.count(*step))
                    for at, src in split_pieces(raw[name], name):
                        nt, w = src.shape[1], src.shape[3]
                        ins = pool.tensor_tensor(m.tok[:, 0:nt, :, HD + at:HD + at + w].bitcast(F32R), src,
                                                 m.tok[:, 0:nt, :, at:at + w], ALU.subtract)
                    ins.then_inc(s["split_done"], 1)

        @block.vector
        def _(dve):
            n = 0
            rows = 0
            run = in_order(dve, s["chain"]) if plan is PREPARE else None
            for step in plan.steps:
                kind, side = step[:2]
                if kind == "early":
                    early_vector(dve, m, s, run, *step[2:])
                elif kind == "split":
                    name = step[2]
                    if name != "q1":
                        dve.wait_ge(s["fill_ready"], plan.up_to(BEFORE[name], side))
                    elif side != sides[0]:
                        dve.wait_ge(s["fill_ready"], plan.up_to(BEFORE[name], sides[0]))
                    dve.wait_ge(s["rotation"], 4 * plan.count("rotate", side, "q" if name == "q1" else name))
                    for at, src in split_pieces(raw[name], name):
                        nt, w = src.shape[1], src.shape[3]
                        ins = dve.tensor_copy(m.tok[:, 0:nt, :, at:at + w].bitcast(F32R), src)
                    ins.then_inc(s["hi_done"], 1)
                elif kind == "whole":
                    dve.wait_ge(s["emptied_dve"], plan.by_dve("max0", side))
                    dve.tensor_reduce(negs[0], partial, AX, ALU.max, negate=True).then_inc(s["max_done"], 1)
                elif kind == "divide":
                    _, _, k, piece = step
                    br, c = SUMS[k]
                    w = CH // PIECES
                    total = m.sums[:, br, c * CH + piece * w:c * CH + (piece + 1) * w]
                    if side == 1:
                        dve.wait_ge(s["banks_free"], len(SUMS) + k + 1)
                    dve.reciprocal(total, total).then_inc(s["inverse_done"], 1)
                if step not in plan.fills:
                    continue
                n += 1
                if kind in BY_ACT:
                    continue
                bank = spare(n - 1)
                dve.wait_ge(s["fill_ready"], n)
                if kind == "max0":
                    _, _, h, i, part = step
                    w = min((part + 1) * CH, (i + 1) * P) - part * CH
                    ins = dve.tensor_reduce(partial[:, h, i, part:part + 1], bank[:, 0:w], AX, ALU.max)
                elif kind in ("max1", "max2"):
                    _, _, h, k = step
                    w = KEEP if kind == "max1" else WN
                    at = h * NT + 2 * k
                    ins = dve.tensor_reduce(negs[1 if kind == "max1" else 2][:, at:at + 2],
                                            bank.rearrange("p (i n) -> p i n", i=2)[:, :, 0:w], AX, ALU.max,
                                            negate=True)
                elif kind == "rows":
                    if rows >= 2:
                        dve.wait_ge(s["max_rows"], 16 * (rows - 1))
                    rows += 1
                    ins = dve.tensor_copy(m.mrows[(rows - 1) % 2].bitcast(F32R), bank[0:HP * NT, 0:P])
                else:
                    cc = slice(step[2] * CH, (step[2] + 1) * CH)
                    ins = dve.tensor_tensor(m.t2[:, cc], m.t2[:, cc], bank, ALU.add)
                ins.then_inc(s["emptied_dve"], 1)
    phase_end(nc, s)
    stack.close()


TILES = -(-NE * HID // P)
BEHIND = 3
RING = 4
GATE_LO = 32
WEIGHTS = ("w1", "w3", "w2", "owner")
STAGES = ("turn 0", "turn 1", "stats 0", "stats 1", "root", "normed 0", "normed 1", "turn back 0", "turn back 1",
          "logits", "shift", "softmax", "compared", "rank", "kept", "gates", "turn gates 0", "turn gates 1")


def ffn_steps(tiles, prepare):
    if not tiles:
        todo = list(STAGES)
        for name, stage in zip(WEIGHTS, ("stats 0", "turn back 0", "shift", "gates")):
            todo.insert(todo.index(stage), name)
        return todo
    first, apart = 2, 2
    todo = []
    for n in range(NC * TILES):
        todo.append(n)
        k, rest = divmod(n - first, apart)
        if prepare and n >= first and rest == 0 and k < len(STAGES):
            todo.append(STAGES[k])
        if n == TILES + BEHIND - 1:
            todo.append("result")
    return todo


def experts_part(nc, d, t2_dram, out, ps, ident, eps, sb):
    m = Mem()
    m.ps, m.d, m.ident, m.eps = ps, d, ident, eps
    m.w1 = [sb(n, [C, TILES * P], F32R) for n in ("w1h", "w1l")]
    m.w3 = [sb(n, [C, TILES * P], F32R) for n in ("w3h", "w3l")]
    m.w2 = [sb(n, [P, TILES * C], F32R) for n in ("w2h", "w2l")]
    m.owner = sb("owner", [P, TILES * P], F32R)
    m.router = sb("router", [C, NE])
    m.tie = sb("tie", [P, NE, NE])
    m.t2 = sb("t2b", [C, T])
    m.xh = sb("xh", [C, T], F32R)
    m.xl = sb("xl", [C, T], F32R)
    m.g = sb("g", [P, T], F32R)
    m.t2n = sb("t2n", [C, T])
    m.xhn = sb("xhn", [C, T], F32R)
    m.xln = sb("xln", [C, T], F32R)
    m.gn = sb("gn", [P, T], F32R)
    m.t_tok = sb("t_tok", [P, NT, P])
    m.xn = sb("xn", [P, NT, P])
    m.xf = sb("xf", [C, T])
    m.st = sb("st", [P, NT, 6])
    m.mv = sb("mv", [P, NT, 2])
    m.std, m.rstd, m.top, m.tot, m.inv = [sb(n, [P, NT]) for n in ("std", "rstd", "top", "tot", "inv")]
    m.pr, m.gt, m.rank = [sb(n, [P, NT, NE]) for n in ("pr", "gt", "rank")]
    m.more, m.same = [sb(n, [P, NT, NE * NE]) for n in ("more", "same")]
    m.act_s = sb("act_s", [P, 2, CH])
    m.mid = sb("mid", [P, 2, CH])
    m.res = sb("res", [C, 2, CH])
    with ExitStack() as stage_mem:
        stage = [stage_mem.enter_context(nc.sbuf_tensor(f"stage_{n}", [P, TILES * P], F32)) 
                 for n in ("w1", "w3", "w2", "owner")]
        experts_block(nc, m, None, t2_dram[0], stage=stage)
    m.hid = sb("hid", [P, RING, CH])
    m.hh = sb("hh", [P, RING, CH], F32R)
    m.hl = sb("hl", [P, RING, CH], F32R)
    with nc.Fori(0, B - 1) as b:
        experts_block(nc, m, (t2_dram[0:B - 1][b], out[0:B - 1][b]), t2_dram[1:B][b])
    experts_block(nc, m, (t2_dram[B - 1], out[B - 1]), None)


def experts_block(nc, m, batch, following, stage=None):
    ps, d = m.ps, m.d
    steps = ffn_steps(batch is not None, following is not None)
    weights = [m.w1, m.w3, m.w2]
    side = ps[:, 7, :]
    stack = ExitStack()
    s = open_sems(nc, stack, "side_ready side_read stream_loaded small_loaded w_loaded w_hi g_zeroed "
                             "next_loaded t_copied stats aggregated std_done xn_done xh_done shifted exp_done "
                             "chain gates_done gh_done h1_ready h3_ready g_ready silu_done mid_done hid_done "
                             "hi_done lo_done used res_done stored moved")

    def once_read(engine, fills):
        if fills:
            engine.wait_ge(s["side_read"], fills)

    HALVES = ("stats 0", "stats 1", "normed 0", "normed 1")
    FILLED = ("turn 0", "turn 1", "turn back 0", "turn back 1", "logits", "turn gates 0", "turn gates 1")
    READS = {"turn 0": 1, "turn 1": 1, "turn back 0": 2, "turn back 1": 2, "logits": 1, "turn gates 0": 1,
             "turn gates 1": 1}

    def reads_before(stage_):
        return sum(READS[x] for x in FILLED[:FILLED.index(stage_)])

    def filled(stage_):
        return FILLED.index(stage_) + 1

    with nc.Block() as block:
        @block.sync
        def _(sp):
            if following is not None:
                sp.dma_start(m.t2n[:], following).then_inc(s["next_loaded"], 16)
            if stage:
                for k, name in enumerate(WEIGHTS):
                    sp.dma_start(stage[k][:], d[name]).then_inc(s["w_loaded"], 16)
                    sp.wait_ge(s["w_loaded"], 16 * (k + 1))
                sp.dma_start(m.router[:], d["router"]).then_inc(s["small_loaded"], 16)
                sp.dma_start(m.tie[:], d["tie"]).then_inc(s["small_loaded"], 16)
                sp.wait_ge(s["small_loaded"], 32)
            if batch:
                sp.dma_start(m.t2[:], batch[0]).then_inc(s["stream_loaded"], 16)
                for c in range(NC):
                    sp.wait_ge(s["res_done"], c + 1)
                    sp.dma_start(batch[1][:, c * CH:(c + 1) * CH], m.res[:, c, :]).then_inc(s["stored"], 16)
                sp.wait_ge(s["stored"], 16 * NC)

        @block.tensor
        def _(pe):
            def three(bank, w, x, first=True, last=True):
                pe.matmul(bank, w[0], x[0], start=first, stop=False)
                pe.matmul(bank, w[0], x[1], start=False, stop=False)
                return pe.matmul(bank, w[1], x[0], start=False, stop=last)

            def hidden(n):
                c, k = divmod(n, TILES)
                kk, cc = slice(k * P, (k + 1) * P), slice(c * CH, (c + 1) * CH)
                if n >= 2:
                    pe.wait_ge(s["mid_done"], n - 1)
                x = (m.xh[:, cc], m.xl[:, cc])
                three(ps[:, n % 2, :], [w[:, kk] for w in m.w1], x).then_inc(s["h1_ready"], 1)
                three(ps[:, 2 + n % 2, :], [w[:, kk] for w in m.w3], x).then_inc(s["h3_ready"], 1)
                if n >= 2:
                    pe.wait_ge(s["hid_done"], n - 1)
                pe.matmul(ps[:, 4 + n % 2, :], m.owner[:, kk], m.g[:, cc], start=True, stop=True)\
                    .then_inc(s["g_ready"], 1)

            def output(n):
                c, k = divmod(n, TILES)
                if c > 0 and k == 0:
                    pe.wait_ge(s["res_done"], c)
                pe.wait_ge(s["hi_done"], n + 1)
                pe.wait_ge(s["lo_done"], n + 1)
                kk = slice(k * C, (k + 1) * C)
                three(ps[:, 6, :], [w[:, kk] for w in m.w2], (m.hh[:, n % RING, :], m.hl[:, n % RING, :]),
                      first=k == 0, last=k == TILES - 1).then_inc(s["used"], 1)

            for step in steps:
                if step in FILLED:
                    once_read(pe, reads_before(step))
                    k = int(step[-1]) if step[-1] in "01" else 0
                if step in ("turn 0", "turn 1"):
                    pe.wait_ge(s["next_loaded"], 16)
                    for i in range(4):
                        t = 4 * k + i
                        mm = pe.transpose(side[:, i * P:(i + 1) * P], m.t2n[:, t * P:(t + 1) * P], m.ident[:])
                elif step in ("turn back 0", "turn back 1"):
                    pe.wait_ge(s["xn_done"], 4 * (k + 1))
                    for i in range(4):
                        mm = pe.transpose(side[:, i * P:(i + 1) * P], m.xn[:, 4 * k + i, :], m.ident[:])
                elif step == "logits":
                    if stage:
                        pe.wait_ge(s["small_loaded"], 32)
                    for t in range(NT):
                        mm = pe.matmul(side[:, t * NE:(t + 1) * NE], m.xf[:, t * P:(t + 1) * P], m.router[:],
                                       start=True, stop=True)
                elif step in ("turn gates 0", "turn gates 1"):
                    pe.wait_ge(s["gates_done"], 1)
                    for i in range(4):
                        mm = pe.transpose(side[0:NE, i * P:(i + 1) * P], m.gt[:, 4 * k + i, :], m.ident[:])
                if step in FILLED:
                    mm.then_inc(s["side_ready"], 1)
                if isinstance(step, int):
                    hidden(step)
                    if step >= BEHIND:
                        output(step - BEHIND)
            if batch:
                for n in range(NC * TILES - BEHIND, NC * TILES):
                    output(n)

        @block.scalar
        def _(act):
            def split(n):
                if n >= RING:
                    act.wait_ge(s["used"], n - RING + 1)
                act.wait_ge(s["hid_done"], n + 1)
                act.copy(m.hh[:, n % RING, :], m.hid[:, n % RING, :]).then_inc(s["hi_done"], 1)

            for step in steps:
                if step in WEIGHTS:
                    k = WEIGHTS.index(step)
                    act.wait_ge(s["w_loaded"], 16 * (k + 1))
                    act.copy(m.owner[:] if step == "owner" else weights[k][0][:], stage[k][:]).then_inc(s["w_hi"], 1)
                if step in FILLED:
                    k = int(step[-1]) if step[-1] in "01" else 0
                    kk = slice(k * CH, (k + 1) * CH)
                if step in ("turn 0", "turn 1"):
                    act.wait_ge(s["side_ready"], filled(step))
                    act.copy(m.t_tok[:, 4 * k:4 * k + 4, :], side.rearrange("p (t n) -> p t n", t=4))\
                        .then_inc(s["side_read"], 1)
                elif step == "root":
                    act.wait_ge(s["aggregated"], NT)
                    act.activation(m.std[:], m.mv[:, :, 1], ACT.Sqrt, bias=m.eps[:, 0:1]).then_inc(s["std_done"], 1)
                elif step in ("turn back 0", "turn back 1"):
                    act.wait_ge(s["side_ready"], filled(step))
                    act.copy(m.xf[:, kk], side).then_inc(s["side_read"], 1)
                    act.copy(m.xhn[:, kk], side).then_inc(s["xh_done"], 1)
                elif step == "shift":
                    act.wait_ge(s["shifted"], 1)
                    act.activation(m.pr[:], m.pr[:], ACT.Exp).then_inc(s["exp_done"], 1)
                elif step in ("turn gates 0", "turn gates 1"):
                    act.wait_ge(s["side_ready"], filled(step))
                    if stage:
                        act.wait_ge(s["g_zeroed"], 1)
                    act.copy(m.gn[0:NE, kk], side[0:NE, :]).then_inc(s["gh_done"], 1)
                elif isinstance(step, int):
                    act.wait_ge(s["h1_ready"], step + 1)
                    if step >= 2:
                        act.wait_ge(s["mid_done"], step - 1)
                    act.activation(m.act_s[:, step % 2, :], ps[:, step % 2, :], ACT.Silu).then_inc(s["silu_done"], 1)
                    if step >= 1:
                        split(step - 1)
            if batch:
                split(NC * TILES - 1)
            if following is not None:
                if batch:
                    act.wait_ge(s["used"], NC * TILES)
                act.copy(m.xh[:], m.xhn[:]).then_inc(s["moved"], 1)

        @block.gpsimd
        def _(pool):
            if stage:
                pool.memset(m.gn[:].bitcast(F32), 0.0).then_inc(s["g_zeroed"], 1)
                for k in range(2):
                    pool.wait_ge(s["w_hi"], k + 1)
                    pool.tensor_tensor(weights[k][1][:], stage[k][:], weights[k][0][:].bitcast(F32), ALU.subtract)
            if batch:
                for n in range(NC * TILES):
                    if n >= RING:
                        pool.wait_ge(s["used"], n - RING + 1)
                    pool.wait_ge(s["hi_done"], n + 1)
                    pool.tensor_tensor(m.hl[:, n % RING, :], m.hid[:, n % RING, :], m.hh[:, n % RING, :].bitcast(F32),
                                       ALU.subtract).then_inc(s["lo_done"], 1)

        @block.vector
        def _(dve):
            run = in_order(dve, s["chain"])

            def result(c):
                dve.wait_ge(s["used"], TILES * (c + 1))
                dve.wait_ge(s["stream_loaded"], 16)
                dve.tensor_tensor(m.res[:, c, :], ps[:, 6, :], m.t2[:, c * CH:(c + 1) * CH], ALU.add)\
                    .then_inc(s["res_done"], 1)

            for step in steps:
                if step in FILLED:
                    k = int(step[-1]) if step[-1] in "01" else 0
                    kk = slice(k * CH, (k + 1) * CH)
                half = range(4 * int(step[-1]), 4 * int(step[-1]) + 4) if step in HALVES else ()
                if step in ("stats 0", "stats 1"):
                    dve.wait_ge(s["side_read"], int(step[-1]) + 1)
                    for t in half:
                        dve.bn_stats(m.st[:, t, :], m.t_tok[:, t, :]).then_inc(s["stats"], 1)
                    dve.wait_ge(s["stats"], half[-1] + 1)
                    for t in half:
                        dve.bn_aggr(m.mv[:, t, :], m.st[:, t, :]).then_inc(s["aggregated"], 1)
                elif step in ("normed 0", "normed 1"):
                    if step == "normed 0":
                        dve.wait_ge(s["std_done"], 1)
                        run(dve.reciprocal(m.rstd[:], m.std[:]))
                    for t in half:
                        dve.tensor_scalar(m.xn[:, t, :], m.t_tok[:, t, :], m.mv[:, t, 0:1], m.rstd[:, t:t + 1],
                                          ALU.subtract, ALU.mult).then_inc(s["xn_done"], 1)
                elif step in ("turn back 0", "turn back 1"):
                    dve.wait_ge(s["xh_done"], k + 1)
                    dve.tensor_tensor(m.xln[:, kk], side, m.xhn[:, kk].bitcast(F32), ALU.subtract)\
                        .then_inc(s["side_read"], 1)
                elif step == "shift":
                    dve.wait_ge(s["side_ready"], filled("logits"))
                    lg = side[:, 0:NT * NE].rearrange("p (t e) -> p t e", t=NT)
                    run(dve.tensor_reduce(m.top[:], lg, AX, ALU.max))
                    dve.tensor_tensor(m.pr[:], lg, each_tile(m.top[:], NE), ALU.subtract).then_inc(s["shifted"], 1)
                elif step == "softmax":
                    dve.wait_ge(s["exp_done"], 1)
                    run(dve.tensor_reduce(m.tot[:], m.pr[:], AX, ALU.add))
                    run(dve.reciprocal(m.inv[:], m.tot[:]))
                    dve.tensor_tensor(m.pr[:], m.pr[:], each_tile(m.inv[:], NE), ALU.mult).then_inc(s["side_read"], 1)
                elif step in ("compared", "rank"):
                    other = m.pr[:].unsqueeze(2).to_broadcast([P, NT, NE, NE])
                    own = m.pr[:].unsqueeze(3).to_broadcast([P, NT, NE, NE])
                    more4 = m.more[:].rearrange("p t (a b) -> p t a b", a=NE)
                    same4 = m.same[:].rearrange("p t (a b) -> p t a b", a=NE)
                    if step == "compared":
                        if stage:
                            dve.wait_ge(s["small_loaded"], 32)
                        dve.wait_ge(s["side_read"], reads_before("turn gates 0"))
                        dve.tensor_tensor(more4, other, own, ALU.is_gt)
                        run(dve.tensor_tensor(same4, other, own, ALU.is_equal))
                    else:
                        tie = each_token(m.tie[:].rearrange("p a b -> p (a b)"), NT)
                        run(dve.tensor_tensor(m.same[:], m.same[:], tie, ALU.mult))
                        run(dve.tensor_tensor(m.more[:], m.more[:], m.same[:], ALU.add))
                elif step == "kept":
                    run(dve.tensor_reduce(m.rank[:], m.more[:].rearrange("p t (a b) -> p t a b", a=NE), AX, ALU.add))
                    run(dve.tensor_scalar(m.rank[:], m.rank[:], 1.5, None, ALU.is_lt))
                    run(dve.tensor_tensor(m.gt[:], m.pr[:], m.rank[:], ALU.mult))
                elif step == "gates":
                    run(dve.tensor_reduce(m.tot[:], m.gt[:], AX, ALU.add))
                    run(dve.tensor_scalar(m.tot[:], m.tot[:], 1e-9, None, ALU.add))
                    run(dve.reciprocal(m.inv[:], m.tot[:]))
                    dve.tensor_tensor(m.gt[:], m.gt[:], each_tile(m.inv[:], NE), ALU.mult).then_inc(s["gates_done"], 1)
                elif step in ("turn gates 0", "turn gates 1"):
                    dve.wait_ge(s["gh_done"], k + 1)
                    dve.tensor_tensor(m.gn[GATE_LO:GATE_LO + NE, kk], side[0:NE, :], m.gn[0:NE, kk].bitcast(F32),
                                      ALU.subtract).then_inc(s["side_read"], 1)
                elif step == "result":
                    result(0)
                elif isinstance(step, int):
                    n = step
                    dve.wait_ge(s["h3_ready"], n + 1)
                    dve.wait_ge(s["silu_done"], n + 1)
                    dve.tensor_tensor(m.mid[:, n % 2, :], ps[:, 2 + n % 2, :], m.act_s[:, n % 2, :], ALU.mult)\
                        .then_inc(s["mid_done"], 1)
                    dve.wait_ge(s["g_ready"], n + 1)
                    dve.wait_ge(s["mid_done"], n + 1)
                    if n >= RING:
                        dve.wait_ge(s["lo_done"], n - RING + 1)
                    dve.tensor_tensor(m.hid[:, n % RING, :], ps[:, 4 + n % 2, :], m.mid[:, n % 2, :], ALU.mult)\
                        .then_inc(s["hid_done"], 1)
            if following is not None:
                if batch:
                    dve.wait_ge(s["used"], NC * TILES)
                if stage:
                    dve.wait_ge(s["g_zeroed"], 1)
                dve.tensor_copy(m.xl[:], m.xln[:].bitcast(F32)).then_inc(s["moved"], 1)
                dve.wait_ge(s["side_read"], reads_before("turn gates 1") + READS["turn gates 1"])
                dve.tensor_copy(m.g[:], m.gn[:].bitcast(F32)).then_inc(s["moved"], 1)
            if batch:
                result(NC - 1)
            if stage:
                dve.wait_ge(s["w_hi"], 3)
                dve.tensor_tensor(weights[2][1][:], stage[2][:], weights[2][0][:].bitcast(F32), ALU.subtract)
    phase_end(nc, s)
    stack.close()


def split_pieces(r, name):
    at = NW + 2 * RW if name == "q1" else 0
    heads = "p t (h n) -> p t h n"
    found = [(0, r[:, :, at:at + NW].rearrange(heads, h=HP))]
    if name != "q":
        found += [(NOPE + k * HALF, r[:, :, NW + k * RW:NW + (k + 1) * RW].rearrange(heads, h=HP)) for k in range(2)]
    return found


def by_turn(w, n):
    w = w.reshape(w.shape[0], NH // HP, HP, -1)
    parts = np.split(w, np.cumsum(n)[:-1], axis=3)
    return [np.roll(p.reshape(w.shape[0], NH // HP, -1), -1, axis=1).reshape(w.shape[0], NG, 2, -1)
            .transpose(1, 0, 2, 3) for p in parts]


def kernel(**inputs):
    import concourse.bacc as bacc
    from concourse.bass_utils import run_bass_kernel_spmd
    from ml_dtypes import bfloat16

    f = {k: np.asarray(x) for k, x in inputs.items()}
    c_, a_, e_ = ({k[len(p):]: x for k, x in f.items() if k.startswith(p)} for p in ("L0_conv_", "L1_attn_", "L1_ffn_"))
    arrays = {"x_next": np.roll(f["x"].reshape(B, C, T), -1, axis=0)}
    a, b = np.arange(P)[:, None], np.arange(P)[None]
    w = np.arange(WN)[None]
    arrays["ident"] = np.eye(P, dtype=np.float32)
    arrays["ident_bf"] = np.eye(P).astype(bfloat16)
    arrays["causal_q"] = np.where(b <= a, 0, MASKED).astype(bfloat16)
    arrays["causal_k"] = np.where(a <= b, 0, MASKED).astype(bfloat16)
    arrays["window_q0"] = np.where((w <= a) & (a - w < WINDOW), 0, MASKED).astype(bfloat16)
    arrays["window_q"] = np.where((w > a) & (w <= a + WINDOW), 0, MASKED).astype(bfloat16)
    arrays["window_k"] = np.where((w >= a) & (w - a < WINDOW), 0, MASKED).astype(bfloat16)
    freq = 1.0 / 10000.0 ** (np.arange(0, 2 * HALF, 2, dtype=np.float32) / (2 * HALF))
    angle = np.outer(np.arange(T, dtype=np.float32), freq)
    for name, fn in (("cos", np.cos), ("sin", np.sin)):
        arrays[name] = fn(angle).astype(np.float32).reshape(NT, P, HALF).transpose(1, 0, 2)
    arrays["before"] = (a < b).astype(np.float32)
    arrays["below"] = (b < a).astype(np.float32)
    arrays["iota"] = np.broadcast_to(np.arange(KEEP, dtype=np.float32), (P, KEEP))
    units_of = np.repeat(np.eye(NE, dtype=np.float32), HID, axis=1)
    arrays["owner"] = np.zeros((P, TILES * P), np.float32)
    for row in (0, GATE_LO):
        arrays["owner"][row:row + NE, :NE * HID] = units_of
    arrays["tie"] = np.broadcast_to(np.tril(np.ones((NE, NE), np.float32), -1), (P, NE, NE))
    twice = lambda x: np.concatenate([x, x], axis=-1)
    arrays["wt2"], arrays["wp2"] = twice(c_["Wt"].T), twice(c_["Wp"].T)
    arrays["wg"], arrays["wo"] = c_["Wg"].T, c_["Wo"].T
    arrays["bias"] = np.stack([twice(c_["bt"]), twice(c_["bp"]), twice(c_["bg"]), c_["bo"]], axis=1)
    arrays["wa"] = np.concatenate([a_["Wcq"], a_["Wckv"], a_["Wk_rope"], a_["W_imp"], a_["Wgate"]], axis=1)
    arrays["qnw"] = np.broadcast_to(a_["q_norm_w"], (P, QR))
    arrays["kvnw"] = np.broadcast_to(a_["kv_norm_w"], (P, KVR))
    arrays["wqn_t"] = a_["Wq_nope"].reshape(QR, NG, P).transpose(2, 1, 0)
    arrays["wproj"] = a_["Wproj"].reshape(NG, P, C).transpose(1, 0, 2)
    arrays["wproj_g"] = a_["Wproj"].reshape(NG, P, C)
    for name, x in (("wk_t", a_["Wk_nope"]), ("wv_t", a_["Wv"])):
        arrays[name] = np.zeros((HG, 32, NG, HG, KVR), np.float32)
        for h in range(HG):
            arrays[name][h, :, :, h, :] = x.reshape(KVR, NG, HG, 32)[:, :, h].transpose(2, 1, 0)
        arrays[name] = arrays[name].reshape(P, NG, P)
    rot = [HALF, HALF]
    arrays["wq"] = np.concatenate(by_turn(a_["Wq_nope"], [NOPE]) + by_turn(a_["Wq_rope"], rot), axis=3)
    arrays["wk"] = np.concatenate(by_turn(a_["Wwin_k"], [NOPE] + rot) + by_turn(a_["Wwin_v"], [VD]), axis=3)
    arrays["ws"] = np.concatenate(by_turn(a_["Wsel_k"], [NOPE] + rot) + by_turn(a_["Wsel_v"], [VD]), axis=3)
    arrays["router"] = e_["router_w"].T
    full = lambda x: np.concatenate([x, np.zeros((TILES * P - NE * HID, C), x.dtype)])
    arrays["w1"] = full(e_["w1"].reshape(NE * HID, C)).T
    arrays["w3"] = full(e_["w3"].reshape(NE * HID, C)).T
    arrays["w2"] = full(e_["w2"].transpose(0, 2, 1).reshape(NE * HID, C)).reshape(TILES, P, C)\
        .transpose(1, 0, 2).reshape(P, TILES * C)
    arrays = {k: np.ascontiguousarray(x) for k, x in arrays.items()}

    nc = bacc.Bacc("TRN2", target_bir_lowering=False, num_devices=1)
    d = {k: nc.dram_tensor("in_" + k, x.shape, mybir.dt.from_np(x.dtype), kind="ExternalInput").ap()
         for k, x in arrays.items()}
    out = nc.dram_tensor("out", (B, C, T), F32, kind="ExternalOutput").ap()
    program(nc, d, out)
    r = run_bass_kernel_spmd(nc, [{"in_" + k: x for k, x in arrays.items()}], core_ids=[0])
    return r.results[0]["out"].reshape(B, C, 32, 32)
```
